# Optimizing a Trainium2 kernel written in Bass

```python
import numpy as np
import jax
import jax.numpy as jnp

def _softmax(x, axis=-1):
    return jax.nn.softmax(x, axis=axis)

def _gelu(x):
    return jax.nn.gelu(x, approximate=True)

def _silu(x):
    return jax.nn.silu(x)

def _sigmoid(x):
    return jax.nn.sigmoid(x)

def _layernorm(x, axis=-1, eps=1e-05):
    m = jnp.mean(x, axis=axis, keepdims=True)
    v = jnp.var(x, axis=axis, keepdims=True)
    return (x - m) / jnp.sqrt(v + eps)

def _scatter_add(tgt, idx, src, axis=0):
    return tgt.at[idx].add(src)

def _segment_sum(src, seg, n):
    return jax.ops.segment_sum(src, seg, n)
kernel_name = 'mk_gnn_preln_d4_gnn_r32_0d3510'

def setup_inputs(seed: int=0):
    np.random.seed(seed)
    _w = jnp.asarray

    def _rec_inputs():
        import jax
        import jax.numpy as jnp
        _gk = jax.random.key(seed)
        x = -0.000202 + 1 * jax.random.normal(jax.random.fold_in(_gk, 1), (3125, 128), jnp.float32)
        _s = jax.random.randint(jax.random.fold_in(_gk, 2), (50000,), 0, 3125, jnp.int32)
        _d = jax.random.randint(jax.random.fold_in(_gk, 3), (50000,), 0, 3125, jnp.int32)
        _loop = jnp.arange(3125, dtype=jnp.int32)
        src = jnp.concatenate([_s, _d, _loop])
        dst = jnp.concatenate([_d, _s, _loop])
        _o = jnp.argsort(dst, stable=True)
        src = src[_o]
        dst = dst[_o]
        edge_attr_16 = 0.000254156 + 0.999948 * jax.random.normal(jax.random.fold_in(_gk, 12), (103125, 16), jnp.float32)
        edge_weight = jax.random.uniform(jax.random.fold_in(_gk, 14), (103125,), jnp.float32, 0.0, 0.999999)
        return (x, src, dst, edge_attr_16, edge_weight)
    x, src, dst, edge_attr_16, edge_weight = _rec_inputs()

    def _L0_gnn_setup():
        import jax, jax.numpy as jnp
        import numpy as np
        N_NODES = 50000
        N_EDGES = 18750
        IN_CH = 128
        OUT_CH = 128
        key = jax.random.key(seed)
        k1, k2, k3, k4 = jax.random.split(key, 4)
        x = jax.random.normal(k1, (N_NODES, IN_CH), dtype=jnp.float32)
        edge_index = jax.random.randint(k2, (2, N_EDGES), 0, N_NODES, dtype=jnp.int64)
        W = jax.random.normal(k3, (OUT_CH, IN_CH), dtype=jnp.float32) * (1.0 / np.sqrt(IN_CH))
        b = jax.random.normal(k4, (OUT_CH,), dtype=jnp.float32) * 0.01
        return {'x': x, 'edge_index': edge_index, 'W': W, 'b': b}
    _L0_gnn_all = _L0_gnn_setup()
    _L0_gnn_in = {k: v for k, v in _L0_gnn_all.items() if k in ('W', 'b')}
    del _L0_gnn_all

    def _L1_gnn_setup():
        import jax, jax.numpy as jnp
        import numpy as np
        N_NODES = 50000
        N_EDGES = 50000
        IN_DIM = 128
        HID = 32
        HEADS = 4
        NEG_SLOPE = 0.2

        def _gat_forward(h, src, dst, Wq, Wk, Wv):
            n = h.shape[0]
            q = jnp.einsum('ni,hio->hno', h, Wq)
            k = jnp.einsum('ni,hio->hno', h, Wk)
            v = jnp.einsum('ni,hio->hno', h, Wv)
            e = jax.nn.leaky_relu(jnp.einsum('hed,hed->he', q[:, src], k[:, dst]), negative_slope=NEG_SLOPE)
            seg_max = jax.vmap(lambda x: jax.ops.segment_max(x, dst, num_segments=n))(e)
            seg_max = jax.lax.stop_gradient(jnp.where(jnp.isfinite(seg_max), seg_max, 0.0))
            ex = jnp.exp(e - seg_max[:, dst])
            denom = jax.vmap(lambda x: jax.ops.segment_sum(x, dst, num_segments=n))(ex)
            alpha = ex / jnp.maximum(denom, 1e-09)[:, dst]
            msg = alpha[..., None] * v[:, src]
            out = jax.vmap(lambda m: jax.ops.segment_sum(m, dst, num_segments=n))(msg)
            return out.transpose(1, 0, 2).reshape(n, HEADS * HID)
        key = jax.random.key(seed)
        ks = jax.random.split(key, 6)
        h = jax.random.normal(ks[0], (N_NODES, IN_DIM), dtype=jnp.float32)
        src = jax.random.randint(ks[1], (N_EDGES,), 0, N_NODES, dtype=jnp.int32)
        dst = jax.random.randint(ks[2], (N_EDGES,), 0, N_NODES, dtype=jnp.int32)
        s = 1.0 / np.sqrt(IN_DIM)
        Wq = jax.random.normal(ks[3], (HEADS, IN_DIM, HID), dtype=jnp.float32) * s
        Wk = jax.random.normal(ks[4], (HEADS, IN_DIM, HID), dtype=jnp.float32) * s
        Wv = jax.random.normal(ks[5], (HEADS, IN_DIM, HID), dtype=jnp.float32) * s
        return {'h': h, 'src': src, 'dst': dst, 'Wq': Wq, 'Wk': Wk, 'Wv': Wv}
    _L1_gnn_all = _L1_gnn_setup()
    _L1_gnn_in = {k: v for k, v in _L1_gnn_all.items() if k in ('Wq', 'Wk', 'Wv')}
    del _L1_gnn_all

    def _L2_gnn_setup():
        import jax, jax.numpy as jnp
        import numpy as np
        N_NODES = 50000
        N_EDGES = 50000
        D = 128
        N_LAYERS = 2
        NEG_SLOPE = 0.2

        def _gcn_layer(x, src, dst, ew, Ws, bs, Wn, bn, bias):
            n = x.shape[0]
            msg = x[src] * ew[:, None]
            agg = jax.ops.segment_sum(msg, dst, num_segments=n)
            agg = agg + x
            cnt = jax.ops.segment_sum(jnp.ones_like(ew), dst, num_segments=n) + 1.0
            neigh = agg / cnt[:, None]
            out = x @ Ws.T + bs + neigh @ Wn.T + bn + bias
            return jnp.where(out > 0, out, NEG_SLOPE * out)
        key = jax.random.key(seed)
        ks = jax.random.split(key, 10)
        user_embeddings = jax.random.normal(ks[0], (N_NODES, D), dtype=jnp.float32)
        social_edge_index = jax.random.randint(ks[1], (2, N_EDGES), 0, N_NODES, dtype=jnp.int64)
        social_edge_weights = jax.random.uniform(ks[2], (N_EDGES,), dtype=jnp.float32)
        s = 1.0 / np.sqrt(D)
        W_self = jax.random.uniform(ks[3], (N_LAYERS, D, D), minval=-s, maxval=s, dtype=jnp.float32)
        b_self = jax.random.uniform(ks[4], (N_LAYERS, D), minval=-s, maxval=s, dtype=jnp.float32)
        W_neigh = jax.random.uniform(ks[5], (N_LAYERS, D, D), minval=-s, maxval=s, dtype=jnp.float32)
        b_neigh = jax.random.uniform(ks[6], (N_LAYERS, D), minval=-s, maxval=s, dtype=jnp.float32)
        layer_bias = jnp.zeros((N_LAYERS, D), dtype=jnp.float32)
        W_agg = jax.random.uniform(ks[7], (D, D), minval=-s, maxval=s, dtype=jnp.float32)
        b_agg = jax.random.uniform(ks[8], (D,), minval=-s, maxval=s, dtype=jnp.float32)
        return {'user_embeddings': user_embeddings, 'social_edge_index': social_edge_index, 'social_edge_weights': social_edge_weights, 'W_self': W_self, 'b_self': b_self, 'W_neigh': W_neigh, 'b_neigh': b_neigh, 'layer_bias': layer_bias, 'W_agg': W_agg, 'b_agg': b_agg}
    _L2_gnn_all = _L2_gnn_setup()
    _L2_gnn_in = {k: v for k, v in _L2_gnn_all.items() if k in ('W_self', 'b_self', 'W_neigh', 'b_neigh', 'layer_bias', 'W_agg', 'b_agg')}
    del _L2_gnn_all

    def _L3_gnn_setup():
        import jax, jax.numpy as jnp
        import numpy as np
        N_NODES = 3125
        N_EDGES = 25000
        D_IN = 128
        D_OUT = 128
        E_DIM = 16
        key = jax.random.key(seed)
        k1, k2, k3, k4, k5 = jax.random.split(key, 5)
        x = jax.random.normal(k1, (N_NODES, D_IN), dtype=jnp.float32)
        edge_index = jax.random.randint(k2, (2, N_EDGES), 0, N_NODES, dtype=jnp.int64)
        edge_attr = jax.random.normal(k3, (N_EDGES, E_DIM), dtype=jnp.float32)
        W = jax.random.uniform(k4, (D_IN, D_OUT), dtype=jnp.float32, minval=-1.0, maxval=1.0) * float(np.sqrt(6.0 / (D_IN + D_OUT)))
        edge_w = jax.random.uniform(k5, (E_DIM, D_OUT), dtype=jnp.float32, minval=-1.0, maxval=1.0) * float(np.sqrt(6.0 / (E_DIM + D_OUT)))
        b = jnp.zeros((D_OUT,), dtype=jnp.float32)
        return {'x': x, 'edge_index': edge_index, 'edge_attr': edge_attr, 'W': W, 'edge_w': edge_w, 'b': b}
    _L3_gnn_all = _L3_gnn_setup()
    _L3_gnn_in = {k: v for k, v in _L3_gnn_all.items() if k in ('W', 'edge_w', 'b')}
    del _L3_gnn_all
    return {'x': x, 'src': src, 'dst': dst, 'edge_attr_16': edge_attr_16, 'edge_weight': edge_weight, 'L0_gnn_W': _L0_gnn_in['W'], 'L0_gnn_b': _L0_gnn_in['b'], 'L1_gnn_Wq': _L1_gnn_in['Wq'], 'L1_gnn_Wk': _L1_gnn_in['Wk'], 'L1_gnn_Wv': _L1_gnn_in['Wv'], 'L2_gnn_W_self': _L2_gnn_in['W_self'], 'L2_gnn_b_self': _L2_gnn_in['b_self'], 'L2_gnn_W_neigh': _L2_gnn_in['W_neigh'], 'L2_gnn_b_neigh': _L2_gnn_in['b_neigh'], 'L2_gnn_layer_bias': _L2_gnn_in['layer_bias'], 'L2_gnn_W_agg': _L2_gnn_in['W_agg'], 'L2_gnn_b_agg': _L2_gnn_in['b_agg'], 'L3_gnn_W': _L3_gnn_in['W'], 'L3_gnn_edge_w': _L3_gnn_in['edge_w'], 'L3_gnn_b': _L3_gnn_in['b']}

def reference(x, src, dst, edge_attr_16, edge_weight, L0_gnn_W, L0_gnn_b, L1_gnn_Wq, L1_gnn_Wk, L1_gnn_Wv, L2_gnn_W_self, L2_gnn_b_self, L2_gnn_W_neigh, L2_gnn_b_neigh, L2_gnn_layer_bias, L2_gnn_W_agg, L2_gnn_b_agg, L3_gnn_W, L3_gnn_edge_w, L3_gnn_b):
    import jax
    import jax.numpy as jnp

    def _L0_gnn_ref(x, edge_index, W, b):
        import jax, jax.numpy as jnp
        import numpy as np
        N_NODES = 50000
        N_EDGES = 18750
        IN_CH = 128
        OUT_CH = 128
        row, col = (edge_index[0], edge_index[1])
        n = x.shape[0]
        deg = jax.ops.segment_sum(jnp.ones_like(row, dtype=x.dtype), row, num_segments=n)
        deg_inv_sqrt = jnp.where(deg > 0, jax.lax.rsqrt(jnp.where(deg > 0, deg, 1.0)), 0.0)
        norm = deg_inv_sqrt[row] * deg_inv_sqrt[col]
        msgs = norm[:, None] * x[col]
        agg = jax.ops.segment_sum(msgs, row, num_segments=n)
        return agg @ W.T + b

    def _L1_gnn_ref(h, src, dst, Wq, Wk, Wv):
        import jax, jax.numpy as jnp
        import numpy as np
        N_NODES = 50000
        N_EDGES = 50000
        IN_DIM = 128
        HID = 32
        HEADS = 4
        NEG_SLOPE = 0.2

        def _gat_forward(h, src, dst, Wq, Wk, Wv):
            n = h.shape[0]
            q = jnp.einsum('ni,hio->hno', h, Wq)
            k = jnp.einsum('ni,hio->hno', h, Wk)
            v = jnp.einsum('ni,hio->hno', h, Wv)
            e = jax.nn.leaky_relu(jnp.einsum('hed,hed->he', q[:, src], k[:, dst]), negative_slope=NEG_SLOPE)
            seg_max = jax.vmap(lambda x: jax.ops.segment_max(x, dst, num_segments=n))(e)
            seg_max = jax.lax.stop_gradient(jnp.where(jnp.isfinite(seg_max), seg_max, 0.0))
            ex = jnp.exp(e - seg_max[:, dst])
            denom = jax.vmap(lambda x: jax.ops.segment_sum(x, dst, num_segments=n))(ex)
            alpha = ex / jnp.maximum(denom, 1e-09)[:, dst]
            msg = alpha[..., None] * v[:, src]
            out = jax.vmap(lambda m: jax.ops.segment_sum(m, dst, num_segments=n))(msg)
            return out.transpose(1, 0, 2).reshape(n, HEADS * HID)
        return _gat_forward(h, src, dst, Wq, Wk, Wv)

    def _L2_gnn_ref(user_embeddings, social_edge_index, social_edge_weights, W_self, b_self, W_neigh, b_neigh, layer_bias, W_agg, b_agg):
        import jax, jax.numpy as jnp
        import numpy as np
        N_NODES = 50000
        N_EDGES = 50000
        D = 128
        N_LAYERS = 2
        NEG_SLOPE = 0.2

        def _gcn_layer(x, src, dst, ew, Ws, bs, Wn, bn, bias):
            n = x.shape[0]
            msg = x[src] * ew[:, None]
            agg = jax.ops.segment_sum(msg, dst, num_segments=n)
            agg = agg + x
            cnt = jax.ops.segment_sum(jnp.ones_like(ew), dst, num_segments=n) + 1.0
            neigh = agg / cnt[:, None]
            out = x @ Ws.T + bs + neigh @ Wn.T + bn + bias
            return jnp.where(out > 0, out, NEG_SLOPE * out)
        src = social_edge_index[0]
        dst = social_edge_index[1]
        x = user_embeddings
        for l in range(N_LAYERS):
            x = _gcn_layer(x, src, dst, social_edge_weights, W_self[l], b_self[l], W_neigh[l], b_neigh[l], layer_bias[l])
        return x @ W_agg.T + b_agg

    def _L3_gnn_ref(x, edge_index, edge_attr, W, edge_w, b):
        import jax, jax.numpy as jnp
        import numpy as np
        N_NODES = 3125
        N_EDGES = 25000
        D_IN = 128
        D_OUT = 128
        E_DIM = 16
        src, dst = (edge_index[0], edge_index[1])
        xw = x @ W
        ew = edge_attr @ edge_w
        msg = xw[src] * ew
        out = jax.ops.segment_sum(msg, dst, num_segments=x.shape[0])
        out = out + b
        return out
    edge_index = jnp.stack([src, dst])
    h = jnp.maximum(_layernorm(x, axis=-1), 0.0)
    x = x + _L0_gnn_ref(h, edge_index, L0_gnn_W, L0_gnn_b)
    h = jnp.maximum(_layernorm(x, axis=-1), 0.0)
    x = x + _L1_gnn_ref(h, src, dst, L1_gnn_Wq, L1_gnn_Wk, L1_gnn_Wv)
    h = jnp.maximum(_layernorm(x, axis=-1), 0.0)
    x = x + _L2_gnn_ref(h, edge_index, edge_weight, L2_gnn_W_self, L2_gnn_b_self, L2_gnn_W_neigh, L2_gnn_b_neigh, L2_gnn_layer_bias, L2_gnn_W_agg, L2_gnn_b_agg)
    h = jnp.maximum(_layernorm(x, axis=-1), 0.0)
    x = x + _L3_gnn_ref(h, edge_index, edge_attr_16, L3_gnn_W, L3_gnn_edge_w, L3_gnn_b)
    return x

_drawn_inputs = setup_inputs


def setup_inputs(seed=0):
    import zlib

    import numpy as np

    out = dict(_drawn_inputs(seed))
    spreads = {'L2_gnn_layer_bias': (0.0, 0.1), 'L3_gnn_b': (0.0, 0.1)}
    factors = {'edge_weight': 8.0, 'L0_gnn_b': 5.406, 'L2_gnn_b_self': 3.128, 'L2_gnn_b_neigh': 2.927}
    for name, (base, spread) in spreads.items():
        noise = np.random.default_rng([zlib.crc32(name.encode()), seed]).standard_normal(out[name].shape)
        drawn = base * np.exp(spread * noise) if base else spread * noise
        out[name] = jnp.asarray(drawn.astype(out[name].dtype))
    for name, factor in factors.items():
        out[name] = (out[name] * factor).astype(out[name].dtype)
    return out
```

```python
from contextlib import ExitStack
from itertools import count

import concourse.bass as bass
from concourse import mybir
from concourse.alu_op_type import AluOpType as ALU

F32 = mybir.dt.float32
BF16 = mybir.dt.bfloat16
I32 = mybir.dt.int32
ACT = mybir.ActivationFunctionType
AX = mybir.AxisListType

N = 3125
E = 103125
D = 128
P = 125
TILES = N // P
WIN = 5
WINDOWS = N // WIN
WPT = P // WIN
BLOCKS = WINDOWS // P
ROW = 25
ROWS = E // ROW
GROWS = 10
SLOTS = ROW * GROWS // 2
CHUNKS = E // P
MAGIC = 1.5 * 2 ** 23
GRP = 5
NGRP = WPT // GRP
EG = 5
EGROUPS = CHUNKS // EG
SPAN = 32
LN_EPS = 1e-5
SLOPE = 0.2
HEADS, HID = 4, 32
EDIM = 16


NAMES = count(1)


def unique(name):
    return f"{name}_{next(NAMES)}"


def chained(eng, sem, start=0):
    done = [start]

    def link(ins):
        done[0] += 1
        ins.then_inc(sem, 1)
        eng.wait_ge(sem, done[0])

    return link


def in_pairs(eng, body, n=TILES):
    with eng.Fori(0, n // 2) as i:
        body(i * 2, 0)
        body(i * 2 + 1, 1)
    if n % 2:
        body(n - 1, 0)


def row_of(ap3, t):
    return ap3[:, bass.ds(t, 1), :].rearrange("p o f -> p (o f)")


def floor_div(nc, link, out, x, d):
    link(nc.vector.tensor_scalar(out, x, 1.0 / d, -((d - 1) // 2) / d, ALU.mult, ALU.add))
    link(nc.vector.tensor_scalar(out, out, MAGIC, -MAGIC, ALU.add, ALU.add))


def layer_norm_relu(nc, dve, link, X, H, stats, mv, rstd, var_ready, std_ready, n=1):
    for t in range(TILES):
        ins = nc.vector.bn_stats(stats[:, t, :], X[:, t, :])
    link(ins)
    for t in range(TILES):
        ins = nc.vector.bn_aggr(mv[:, t, :], stats[:, t, :])
    link(ins)
    nc.vector.tensor_scalar(rstd[:], mv[:, :, 1], LN_EPS, None, ALU.add).then_inc(var_ready, 1)
    dve.wait_ge(std_ready, n)
    link(nc.vector.reciprocal(rstd[:], rstd[:]))
    for t in range(TILES):
        ins = nc.vector.tensor_scalar(H[:, t, :], X[:, t, :], mv[:, t, 0:1], rstd[:, t:t + 1],
                                      ALU.subtract, ALU.mult)
    link(ins)
    link(nc.vector.tensor_scalar(H[:], H[:], 0.0, None, ALU.max))


def standard_deviation(nc, act, rstd, var_ready, std_ready, n=1):
    act.wait_ge(var_ready, n)
    nc.scalar.activation(rstd[:], rstd[:], ACT.Sqrt).then_inc(std_ready, 1)


def window_starts(nc, T, table, starts, X, H, stats, mv, rstd, ident, ones, iota, iota_tile):
    with ExitStack() as c:
        e = c.enter_context
        dst_i = e(nc.sbuf_tensor(unique("dst_i"), [P, CHUNKS], I32))
        win_hi = e(nc.sbuf_tensor(unique("win_hi"), [P, CHUNKS], F32))
        win_lo = e(nc.sbuf_tensor(unique("win_lo"), [P, CHUNKS], F32))
        one_hi = e(nc.sbuf_tensor(unique("one_hi"), [P, CHUNKS, TILES], BF16))
        one_lo = e(nc.sbuf_tensor(unique("one_lo"), [P, CHUNKS, WPT], BF16))
        pad = e(nc.sbuf_tensor(unique("pad"), [GROWS, 3 * ROW], I32))
        iota_i = e(nc.sbuf_tensor(unique("iota_i"), [P, P], I32))
        iota_ti = e(nc.sbuf_tensor(unique("iota_ti"), [P, TILES], I32))
        fold = e(nc.sbuf_tensor(unique("fold"), [P, TILES], F32))
        same = e(nc.sbuf_tensor(unique("same"), [P, GRP], F32))
        before = e(nc.sbuf_tensor(unique("before"), [TILES, TILES], F32))
        pairs = e(nc.sbuf_tensor(unique("pairs"), [P, P], F32))
        hist = e(nc.sbuf_tensor(unique("hist"), [TILES, WPT], F32))
        upto = e(nc.sbuf_tensor(unique("upto"), [TILES, WPT], F32))
        zeros = e(nc.sbuf_tensor(unique("zeros"), [TILES, WPT], F32))
        first = e(nc.sbuf_tensor(unique("first"), [TILES, WPT], F32))
        first_i = e(nc.sbuf_tensor(unique("first_i"), [TILES, WPT], I32))
        pairs_ps = e(nc.psum_tensor(unique("pairs_ps"), [P, P], F32))
        hist_ps = e(nc.psum_tensor(unique("hist_ps"), [TILES, P], F32))
        off_ps = e(nc.psum_tensor(unique("off_ps"), [TILES, 2], F32))
        x_in = e(nc.semaphore(unique("x_in")))
        dst_in = e(nc.semaphore(unique("dst_loaded")))
        table_done = e(nc.semaphore(unique("table_done")))
        pool_done = e(nc.semaphore(unique("pool_done")))
        dve_done = e(nc.semaphore(unique("dve_done")))
        pe_done = e(nc.semaphore(unique("pe_done")))
        starts_done = e(nc.semaphore(unique("starts_done")))
        var_ready = e(nc.semaphore(unique("var_ready")))
        std_ready = e(nc.semaphore(unique("std_ready")))
        block = e(nc.Block())
        marks = {}

        @block.gpsimd
        def _(pool):
            link = chained(pool, pool_done)
            link(nc.gpsimd.memset(ident[:], 0.0))
            link(nc.gpsimd.memset(before[:], 1.0))
            link(nc.gpsimd.affine_select(out=ident[:], in_=ident[:], compare_op=ALU.not_equal, fill=1.0, base=0,
                                         pattern=[[-1, 128]], channel_multiplier=1))
            link(nc.gpsimd.affine_select(out=before[:], in_=before[:], compare_op=ALU.is_gt, fill=0.0, base=0,
                                         pattern=[[1, TILES]], channel_multiplier=-1))
            link(nc.gpsimd.iota(iota_i[:], [[1, P]], base=0, channel_multiplier=0))
            link(nc.gpsimd.iota(iota_ti[:], [[P, TILES]], base=0, channel_multiplier=0))
            link(nc.gpsimd.memset(pad[:, 0:2 * ROW], -1))
            link(nc.gpsimd.memset(pad[:, 2 * ROW:], 0))
            link(nc.gpsimd.memset(zeros[:], 0.0))
            link(nc.gpsimd.memset(ones[:], 1.0))

        def vector(dve):
            count = [0]

            def link(ins):
                count[0] += 1
                ins.then_inc(dve_done, 1)
                dve.wait_ge(dve_done, count[0])

            dve.wait_ge(pool_done, 10)
            link(nc.vector.tensor_copy(iota[:], iota_i[:]))
            link(nc.vector.tensor_copy(iota_tile[:], iota_ti[:]))
            blocks = ident[0:P, 0:P].rearrange("p (j h) -> p j h", h=TILES)
            link(nc.vector.tensor_reduce(fold[:], blocks.rearrange("p j h -> p h j"), axis=AX.X, op=ALU.add))
            link(nc.vector.tensor_reduce(same[:], blocks, axis=AX.X, op=ALU.add))
            dve.wait_ge(dst_in, 16)
            link(nc.vector.tensor_copy(win_lo[:], dst_i[:]))
            floor_div(nc, link, win_lo[:], win_lo[:], WIN)
            floor_div(nc, link, win_hi[:], win_lo[:], WPT)
            link(nc.vector.scalar_tensor_tensor(win_lo[:], win_hi[:], -float(WPT), win_lo[:], ALU.mult, ALU.add))
            step = CHUNKS // 5
            for k in range(5):
                part = slice(k * step, (k + 1) * step)
                for one, win in ((one_hi, win_hi), (one_lo, win_lo)):
                    link(nc.vector.tensor_tensor(one[:, part, :],
                                                 win[:, part].unsqueeze(2).broadcast_to([P, step, TILES]),
                                                 iota[:, 0:TILES].unsqueeze(1).broadcast_to([P, step, TILES]),
                                                 ALU.is_equal))
                marks["one", k] = count[0]
            dve.wait_ge(x_in, 16)
            layer_norm_relu(nc, dve, link, X, H, stats, mv, rstd, var_ready, std_ready)
            dve.wait_ge(pe_done, 1)
            link(nc.vector.tensor_tensor(pairs[:].rearrange("p (j m) -> p j m", m=WPT),
                                         pairs_ps[:].rearrange("p (j m) -> p j m", m=WPT),
                                         same[:].unsqueeze(2).broadcast_to([P, GRP, WPT]), ALU.mult))
            marks["pairs"] = count[0]
            dve.wait_ge(pe_done, 2)
            link(nc.vector.tensor_reduce(hist[:], hist_ps[:].rearrange("h (j m) -> h m j", m=WPT), axis=AX.X,
                                         op=ALU.add))
            link(nc.vector.tensor_tensor_scan(upto[:], hist[:], zeros[:], 0.0, ALU.add, ALU.add))
            marks["upto"] = count[0]
            dve.wait_ge(pe_done, 3)
            link(nc.vector.tensor_tensor(first[:], upto[:], hist[:], ALU.subtract))
            link(nc.vector.tensor_scalar(first[:], first[:], off_ps[:, 0:1], None, ALU.add))
            floor_div(nc, link, first[:], first[:], ROW)
            link(nc.vector.tensor_copy(first_i[:], first[:]))
            marks["starts"] = count[0]

        block.vector(vector)

        @block.scalar
        def _(act):
            standard_deviation(nc, act, rstd, var_ready, std_ready)

        @block.tensor
        def _(pe):
            per = CHUNKS // GRP
            for k in range(per):
                if k % (per // 5) == 0:
                    pe.wait_ge(dve_done, marks["one", k // (per // 5)])
                ins = nc.tensor.matmul(pairs_ps[:], one_hi[:, GRP * k:GRP * (k + 1), :].rearrange("p j h -> p (j h)"),
                                       one_lo[:, GRP * k:GRP * (k + 1), :].rearrange("p j h -> p (j h)"),
                                       start=(k == 0), stop=(k == per - 1))
            ins.then_inc(pe_done, 1)
            pe.wait_ge(dve_done, marks["pairs"])
            nc.tensor.matmul(hist_ps[:], fold[:], pairs[:], start=True, stop=True).then_inc(pe_done, 1)
            pe.wait_ge(dve_done, marks["upto"])
            nc.tensor.matmul(off_ps[:, 0:1], before[:], upto[:, WPT - 1:WPT], start=True, stop=True).then_inc(pe_done, 1)

        @block.sync
        def _(sp):
            sp.dma_start(dst_i[:], T["dst"].rearrange("(p c) -> p c", p=P)).then_inc(dst_in, 16)
            sp.dma_start(X[:], T["x"].rearrange("(t p) f -> p t f", p=P)).then_inc(x_in, 16)
            for k, name in enumerate(("src", "dst", "edge_weight")):
                column = table[0:ROWS, k * ROW:(k + 1) * ROW]
                if name == "edge_weight":
                    column = column.bitcast(F32)
                sp.dma_start(column, T[name].rearrange("(r e) -> r e", e=ROW)).then_inc(table_done, 16)
            sp.wait_ge(pool_done, 10)
            sp.dma_start(table[ROWS:ROWS + GROWS, :], pad[:]).then_inc(table_done, 16)
            sp.wait_ge(table_done, 64)
            sp.wait_ge(dve_done, marks["starts"])
            sp.dma_start(starts.rearrange("(h m) -> h m", m=WPT), first_i[:]).then_inc(starts_done, 16)
            sp.wait_ge(starts_done, 16)


def edge_slots(nc, table, starts, ident, src_hi, src_lo, dst_in, weight):
    KINDS = 3
    with ExitStack() as c:
        e = c.enter_context
        row0 = e(nc.sbuf_tensor(unique("row0"), [P, BLOCKS], I32))
        row_f = e(nc.sbuf_tensor(unique("row_f"), [P, BLOCKS], F32))
        off_i = e(nc.sbuf_tensor(unique("off_i"), [P, GROWS], I32))
        off_f = e(nc.sbuf_tensor(unique("off_f"), [P, GROWS], F32))
        index = e(nc.sbuf_tensor(unique("index"), [P, GROWS, BLOCKS], I32))
        rows = e(nc.sbuf_tensor(unique("rows"), [P, BLOCKS, GROWS, KINDS * ROW], I32))
        flat = e(nc.sbuf_tensor(unique("flat"), [P, BLOCKS, KINDS, GROWS * ROW], F32))
        win_i = e(nc.sbuf_tensor(unique("win_i"), [P, 2 * WINDOWS], I32))
        src_f = e(nc.sbuf_tensor(unique("src_f"), [P, 2 * WINDOWS], F32))
        turned = e(nc.psum_tensor(unique("turned"), [P, 2, 512], F32))
        loaded = e(nc.semaphore(unique("loaded")))
        pool_ready = e(nc.semaphore(unique("pool_ready")))
        gathered = [e(nc.semaphore(unique(f"gathered{b}"))) for b in range(BLOCKS)]
        index_ready = e(nc.semaphore(unique("index_ready")))
        flat_ready = e(nc.semaphore(unique("flat_ready")))
        turn_done = e(nc.semaphore(unique("turn_done")))
        copied = e(nc.semaphore(unique("copied")))
        slots_done = e(nc.semaphore(unique("slots_done")))
        block = e(nc.Block())

        @block.sync
        def _(sp):
            with nc.allow_non_contiguous_dma(reason="one start a partition"):
                sp.dma_start(row0[:], starts.rearrange("(b p) -> p b", p=P)).then_inc(loaded, 16)

        @block.gpsimd
        def _(pool):
            nc.gpsimd.iota(off_i[:], [[1, GROWS]], base=0, channel_multiplier=0).then_inc(pool_ready, 1)
            nc.gpsimd.iota(win_i[:].rearrange("p (w h) -> p w h", h=2), [[WIN, WINDOWS], [0, 2]], base=0,
                           channel_multiplier=0).then_inc(pool_ready, 1)
            pool.wait_ge(index_ready, 1)
            for b in range(BLOCKS):
                for j in range(GROWS):
                    nc.gpsimd.indirect_dma_start(rows[:, b, j, :], None, table,
                                                 bass.IndirectOffsetOnAxis(ap=index[:, j, b:b + 1], axis=0)
                                                 ).then_inc(gathered[b], 16)

        @block.vector
        def _(dve):
            link = chained(dve, slots_done)
            dve.wait_ge(pool_ready, 2)
            link(nc.vector.tensor_copy(off_f[:], off_i[:]))
            dve.wait_ge(loaded, 16)
            link(nc.vector.tensor_copy(row_f[:], row0[:]))
            nc.vector.tensor_tensor(index[:], row_f[:].unsqueeze(1).broadcast_to([P, GROWS, BLOCKS]),
                                    off_f[:].unsqueeze(2).broadcast_to([P, GROWS, BLOCKS]),
                                    ALU.add).then_inc(index_ready, 1)
            for b in range(BLOCKS):
                dve.wait_ge(gathered[b], 16 * GROWS)
                for k in range(KINDS):
                    part = rows[:, b, :, k * ROW:(k + 1) * ROW]
                    if k == 2:
                        part = part.bitcast(F32)
                    nc.vector.tensor_copy(flat[:, b, k, :].rearrange("p (j e) -> p j e", e=ROW),
                                          part).then_inc(flat_ready, 1)
            dve.wait_ge(copied, 3 * 2 * BLOCKS)
            floor_div(nc, link, src_hi[:], src_f[:], P)
            link(nc.vector.tensor_scalar(src_hi[:], src_hi[:], float(P), None, ALU.mult))
            link(nc.vector.tensor_tensor(src_lo[:], src_f[:], src_hi[:], ALU.subtract))
            link(nc.vector.tensor_copy(src_f[:], win_i[:]))
            link(nc.vector.tensor_tensor(dst_in[:], dst_in[:], src_f[:], ALU.subtract))

        @block.tensor
        def _(pe):
            for b in range(BLOCKS):
                pe.wait_ge(flat_ready, KINDS * (b + 1))
                for h in range(2):
                    n = 2 * b + h
                    if n >= 2:
                        pe.wait_ge(copied, 3 * (n - 1))
                    for k in range(KINDS):
                        ins = nc.tensor.transpose(turned[:, h, k * P:(k + 1) * P], flat[:, b, k, h * P:(h + 1) * P],
                                                  ident[0:P, 0:P])
                    ins.then_inc(turn_done, 1)

        @block.scalar
        def _(act):
            for b in range(BLOCKS):
                for h in range(2):
                    act.wait_ge(turn_done, 2 * b + h + 1)
                    for k, out in enumerate((src_f, dst_in, weight)):
                        out = out[:].rearrange("p (w h) -> p h w", h=2)[:, h, b * P:(b + 1) * P]
                        nc.scalar.copy(out, turned[:, h, k * P:(k + 1) * P]).then_inc(copied, 1)


def adjacency(nc, counts, countsT, weightsT, ident, ones, src_hi, src_lo, dst_in, weight, iota, iota_tile,
              out_degree, in_parts):
    PER = 3 + 2 * NGRP
    G = 2 * GRP
    WID = 2 * WIN
    ROUNDS = (TILES + 3) // 4
    with ExitStack() as c:
        e = c.enter_context
        tile_hot = e(nc.sbuf_tensor(unique("tile_hot"), [P, 2, 2 * WPT, TILES], F32))
        dst_hot = e(nc.sbuf_tensor(unique("dst_hot"), [P, 2, 2 * WPT, WID], F32))
        lo_hot = e(nc.sbuf_tensor(unique("lo_hot"), [P, 2, G, P], F32))
        pair_hot = e(nc.sbuf_tensor(unique("pair_hot"), [P, 2, G, TILES * WID], F32))
        cT = e(nc.sbuf_tensor(unique("cT"), [P, 2, N], F32))
        wT = e(nc.sbuf_tensor(unique("wT"), [P, 2, N], F32))
        cc = e(nc.sbuf_tensor(unique("cc"), [P, 2, N], F32))
        degree_parts = e(nc.sbuf_tensor(unique("degree_parts"), [P, TILES, TILES], F32))
        built = [e(nc.psum_tensor(unique(f"built{i}"), [P, 3 * 512], F32)) for i in range(2)]
        flipped = e(nc.psum_tensor(unique("flipped"), [P, 2, 512], F32))
        made = e(nc.semaphore(unique("made")))
        grouped = e(nc.semaphore(unique("grouped")))
        copied = e(nc.semaphore(unique("cT_copied")))
        turned = e(nc.semaphore(unique("tile_turned")))
        straight = e(nc.semaphore(unique("straight")))
        summed = e(nc.semaphore(unique("summed")))
        added = e(nc.semaphore(unique("added")))
        stored = [e(nc.semaphore(unique(f"stored{u}"))) for u in range(2)]
        free = e(nc.semaphore(unique("tiles_free")))
        block = e(nc.Block())

        @block.vector
        def _(dve):
            def tile(t, u):
                halves = bass.ds(t * (2 * WPT), 2 * WPT)
                nc.vector.tensor_tensor(tile_hot[:, u], src_hi[:, halves].unsqueeze(2).broadcast_to([P, 2 * WPT, TILES]),
                                        iota_tile[:].unsqueeze(1).broadcast_to([P, 2 * WPT, TILES]),
                                        ALU.is_equal).then_inc(made, 1)
                nc.vector.tensor_tensor(dst_hot[:, u, :, 0:WIN],
                                        dst_in[:, halves].unsqueeze(2).broadcast_to([P, 2 * WPT, WIN]),
                                        iota[:, 0:WIN].unsqueeze(1).broadcast_to([P, 2 * WPT, WIN]),
                                        ALU.is_equal).then_inc(made, 1)
                dve.wait_ge(made, t * PER + 2)
                nc.vector.tensor_tensor(dst_hot[:, u, :, WIN:WID], dst_hot[:, u, :, 0:WIN],
                                        weight[:, halves].unsqueeze(2).broadcast_to([P, 2 * WPT, WIN]),
                                        ALU.mult).then_inc(made, 1)
                dve.wait_ge(made, t * PER + 3)
                for q in range(NGRP):
                    b = (NGRP * u + q) % 2
                    dve.wait_ge(grouped, t * NGRP + (q + 1))
                    nc.vector.tensor_tensor(lo_hot[:, b],
                                            src_lo[:, bass.ds(t * (2 * WPT) + q * G, G)].unsqueeze(2).broadcast_to([P, G, P]),
                                            iota[:].unsqueeze(1).broadcast_to([P, G, P]),
                                            ALU.is_equal).then_inc(made, 1)
                    part = slice(q * G, (q + 1) * G)
                    nc.vector.tensor_tensor(pair_hot[:, b].rearrange("p g (a k) -> p g a k", k=WID),
                                            tile_hot[:, u, part].unsqueeze(3).broadcast_to([P, G, TILES, WID]),
                                            dst_hot[:, u, part].unsqueeze(2).broadcast_to([P, G, TILES, WID]),
                                            ALU.mult).then_inc(made, 1)

            in_pairs(dve, tile)
            dve.wait_ge(added, 1 + TILES)
            nc.vector.tensor_reduce(out_degree[:], degree_parts[:].rearrange("p t a -> p a t"), axis=AX.X, op=ALU.add)

        @block.tensor
        def _(pe):
            pe.sem_inc(grouped, 2)

            def tile(t, u):
                for q in range(NGRP):
                    b = (NGRP * u + q) % 2
                    pe.wait_ge(made, t * PER + (3 + 2 * (q + 1)))
                    pe.wait_ge(copied, t * (2 * NGRP) + 2 * (q + 1))
                    for w in range(GRP):
                        for h in range(2):
                            ins = nc.tensor.matmul(built[b][:, 256 * w:256 * w + TILES * WID], lo_hot[:, b, 2 * w + h],
                                                   pair_hot[:, b, 2 * w + h], start=(h == 0), stop=(h == 1))
                    ins.then_inc(grouped, 1)
                pe.wait_ge(copied, t * (2 * NGRP) + (4 + 2 * NGRP))
                pe.wait_ge(added, t + 1)
                for r in range(ROUNDS):
                    b = r % 2
                    pe.wait_ge(straight, t * ROUNDS + (r + 1) + (1 if r == 0 else 0))
                    for a in range(4 * r, min(4 * r + 4, TILES)):
                        ins = nc.tensor.transpose(flipped[:, b, (a % 4) * P:(a % 4 + 1) * P],
                                                  cT[:, u, a * P:(a + 1) * P], ident[0:P, 0:P])
                    ins.then_inc(turned, 1)
                pe.wait_ge(straight, t * ROUNDS + (2 + ROUNDS))
                for a in range(TILES):
                    ins = nc.tensor.matmul(flipped[:, 0, 256 + a:257 + a], cc[:, u, a * P:(a + 1) * P], ones[0:P, 0:1],
                                           start=True, stop=True)
                ins.then_inc(summed, 1)

            in_pairs(pe, tile)

        @block.scalar
        def _(act):
            act.sem_inc(copied, 4)
            act.sem_inc(straight, 2)
            act.sem_inc(added, 1)

            def tile(t, u):
                act.wait_ge(free, t + 1)
                for q in range(NGRP):
                    b = (NGRP * u + q) % 2
                    act.wait_ge(grouped, t * NGRP + (q + 3))
                    seen = built[b][:, 0:256 * GRP].rearrange("p (w k) -> p w k", k=256)[:, :, 0:TILES * WID]
                    seen = seen.rearrange("p w (a k) -> p w a k", k=WID)
                    for out, k in ((cT, 0), (wT, WIN)):
                        o = out[:, u, :].rearrange("p (a w k) -> p w a k", w=WPT, k=WIN)[:, q * GRP:(q + 1) * GRP]
                        nc.scalar.copy(o, seen[:, :, :, k:k + WIN]).then_inc(copied, 1)
                for r in range(ROUNDS):
                    b = r % 2
                    n = min(4, TILES - 4 * r) * P
                    act.wait_ge(turned, t * ROUNDS + (r + 1))
                    nc.scalar.activation(cc[:, u, 4 * P * r:4 * P * r + n], flipped[:, b, 0:n], ACT.Copy,
                                         accum_out=in_parts[:, bass.ds(t, 1), r:r + 1].rearrange("p o f -> p (o f)")
                                         ).then_inc(straight, 1)
                act.wait_ge(summed, t + 1)
                nc.scalar.copy(row_of(degree_parts, t), flipped[:, 0, 256:256 + TILES]).then_inc(added, 1)

            in_pairs(act, tile)

        @block.sync
        def _(sp):
            sp.sem_inc(free, 2)

            def tile(t, u):
                sp.wait_ge(copied, t * (2 * NGRP) + (4 + 2 * NGRP))
                row = lambda d: d[bass.ds(t, 1)].rearrange("o p n -> (o p) n")
                sp.dma_start(row(countsT), cT[:, u, :]).then_inc(stored[u], 16)
                sp.dma_start(row(weightsT), wT[:, u, :]).then_inc(stored[u], 16)
                sp.wait_ge(straight, t * ROUNDS + (2 + ROUNDS))
                sp.dma_start(row(counts), cc[:, u, :]).then_inc(stored[u], 16)
                sp.wait_ge(stored[u], (t - u) * 24 + 48)
                sp.sem_inc(free, 1)

            in_pairs(sp, tile)


def in_turns(eng, body, k, n=TILES):
    assert n % k == 0
    with eng.Fori(0, n // k) as i:
        for u in range(k):
            body(i * k + u, u)


def quads():
    return [(r, 4 * r, min(4, TILES - 4 * r)) for r in range((TILES + 3) // 4)]


def turn_tiles(nc, pe, X, ident, flipped, turned, moved, before):
    for r, a0, n in quads():
        if r >= 2:
            pe.wait_ge(moved, before + r - 1)
        for a in range(a0, a0 + n):
            ins = nc.tensor.transpose(flipped[:, r % 2, (a - a0) * P:(a - a0 + 1) * P], X[:, a, :], ident[0:P, 0:P])
        ins.then_inc(turned, 1)


def move_tiles(nc, act, XT, flipped, turned, moved, before):
    for r, a0, n in quads():
        act.wait_ge(turned, before + r + 1)
        nc.scalar.copy(XT[:, a0 * P:(a0 + n) * P], flipped[:, r % 2, 0:n * P]).then_inc(moved, 1)


def load_weights(nc, T, W, ident):
    turned_names = [("W0", T["L0_gnn_W"]), ("Ws0", T["L2_gnn_W_self"][0]), ("Ws1", T["L2_gnn_W_self"][1]),
                    ("Wn0", T["L2_gnn_W_neigh"][0]), ("Wn1", T["L2_gnn_W_neigh"][1]), ("Wa", T["L2_gnn_W_agg"])]
    with ExitStack() as c:
        e = c.enter_context
        raw = e(nc.sbuf_tensor(unique("raw"), [D, len(turned_names), D], F32))
        parts = e(nc.sbuf_tensor(unique("parts"), [1, 6, D], F32))
        flipped = e(nc.psum_tensor(unique("flipped_w"), [D, 2, 512], F32))
        raw_in = e(nc.semaphore(unique("raw_in")))
        rest_in = e(nc.semaphore(unique("rest_in")))
        turned = e(nc.semaphore(unique("w_turned")))
        moved = e(nc.semaphore(unique("w_moved")))
        block = e(nc.Block())

        @block.sync
        def _(sp):
            for k, (_, w) in enumerate(turned_names):
                sp.dma_start(raw[:, k, :], w).then_inc(raw_in, 16)
            for k, name in enumerate(("Wq", "Wk", "Wv")):
                sp.dma_start(W[name][:].rearrange("i (h o) -> i h o", h=HEADS),
                             T["L1_gnn_" + name].rearrange("h i o -> i h o")).then_inc(rest_in, 16)
            sp.dma_start(W["W3"][:], T["L3_gnn_W"]).then_inc(rest_in, 16)
            rows = [T["L2_gnn_b_self"], T["L2_gnn_b_neigh"], T["L2_gnn_layer_bias"]]
            for k, b in enumerate(rows):
                sp.dma_start(parts[0:1, 2 * k:2 * k + 2, :], b.rearrange("(o l) d -> o l d", o=1)).then_inc(rest_in, 16)
            for k, name in enumerate(("L0_gnn_b", "L2_gnn_b_agg", "L3_gnn_b")):
                sp.dma_start(W["bias"][0:1, k, :], T[name].rearrange("(o d) -> o d", o=1)).then_inc(rest_in, 16)
            sp.wait_ge(rest_in, 16 * 10)

        @block.tensor
        def _(pe):
            pe.wait_ge(raw_in, 16 * len(turned_names))
            for k in range(len(turned_names)):
                ins = nc.tensor.transpose(flipped[:, k // 4, (k % 4) * D:(k % 4 + 1) * D], raw[:, k, :], ident[:])
            ins.then_inc(turned, 1)

        @block.vector
        def _(dve):
            dve.wait_ge(turned, 1)
            for k, (name, _) in enumerate(turned_names):
                nc.vector.tensor_copy(W[name][:], flipped[:, k // 4, (k % 4) * D:(k % 4 + 1) * D])
            dve.wait_ge(rest_in, 16 * 10)
            nc.vector.tensor_tensor(parts[0:1, 0:2, :], parts[0:1, 0:2, :], parts[0:1, 2:4, :], ALU.add).then_inc(moved, 1)
            dve.wait_ge(moved, 1)
            nc.vector.tensor_tensor(W["bias"][0:1, 3:5, :], parts[0:1, 0:2, :], parts[0:1, 4:6, :], ALU.add)


def gcn_layer(nc, counts, X, H, W, ones, out_degree):
    BUFS = 5
    with ExitStack() as c:
        e = c.enter_context
        block_in = e(nc.sbuf_tensor(unique("counts_in"), [P, BUFS, N], F32))
        scaled = e(nc.sbuf_tensor(unique("scaled"), [P, BUFS, D], F32))
        inv = e(nc.sbuf_tensor(unique("inv"), [P, TILES], F32))
        some = e(nc.sbuf_tensor(unique("some"), [P, TILES], F32))
        aggT = e(nc.sbuf_tensor(unique("aggT"), [D, N], F32))
        agg = e(nc.psum_tensor(unique("agg"), [D, 7, 512], F32))
        last = e(nc.psum_tensor(unique("last_bank"), [P, 512], F32))
        loaded = [e(nc.semaphore(unique(f"loaded{u}"))) for u in range(BUFS)]
        used = e(nc.semaphore(unique("used")))
        scaled_done = e(nc.semaphore(unique("scaled_done")))
        bias_done = e(nc.semaphore(unique("bias_done")))
        agg_moved = e(nc.semaphore(unique("agg_moved")))
        inv_done = e(nc.semaphore(unique("inv_done")))
        root_ready = e(nc.semaphore(unique("root_ready")))
        root_done = e(nc.semaphore(unique("root_done")))
        lin_done = e(nc.semaphore(unique("lin_done")))
        lin_added = e(nc.semaphore(unique("lin_added")))
        block = e(nc.Block())

        @block.sync
        def _(sp):
            def tile(t, u):
                sp.wait_ge(used, t + 1)
                sp.dma_start(block_in[:, u, :], counts[bass.ds(t, 1)].rearrange("o p n -> (o p) n")).then_inc(loaded[u], 16)

            in_turns(sp, tile, BUFS)

        @block.scalar
        def _(act):
            act.wait_ge(root_ready, 1)
            nc.scalar.activation(inv[:], inv[:], ACT.Sqrt).then_inc(root_done, 1)
            act.wait_ge(used, BUFS + TILES)
            for k in range(7):
                n = min(512, N - 512 * k)
                if k % 2:
                    nc.scalar.copy(aggT[:, 512 * k:512 * k + n], agg[:, k, 0:n]).then_inc(agg_moved, 1)

        @block.vector
        def _(dve):
            link = chained(dve, inv_done)
            link(nc.vector.tensor_scalar(some[:], out_degree[:], 0.0, None, ALU.is_gt))
            nc.vector.tensor_scalar(inv[:], out_degree[:], 1.0, None, ALU.max).then_inc(root_ready, 1)
            dve.wait_ge(root_done, 1)
            link(nc.vector.reciprocal(inv[:], inv[:]))
            link(nc.vector.tensor_tensor(inv[:], inv[:], some[:], ALU.mult))

            def tile(t, u):
                dve.wait_ge(used, t + 1)
                nc.vector.tensor_scalar(scaled[:, u, :], row_of(H, t), inv[:, bass.ds(t, 1)], None,
                                        ALU.mult).then_inc(scaled_done, 1)

            in_turns(dve, tile, BUFS)
            dve.wait_ge(bias_done, 1)
            link(nc.vector.tensor_tensor(X[:], X[:], last[:, 0:D].unsqueeze(1).broadcast_to([P, TILES, D]), ALU.add))
            dve.wait_ge(used, BUFS + TILES)
            for k in range(0, 7, 2):
                n = min(512, N - 512 * k)
                nc.vector.tensor_copy(aggT[:, 512 * k:512 * k + n], agg[:, k, 0:n]).then_inc(agg_moved, 1)
            for r, a0, n in quads():
                dve.wait_ge(lin_done, r + 1)
                for a in range(a0, a0 + n):
                    ins = nc.vector.scalar_tensor_tensor(X[:, a, :], agg[0:P, r % 2, (a - a0) * D:(a - a0 + 1) * D],
                                                         inv[:, a:a + 1], X[:, a, :], ALU.mult, ALU.add)
                ins.then_inc(lin_added, 1)

        @block.tensor
        def _(pe):
            pe.sem_inc(used, BUFS)
            nc.tensor.matmul(last[:, 0:D], ones[0:1, 0:P], W["bias"][0:1, 0, :], start=True, stop=True).then_inc(bias_done, 1)

            def turn(i, first=False, last_turn=False):
                for u in range(BUFS):
                    pe.wait_ge(scaled_done, i * BUFS + (u + 1))
                    pe.wait_ge(loaded[u], i * 16 + 16)
                    for k in range(7):
                        n = min(512, N - 512 * k)
                        ins = nc.tensor.matmul(agg[:, k, 0:n], scaled[:, u, :], block_in[:, u, 512 * k:512 * k + n],
                                               start=(first and u == 0), stop=(last_turn and u == BUFS - 1))
                    ins.then_inc(used, 1)

            turn(0, first=True)
            with pe.Fori(1, TILES // BUFS - 1) as i:
                turn(i)
            turn(TILES // BUFS - 1, last_turn=True)
            pe.wait_ge(agg_moved, 7)
            for r, a0, n in quads():
                if r >= 2:
                    pe.wait_ge(lin_added, r - 1)
                for a in range(a0, a0 + n):
                    ins = nc.tensor.matmul(agg[0:P, r % 2, (a - a0) * D:(a - a0 + 1) * D], aggT[:, a * P:(a + 1) * P],
                                           W["W0"][:], start=True, stop=True)
                ins.then_inc(lin_done, 1)


def normalize(nc, X, H, HT, stats, mv, rstd, ident):
    with ExitStack() as c:
        e = c.enter_context
        flipped = e(nc.psum_tensor(unique("flipped_h"), [D, 2, 512], F32))
        normed = e(nc.semaphore(unique("normed")))
        var_ready = e(nc.semaphore(unique("var_ready")))
        std_ready = e(nc.semaphore(unique("std_ready")))
        h_ready = e(nc.semaphore(unique("h_ready")))
        turned = e(nc.semaphore(unique("h_turned")))
        moved = e(nc.semaphore(unique("h_moved")))
        block = e(nc.Block())

        @block.vector
        def _(dve):
            layer_norm_relu(nc, dve, chained(dve, normed), X, H, stats, mv, rstd, var_ready, std_ready)
            dve.sem_inc(h_ready, 1)

        @block.scalar
        def _(act):
            standard_deviation(nc, act, rstd, var_ready, std_ready)
            move_tiles(nc, act, HT, flipped, turned, moved, 0)

        @block.tensor
        def _(pe):
            pe.wait_ge(h_ready, 1)
            turn_tiles(nc, pe, H, ident, flipped, turned, moved, 0)


def turn(nc, Y, YT, ident):
    with ExitStack() as c:
        e = c.enter_context
        flipped = e(nc.psum_tensor(unique("flipped_y"), [D, 2, 512], F32))
        turned = e(nc.semaphore(unique("y_turned")))
        moved = e(nc.semaphore(unique("y_moved")))
        block = e(nc.Block())

        @block.scalar
        def _(act):
            move_tiles(nc, act, YT, flipped, turned, moved, 0)

        @block.tensor
        def _(pe):
            turn_tiles(nc, pe, Y, ident, flipped, turned, moved, 0)


def project(nc, HT, W, QA, QB, KA, KB, V):
    CH = 500
    pieces = [(k, CH * k, min(CH, N - CH * k)) for k in range((N + CH - 1) // CH)]
    n = len(pieces)
    with ExitStack() as c:
        e = c.enter_context
        part = [[e(nc.sbuf_tensor(unique("part"), [D, N], BF16)) for _ in range(3)] for _ in range(2)]
        rest = e(nc.sbuf_tensor(unique("rest"), [D, 2, CH], F32))
        out = e(nc.psum_tensor(unique("projection"), [D, 2, 512], F32))
        multiplied = e(nc.semaphore(unique("projected")))
        first = e(nc.semaphore(unique("first_parts")))
        split = e(nc.semaphore(unique("split")))
        v_ready = e(nc.semaphore(unique("v_multiplied")))
        v_moved = e(nc.semaphore(unique("v_moved")))
        spread = e(nc.semaphore(unique("spread")))
        block = e(nc.Block())

        @block.tensor
        def _(pe):
            for m, name in enumerate(("Wq", "Wk")):
                for k, at, w in pieces:
                    p = m * n + k
                    if p >= 2:
                        pe.wait_ge(split, 3 * (p - 1))
                    nc.tensor.matmul(out[:, p % 2, 0:w], W[name][:], HT[:, at:at + w], start=True, stop=True).then_inc(multiplied, 1)
            pe.wait_ge(split, 3 * 2 * n)
            for r, a0, m in quads():
                if r >= 2:
                    pe.wait_ge(v_moved, r - 1)
                for a in range(a0, a0 + m):
                    ins = nc.tensor.matmul(out[0:P, r % 2, (a - a0) * D:(a - a0 + 1) * D], HT[:, a * P:(a + 1) * P],
                                           W["Wv"][:], start=True, stop=True)
                ins.then_inc(v_ready, 1)

        @block.scalar
        def _(act):
            for m in range(2):
                for k, at, w in pieces:
                    p = m * n + k
                    act.wait_ge(multiplied, p + 1)
                    nc.scalar.copy(part[m][0][:, at:at + w], out[:, p % 2, 0:w]).then_inc(first, 1)
            for r, a0, m in quads():
                act.wait_ge(v_ready, r + 1)
                nc.scalar.copy(V[:, a0:a0 + m, :, 0:HID],
                               out[0:P, r % 2, 0:m * D].rearrange("p (a h o) -> p a h o", h=HEADS, o=HID)).then_inc(v_moved, 1)

        @block.vector
        def _(dve):
            nc.vector.memset(V[:, :, :, HID:HID + 1], 1.0)
            for m in range(2):
                for k, at, w in pieces:
                    p = m * n + k
                    dve.wait_ge(first, p + 1)
                    here = slice(at, at + w)
                    r = rest[:, p % 2, 0:w]
                    nc.vector.tensor_tensor(r, out[:, p % 2, 0:w], part[m][0][:, here], ALU.subtract).then_inc(split, 1)
                    dve.wait_ge(split, 3 * p + 1)
                    nc.vector.tensor_copy(part[m][1][:, here], r).then_inc(split, 1)
                    dve.wait_ge(split, 3 * p + 2)
                    nc.vector.tensor_tensor(part[m][2][:, here], r, part[m][1][:, here], ALU.subtract).then_inc(split, 1)

        @block.sync
        def _(sp):
            count = 0
            for m, (A, B, rows_a, rows_b) in enumerate(((QA, QB, (0, 1, 0, 1), (2, 0)), (KA, KB, (0, 0, 1, 1), (0, 2)))):
                sp.wait_ge(split, 3 * n * (m + 1))
                for h in range(HEADS):
                    head = slice(h * HID, (h + 1) * HID)
                    for k, which in enumerate(rows_a):
                        sp.dma_start(A[k * HID:(k + 1) * HID, h, :], part[m][which][head, :]).then_inc(spread, 16)
                    for k, which in enumerate(rows_b):
                        at = 64 * (h % 2) + k * HID
                        sp.dma_start(B[at:at + HID, h // 2, :], part[m][which][head, :]).then_inc(spread, 16)
                    count += 6
            sp.wait_ge(spread, 16 * count)


def attention(nc, counts, countsT, X, H, QA, QB, KA, KB, V, ident):
    PW = 1000
    PIECES = (N + PW - 1) // PW
    QUADS = len(quads())
    width = [min(PW, N - PW * j) for j in range(PIECES)]
    with ExitStack() as c:
        e = c.enter_context
        count_in = e(nc.sbuf_tensor(unique("count_in"), [P, N], F32))
        countT_in = e(nc.sbuf_tensor(unique("countT_in"), [P, 2, N], F32))
        absent = e(nc.sbuf_tensor(unique("absent"), [P, 2, N], BF16))
        low = e(nc.sbuf_tensor(unique("low"), [P, P], BF16))
        key_a = e(nc.sbuf_tensor(unique("key_a"), [D, 2, HEADS, P], BF16))
        key_b = e(nc.sbuf_tensor(unique("key_b"), [D, 2, HEADS, P], BF16))
        score1 = e(nc.sbuf_tensor(unique("score1"), [P, N], F32))
        score = [H[:].rearrange("p t d -> p (t d)")[:, 0:N], score1[:]]
        rising = e(nc.sbuf_tensor(unique("rising"), [P, 2, PW], F32))
        weighed = e(nc.sbuf_tensor(unique("weighed"), [P, 4, 4 * P], F32))
        peaks = e(nc.sbuf_tensor(unique("peaks"), [P, 2, PIECES], F32))
        shift = e(nc.sbuf_tensor(unique("shift"), [P, 2, 2], F32))
        norm = e(nc.sbuf_tensor(unique("norm"), [P, 2 * HEADS], F32))
        heads_out = e(nc.sbuf_tensor(unique("heads_out"), [P, HEADS, HID], F32))
        raw = [e(nc.psum_tensor(unique(f"raw{b}"), [P, 2, 512], F32)) for b in range(2)]
        probsT = e(nc.psum_tensor(unique("probsT"), [P, 2, 512], F32))
        mixed = e(nc.psum_tensor(unique("mixed_values"), [P, HEADS, HID + 1], F32))
        c_loaded = e(nc.semaphore(unique("c_loaded")))
        ct_loaded = [e(nc.semaphore(unique(f"ct_loaded{u}"))) for u in range(2)]
        low_ready = e(nc.semaphore(unique("low_ready")))
        absent_done = e(nc.semaphore(unique("absent_done")))
        vector_go = e(nc.semaphore(unique("vector_go")))
        pool_go = e(nc.semaphore(unique("pool_go")))
        keys_done = e(nc.semaphore(unique("keys_done")))
        scored = e(nc.semaphore(unique("scored")))
        scaled = e(nc.semaphore(unique("scaled")))
        leaky = e(nc.semaphore(unique("leaky")))
        shifted = e(nc.semaphore(unique("shifted")))
        exped = e(nc.semaphore(unique("exped")))
        turned = e(nc.semaphore(unique("probs_turned")))
        counted = e(nc.semaphore(unique("counted")))
        summed = e(nc.semaphore(unique("values_summed")))
        norm_steps = e(nc.semaphore(unique("norm_steps")))
        tile_out = e(nc.semaphore(unique("tile_out")))
        block = e(nc.Block())

        @block.sync
        def _(sp):
            def tile(t, u):
                row = lambda d: d[bass.ds(t, 1)].rearrange("o p n -> (o p) n")
                sp.wait_ge(absent_done, t + 1)
                sp.dma_start(count_in[:], row(counts)).then_inc(c_loaded, 16)
                sp.wait_ge(tile_out, t + 1)
                sp.dma_start(countT_in[:, u, :], row(countsT)).then_inc(ct_loaded[u], 16)

            in_pairs(sp, tile)

        @block.gpsimd
        def _(pool):
            nc.gpsimd.memset(key_b[:], 0.0).then_inc(keys_done, 1)
            pool.sem_inc(absent_done, 1)
            pool.wait_ge(keys_done, 1)

            def tile(t, u):
                pool.wait_ge(tile_out, t + 1)
                pool.sem_inc(pool_go, 1)
                here = bass.ds(t * P, P)
                nc.gpsimd.tensor_copy(key_a[:, u], KA[:, :, here]).then_inc(keys_done, 1)
                for s in range(2):
                    pool.wait_ge(keys_done, t * 3 + (2 + s))
                    pool.sem_inc(pool_go, 1)
                    rows = slice(64 * s, 64 * s + 64)
                    nc.gpsimd.tensor_copy(key_b[rows, u].rearrange("p (j s) n -> p s j n", s=2)[:, s], KB[rows, :, here]).then_inc(keys_done, 1)
                pool.wait_ge(c_loaded, t * 16 + 16)
                pool.wait_ge(keys_done, t * 3 + 4)
                pool.sem_inc(pool_go, 1)
                nc.gpsimd.tensor_scalar(absent[:, u, :], count_in[:], 0.0, None, ALU.is_equal).then_inc(absent_done, 1)

            in_pairs(pool, tile)

        @block.tensor
        def _(pe):
            pe.sem_inc(summed, 4)
            pe.wait_ge(low_ready, 1)

            def scores(t, u, h):
                if h == 0:
                    pe.wait_ge(absent_done, t + 2)
                    pe.wait_ge(keys_done, t * 3 + 4)
                for j, w in enumerate(width):
                    pe.wait_ge(leaky, t * (HEADS * PIECES) + (h * PIECES + j + 1))
                    halves = [(b, PW * j + 500 * b, min(500, w - 500 * b)) for b in range(2) if w > 500 * b]
                    for b, at, m in halves:
                        out = raw[j % 2][:, b, 0:m]
                        nc.tensor.matmul(out, key_a[:, u, h, :], QA[:, h, at:at + m], start=True, stop=False)
                        nc.tensor.matmul(out, key_b[:, u, h, :], QB[:, h // 2, at:at + m], start=False, stop=False)
                        ins = nc.tensor.matmul(out, low[:], absent[:, u, at:at + m], start=False, stop=True)
                    ins.then_inc(scored, 1)

            def values(t, u, h):
                pe.wait_ge(exped, t * HEADS + (h + 1))
                if h == 0:
                    pe.wait_ge(tile_out, t + 2)
                base = h * QUADS

                def sum_quad(r, a0, m):
                    pe.wait_ge(counted, t * (HEADS * QUADS) + (base + r + 3))
                    for a in range(a0, a0 + m):
                        ins = nc.tensor.matmul(mixed[:, h, :], weighed[:, (base + r) % 4, (a - a0) * P:(a - a0 + 1) * P],
                                               V[:, a, h, :], start=(a == 0), stop=(a == TILES - 1))
                    ins.then_inc(summed, 1)

                before = None
                for r, a0, m in quads():
                    pe.wait_ge(counted, t * (HEADS * QUADS) + (base + r + 1))
                    for a in range(a0, a0 + m):
                        ins = nc.tensor.transpose(probsT[:, (base + r) % 2, (a - a0) * P:(a - a0 + 1) * P],
                                                  score[h % 2][:, a * P:(a + 1) * P], ident[0:P, 0:P])
                    ins.then_inc(turned, 1)
                    if before:
                        sum_quad(*before)
                    before = (r, a0, m)
                sum_quad(*before)

            scores(0, 0, 0)

            def tile(t, u, last=False):
                for h in range(HEADS):
                    if h + 1 < HEADS:
                        scores(t, u, h + 1)
                    elif not last:
                        scores(t + 1, 1 - u, 0)
                    values(t, u, h)

            with pe.Fori(0, TILES // 2) as i:
                tile(i * 2, 0)
                tile(i * 2 + 1, 1)
            tile(TILES - 1, 0, last=True)

        @block.scalar
        def _(act):
            def scores(t, u, h):
                for j, w in enumerate(width):
                    act.wait_ge(scored, t * (HEADS * PIECES) + (h * PIECES + j + 1))
                    act.wait_ge(leaky, t * (HEADS * PIECES) + (h * PIECES + j + 1))
                    if w > 500:
                        src, out = raw[j % 2][:, :, 0:500], rising[:, j % 2, :].rearrange("p (b n) -> p b n", b=2)
                    else:
                        src, out = raw[j % 2][:, 0, 0:w], rising[:, j % 2, 0:w]
                    nc.scalar.activation(out, src, ACT.Relu, scale=1.0 / SLOPE - 1.0).then_inc(scaled, 1)
                act.wait_ge(shifted, t * (2 * HEADS) + (2 * h + 2))
                nc.scalar.activation(score[h % 2], score[h % 2], ACT.Exp, bias=shift[:, h % 2, 1:2]).then_inc(exped, 1)

            def tile(t, u):
                for h in range(HEADS):
                    scores(t, u, h)

            in_pairs(act, tile)

        @block.vector
        def _(dve):
            dve.sem_inc(leaky, 2)
            dve.sem_inc(counted, 2)
            dve.sem_inc(tile_out, 2)
            nc.vector.tensor_scalar(low[:], ident[0:P, 0:P], -1e30, None, ALU.mult).then_inc(low_ready, 1)

            def scores(t, u, h):
                b = h % 2
                for j, w in enumerate(width):
                    dve.wait_ge(scaled, t * (HEADS * PIECES) + (h * PIECES + j + 1))
                    dve.sem_inc(vector_go, 1)
                    if w > 500:
                        two = lambda x: x.rearrange("p (b n) -> p b n", b=2)
                        out, in0, in1 = two(score[b][:, PW * j:PW * j + w]), raw[j % 2][:, :, 0:500], two(rising[:, j % 2, :])
                    else:
                        out, in0, in1 = score[b][:, PW * j:PW * j + w], raw[j % 2][:, 0, 0:w], rising[:, j % 2, 0:w]
                    nc.vector.tensor_tensor_reduce(out=out, in0=in0, in1=in1, scale=SLOPE, scalar=-3e38, op0=ALU.add,
                                                   op1=ALU.max, accum_out=peaks[:, b, j:j + 1]).then_inc(leaky, 1)
                dve.wait_ge(leaky, t * (HEADS * PIECES) + ((h + 1) * PIECES + 2))
                nc.vector.tensor_reduce(shift[:, b, 0:1], peaks[:, b, :], axis=AX.X, op=ALU.max).then_inc(shifted, 1)
                dve.wait_ge(shifted, t * (2 * HEADS) + (2 * h + 1))
                nc.vector.tensor_scalar(shift[:, b, 1:2], shift[:, b, 0:1], -1.0, None, ALU.mult).then_inc(shifted, 1)

            def values(t, u, h):
                base = h * QUADS
                if h == 0:
                    dve.wait_ge(ct_loaded[u], (t - u) * 8 + 16)
                for r, a0, m in quads():
                    dve.wait_ge(turned, t * (HEADS * QUADS) + (base + r + 1))
                    dve.wait_ge(summed, t * (HEADS * QUADS) + (base + r + 1))
                    nc.vector.tensor_tensor(weighed[:, (base + r) % 4, 0:m * P], probsT[:, (base + r) % 2, 0:m * P],
                                            countT_in[:, u, a0 * P:(a0 + m) * P], ALU.mult).then_inc(counted, 1)

            def finish(t):
                dve.wait_ge(summed, t * (HEADS * QUADS) + (HEADS * QUADS + 4))
                nc.vector.tensor_scalar(norm[:, 0:HEADS], mixed[:, :, HID], 1e-9, None, ALU.max).then_inc(norm_steps, 1)
                dve.wait_ge(norm_steps, t * 3 + 1)
                nc.vector.reciprocal(norm[:, HEADS:], norm[:, 0:HEADS]).then_inc(norm_steps, 1)
                dve.wait_ge(norm_steps, t * 3 + 2)
                nc.vector.tensor_tensor(heads_out[:], mixed[:, :, 0:HID],
                                        norm[:, HEADS:].unsqueeze(2).broadcast_to([P, HEADS, HID]), ALU.mult).then_inc(norm_steps, 1)
                dve.wait_ge(norm_steps, t * 3 + 3)
                nc.vector.tensor_tensor(row_of(X, t), row_of(X, t), heads_out[:].rearrange("p h o -> p (h o)"),
                                        ALU.add).then_inc(tile_out, 1)

            scores(0, 0, 0)

            def tile(t, u, last=False):
                for h in range(HEADS):
                    if h + 1 < HEADS:
                        scores(t, u, h + 1)
                    elif not last:
                        scores(t + 1, 1 - u, 0)
                    values(t, u, h)
                finish(t)

            with dve.Fori(0, TILES // 2) as i:
                tile(i * 2, 0)
                tile(i * 2 + 1, 1)
            tile(TILES - 1, 0, last=True)


def one_over_degree(nc, in_parts, per_node):
    with nc.semaphore(unique("degree_done")) as degree_done, nc.Block() as block:
        @block.vector
        def _(dve):
            link = chained(dve, degree_done)
            link(nc.vector.tensor_reduce(per_node[:], in_parts[:], axis=AX.X, op=ALU.add))
            link(nc.vector.tensor_scalar(per_node[:], per_node[:], 1.0, None, ALU.add))
            link(nc.vector.reciprocal(per_node[:], per_node[:]))


def weighted_step(nc, weightsT, Y, YT, Z, W, ones, per_node, step):
    BUFS = 5
    with ExitStack() as c:
        e = c.enter_context
        block_in = e(nc.sbuf_tensor(unique("weights_in"), [P, BUFS, N], F32))
        own = e(nc.sbuf_tensor(unique("own"), [D, BUFS, P], F32))
        total = e(nc.sbuf_tensor(unique("total"), [D, BUFS, P], F32))
        self_part = e(nc.sbuf_tensor(unique("self_part"), [P, D], F32))
        mixed = e(nc.sbuf_tensor(unique("mixed"), [P, D], F32))
        agg = e(nc.psum_tensor(unique("agg"), [D, BUFS, 512], F32))
        lin = e(nc.psum_tensor(unique("lin"), [P, 2 * D], F32))
        loaded = [e(nc.semaphore(unique(f"w_loaded{u}"))) for u in range(BUFS)]
        summed = e(nc.semaphore(unique("agg_summed")))
        own_ready = e(nc.semaphore(unique("own_ready")))
        totalled = e(nc.semaphore(unique("totalled")))
        applied = e(nc.semaphore(unique("applied")))
        self_copied = e(nc.semaphore(unique("self_copied")))
        mixed_done = e(nc.semaphore(unique("mixed_done")))
        z_done = e(nc.semaphore(unique("z_done")))
        block = e(nc.Block())

        @block.sync
        def _(sp):
            def tile(t, u):
                sp.wait_ge(summed, t + 1)
                sp.dma_start(block_in[:, u, :], weightsT[bass.ds(t, 1)].rearrange("o p n -> (o p) n")).then_inc(loaded[u], 16)

            in_turns(sp, tile, BUFS)

        @block.scalar
        def _(act):
            def copy_own(t, u):
                act.wait_ge(applied, t + 1)
                nc.scalar.copy(own[:, u, :], YT[:, bass.ds(t * P, P)]).then_inc(own_ready, 1)

            def tile(t, u):
                copy_own(t, u)
                act.wait_ge(applied, t + (BUFS + 1))
                act.wait_ge(mixed_done, t + 1)
                nc.scalar.copy(self_part[:], lin[:, D:2 * D]).then_inc(self_copied, 1)

            in_turns(act, tile, BUFS)

        @block.vector
        def _(dve):
            dve.sem_inc(totalled, BUFS)
            dve.sem_inc(mixed_done, 1)

            def tile(t, u):
                dve.wait_ge(summed, t + (BUFS + 1))
                dve.wait_ge(own_ready, t + 1)
                nc.vector.tensor_tensor(total[:, u, :], agg[:, u, 0:P], own[:, u, :], ALU.add).then_inc(totalled, 1)
                dve.wait_ge(self_copied, t + 1)
                nc.vector.scalar_tensor_tensor(mixed[:], lin[:, 0:D], per_node[:, bass.ds(t, 1)], self_part[:],
                                               ALU.mult, ALU.add).then_inc(mixed_done, 1)
                dve.wait_ge(mixed_done, t + 2)
                nc.vector.scalar_tensor_tensor(row_of(Z, t), mixed[:], SLOPE, mixed[:], ALU.mult,
                                               ALU.max).then_inc(z_done, 1)

            in_turns(dve, tile, BUFS)

        @block.tensor
        def _(pe):
            pe.sem_inc(summed, BUFS)
            pe.sem_inc(applied, BUFS)

            def tile(t, u, i):
                pe.wait_ge(loaded[u], i * 16 + 16)
                pe.wait_ge(totalled, t + 1)
                for a in range(TILES):
                    ins = nc.tensor.matmul(agg[:, u, 0:P], Y[:, a, :], block_in[:, u, a * P:(a + 1) * P],
                                           start=(a == 0), stop=(a == TILES - 1))
                ins.then_inc(summed, 1)
                pe.wait_ge(totalled, t + (BUFS + 1))
                pe.wait_ge(mixed_done, t + 1)
                nc.tensor.matmul(lin[:, 0:D], total[:, u, :], W[f"Wn{step}"][:], start=True, stop=True)
                nc.tensor.matmul(lin[:, D:2 * D], own[:, u, :], W[f"Ws{step}"][:], start=True, stop=False)
                nc.tensor.matmul(lin[:, D:2 * D], ones[0:1, 0:P], W["bias"][0:1, 3 + step, :], start=False,
                                 stop=True).then_inc(applied, 1)

            with pe.Fori(0, TILES // BUFS) as i:
                for u in range(BUFS):
                    tile(i * BUFS + u, u, i)


def weighted_output(nc, X, YT, W, ones):
    with ExitStack() as c:
        e = c.enter_context
        lin = e(nc.psum_tensor(unique("lin"), [P, 2, 512], F32))
        bias = e(nc.psum_tensor(unique("bias_rows"), [P, D], F32))
        multiplied = e(nc.semaphore(unique("multiplied")))
        added = e(nc.semaphore(unique("rows_added")))
        block = e(nc.Block())

        @block.tensor
        def _(pe):
            nc.tensor.matmul(bias[:], ones[0:1, 0:P], W["bias"][0:1, 1, :], start=True, stop=True)
            for r, a0, n in quads():
                if r >= 2:
                    pe.wait_ge(added, r)
                for a in range(a0, a0 + n):
                    ins = nc.tensor.matmul(lin[:, r % 2, (a - a0) * D:(a - a0 + 1) * D], YT[:, a * P:(a + 1) * P],
                                           W["Wa"][:], start=True, stop=True)
                ins.then_inc(multiplied, 1)

        @block.vector
        def _(dve):
            dve.wait_ge(multiplied, 1)
            nc.vector.tensor_tensor(X[:], X[:], bias[:].unsqueeze(1).broadcast_to([P, TILES, D]), ALU.add).then_inc(added, 1)
            dve.wait_ge(added, 1)
            for r, a0, n in quads():
                dve.wait_ge(multiplied, r + 1)
                part = X[:, a0:a0 + n, :].rearrange("p a d -> p (a d)")
                nc.vector.tensor_tensor(part, part, lin[:, r % 2, 0:n * D], ALU.add).then_inc(added, 1)


def edge_layer(nc, T, X, HT, W, ones, ident, projected):
    BUFS = 3
    EDGES = EG * P
    ROWS16 = EG * EDIM
    with ExitStack() as c:
        e = c.enter_context
        rows = e(nc.sbuf_tensor(unique("xw_rows"), [P, TILES, D], F32))
        src_i = e(nc.sbuf_tensor(unique("src_i"), [P, EGROUPS, EG], I32))
        dst_i = e(nc.sbuf_tensor(unique("dst_i"), [P, EGROUPS, EG], I32))
        dst_rel = e(nc.sbuf_tensor(unique("dst_rel"), [P, EGROUPS, EG], F32))
        base_i = e(nc.sbuf_tensor(unique("base_i"), [1, EGROUPS], I32))
        base_f = e(nc.sbuf_tensor(unique("base_f"), [1, EGROUPS], F32))
        span_i = e(nc.sbuf_tensor(unique("span_i"), [P, SPAN], I32))
        span = e(nc.sbuf_tensor(unique("span"), [P, SPAN], F32))
        attr = e(nc.sbuf_tensor(unique("attr"), [P, BUFS, ROWS16], F32))
        mix = e(nc.sbuf_tensor(unique("mix"), [ROWS16, EG, D], F32))
        attrT = e(nc.sbuf_tensor(unique("attrT"), [ROWS16, BUFS, P], F32))
        gathered = e(nc.sbuf_tensor(unique("gathered_rows"), [P, BUFS, EG, D], F32))
        message = e(nc.sbuf_tensor(unique("message"), [P, BUFS, EG, D], F32))
        index = e(nc.sbuf_tensor(unique("index"), [P, BUFS, EG], I32))
        hot = e(nc.sbuf_tensor(unique("hot"), [P, BUFS, EG, SPAN], F32))
        acc = e(nc.sbuf_tensor(unique("acc"), [D, N + SPAN], F32))
        with ExitStack() as c1:
            e = c1.enter_context
            lin = e(nc.psum_tensor(unique("lin"), [P, 2, 512], F32))
            bias = e(nc.psum_tensor(unique("bias_rows"), [P, D], F32))
            bases = e(nc.psum_tensor(unique("bases"), [P, EGROUPS], F32))
            edges_in = e(nc.semaphore(unique("edges_in")))
            attr_in = e(nc.semaphore(unique("attr_in")))
            mix_zero = e(nc.semaphore(unique("mix_zero")))
            pool_done = e(nc.semaphore(unique("pool_done")))
            multiplied = e(nc.semaphore(unique("multiplied")))
            copied = e(nc.semaphore(unique("rows_copied")))
            rel_done = e(nc.semaphore(unique("rel_done")))
            base_ready = e(nc.semaphore(unique("base_ready")))
            base_spread = e(nc.semaphore(unique("base_spread")))
            stored = e(nc.semaphore(unique("rows_stored")))
            block = e(nc.Block())

            @block.gpsimd
            def _(pool):
                nc.gpsimd.memset(mix[:], 0.0).then_inc(mix_zero, 1)
                nc.gpsimd.memset(acc[:], 0.0)
                nc.gpsimd.iota(span_i[:], [[1, SPAN]], base=0, channel_multiplier=0).then_inc(pool_done, 1)

            @block.sync
            def _(sp):
                with nc.allow_non_contiguous_dma(reason="runs of five edges, and one destination of every group"):
                    sp.dma_start(base_i[:], T["dst"].rearrange("(o g r) -> o g r", o=1, r=EDGES)[:, :, 0]).then_inc(edges_in, 16)
                    sp.dma_start(src_i[:], T["src"].rearrange("(g p c) -> p g c", p=P, c=EG)).then_inc(edges_in, 16)
                    sp.dma_start(dst_i[:], T["dst"].rearrange("(g p c) -> p g c", p=P, c=EG)).then_inc(edges_in, 16)
                sp.wait_ge(mix_zero, 1)
                for k in range(EG):
                    sp.dma_start(mix[k * EDIM:(k + 1) * EDIM, k, :], T["L3_gnn_edge_w"]).then_inc(attr_in, 16)
                sp.wait_ge(copied, len(quads()))
                sp.dma_start(projected.rearrange("(t p) f -> p t f", p=P), rows[:]).then_inc(stored, 16)
                sp.wait_ge(stored, 16)
                sp.wait_ge(attr_in, 16 * EG)

            @block.tensor
            def _(pe):
                for r, a0, n in quads():
                    if r >= 2:
                        pe.wait_ge(copied, r - 1)
                    for a in range(a0, a0 + n):
                        ins = nc.tensor.matmul(lin[:, r % 2, (a - a0) * D:(a - a0 + 1) * D], HT[:, a * P:(a + 1) * P],
                                               W["W3"][:], start=True, stop=True)
                    ins.then_inc(multiplied, 1)
                nc.tensor.matmul(bias[:], ones[0:1, 0:P], W["bias"][0:1, 2, :], start=True, stop=True).then_inc(base_spread, 1)
                pe.wait_ge(base_ready, 1)
                nc.tensor.matmul(bases[:], ones[0:1, 0:P], base_f[:], start=True, stop=True).then_inc(base_spread, 1)

            @block.scalar
            def _(act):
                for r, a0, n in quads():
                    act.wait_ge(multiplied, r + 1)
                    nc.scalar.copy(rows[:, a0:a0 + n, :].rearrange("p a d -> p (a d)"), lin[:, r % 2, 0:n * D]).then_inc(copied, 1)

            @block.vector
            def _(dve):
                link = chained(dve, rel_done)
                dve.wait_ge(pool_done, 1)
                nc.vector.tensor_copy(span[:], span_i[:])
                dve.wait_ge(edges_in, 48)
                nc.vector.tensor_copy(base_f[:], base_i[:]).then_inc(base_ready, 1)
                link(nc.vector.tensor_copy(dst_rel[:], dst_i[:]))
                dve.wait_ge(base_spread, 2)
                nc.vector.tensor_tensor(X[:], X[:], bias[:].unsqueeze(1).broadcast_to([P, TILES, D]), ALU.add)
                link(nc.vector.tensor_tensor(dst_rel[:], dst_rel[:], bases[:].unsqueeze(2).broadcast_to([P, EGROUPS, EG]),
                                             ALU.subtract))

        with ExitStack() as c2:
            e = c2.enter_context
            flat = e(nc.psum_tensor(unique("attr_flipped"), [ROWS16, P], F32))
            factor = [e(nc.psum_tensor(unique(f"factor{u}"), [P, 2, 512], F32)) for u in range(BUFS)]
            sums = e(nc.psum_tensor(unique("sums"), [D, SPAN], F32))
            started = e(nc.semaphore(unique("started")))
            arrived = [e(nc.semaphore(unique(f"arrived{u}"))) for u in range(BUFS)]
            attr_loaded = [e(nc.semaphore(unique(f"attr_loaded{u}"))) for u in range(BUFS)]
            turned = e(nc.semaphore(unique("attr_turned")))
            kept = e(nc.semaphore(unique("attr_kept")))
            factored = e(nc.semaphore(unique("factored")))
            made = e(nc.semaphore(unique("message_made")))
            reduced = e(nc.semaphore(unique("reduced")))
            added = e(nc.semaphore(unique("sums_added")))
            indexed = e(nc.semaphore(unique("indexed")))
            block = e(nc.Block())

            @block.sync
            def _(sp):
                attributes = T["edge_attr_16"].rearrange("(g p c) k -> g p (c k)", p=P, c=EG)

                def group(g, u):
                    sp.wait_ge(factored, g + 1)
                    sp.dma_start(attr[:, u, :], attributes[bass.ds(g, 1)].rearrange("o p n -> (o p) n")).then_inc(attr_loaded[u], 16)

                in_turns(sp, group, BUFS, EGROUPS)

            @block.gpsimd
            def _(pool):
                def group(g, u):
                    pool.wait_ge(indexed, g + 1)
                    pool.sem_inc(started, 1)
                    for k in range(EG):
                        nc.gpsimd.indirect_dma_start(gathered[:, u, k, :], None, projected,
                                                     bass.IndirectOffsetOnAxis(ap=index[:, u, k:k + 1], axis=0)
                                                     ).then_inc(arrived[u], 16)

                in_turns(pool, group, BUFS, EGROUPS)

            @block.scalar
            def _(act):
                act.sem_inc(kept, 1)

                def group(g, u):
                    act.wait_ge(made, g + 1)
                    nc.scalar.copy(index[:, u, :], row_of(src_i, g)).then_inc(indexed, 1)
                    act.wait_ge(turned, g + 1)
                    act.wait_ge(factored, g + 1)
                    nc.scalar.copy(attrT[:, u, :], flat[:]).then_inc(kept, 1)

                in_turns(act, group, BUFS, EGROUPS)

            @block.tensor
            def _(pe):
                pe.sem_inc(factored, BUFS)
                pe.sem_inc(reduced, BUFS)

                def group(g, u, i):
                    pe.wait_ge(kept, g + 1)
                    pe.wait_ge(attr_loaded[u], i * 16 + 16)
                    nc.tensor.transpose(flat[:], attr[:, u, :], ident[0:P, 0:P]).then_inc(turned, 1)
                    pe.wait_ge(kept, g + 2)
                    pe.wait_ge(made, g + 1)
                    for h in range(2):
                        ins = nc.tensor.matmul(factor[u][:, h, 0:EG * D // 2], attrT[:, u, :],
                                               mix[:].rearrange("r c d -> r (c d)")[:, h * EG * D // 2:(h + 1) * EG * D // 2],
                                               start=True, stop=True)
                    ins.then_inc(factored, 1)
                    pe.wait_ge(made, g + (BUFS + 1))
                    pe.wait_ge(added, g + 1)
                    for k in range(EG):
                        ins = nc.tensor.matmul(sums[:], message[:, u, k, :], hot[:, u, k, :], start=(k == 0),
                                               stop=(k == EG - 1))
                    ins.then_inc(reduced, 1)

                with pe.Fori(0, EGROUPS // BUFS) as i:
                    for u in range(BUFS):
                        group(i * BUFS + u, u, i)

            @block.vector
            def _(dve):
                dve.sem_inc(made, BUFS)
                dve.sem_inc(added, 1)
                with dve.Fori(0, EGROUPS // BUFS) as i:
                    for u in range(BUFS):
                        g = i * BUFS + u
                        dve.wait_ge(reduced, g + 1)
                        nc.vector.tensor_tensor(hot[:, u], dst_rel[:, bass.ds(g, 1), :].rearrange("p o c -> p (o c)").unsqueeze(2).broadcast_to([P, EG, SPAN]),
                                                span[:].unsqueeze(1).broadcast_to([P, EG, SPAN]), ALU.is_equal)
                        dve.wait_ge(factored, g + (BUFS + 1))
                        dve.wait_ge(arrived[u], i * (16 * EG) + 16 * EG)
                        nc.vector.tensor_tensor(message[:, u].rearrange("p c d -> p (c d)").rearrange("p (h n) -> p h n", h=2),
                                                gathered[:, u].rearrange("p c d -> p (c d)").rearrange("p (h n) -> p h n", h=2),
                                                factor[u][:, :, 0:EG * D // 2], ALU.mult).then_inc(made, 1)
                        base = dve.value_load(base_i[0:1, bass.ds(g, 1)], min_val=0, max_val=N - 1)
                        dve.wait_ge(reduced, g + (BUFS + 1))
                        dve.wait_ge(added, g + 1)
                        nc.vector.tensor_tensor(acc[:, bass.ds(base, SPAN)], acc[:, bass.ds(base, SPAN)], sums[:],
                                                ALU.add).then_inc(added, 1)

        with ExitStack() as c3:
            e = c3.enter_context
            back = e(nc.psum_tensor(unique("back"), [P, 2, 512], F32))
            turned = e(nc.semaphore(unique("acc_turned")))
            added = e(nc.semaphore(unique("acc_added")))
            stored = e(nc.semaphore(unique("out_stored")))
            block = e(nc.Block())

            @block.tensor
            def _(pe):
                for r, a0, n in quads():
                    if r >= 2:
                        pe.wait_ge(added, r - 1)
                    for a in range(a0, a0 + n):
                        ins = nc.tensor.transpose(back[:, r % 2, (a - a0) * D:(a - a0 + 1) * D], acc[:, a * P:(a + 1) * P], ident[:])
                    ins.then_inc(turned, 1)

            @block.vector
            def _(dve):
                for r, a0, n in quads():
                    dve.wait_ge(turned, r + 1)
                    part = X[:, a0:a0 + n, :].rearrange("p a d -> p (a d)")
                    nc.vector.tensor_tensor(part, part, back[:, r % 2, 0:n * D], ALU.add).then_inc(added, 1)

            @block.sync
            def _(sp):
                out = T["out"].rearrange("(t p) f -> p t f", p=P)
                for r, a0, n in quads():
                    sp.wait_ge(added, r + 1)
                    sp.dma_start(out[:, a0:a0 + n, :], X[:, a0:a0 + n, :]).then_inc(stored, 16)
                sp.wait_ge(stored, 16 * len(quads()))


def program(nc, T):
    dram = lambda name, shape, dt: nc.dram_tensor(name, shape, dt, kind="Internal").ap()
    table = dram("scratch_table", (ROWS + GROWS, 3 * ROW), I32)
    starts = dram("scratch_starts", (WINDOWS,), I32)
    countsT = dram("scratch_countsT", (TILES, P, N), F32)
    weightsT = dram("scratch_weightsT", (TILES, P, N), F32)
    projected = dram("scratch_projected", (N, D), F32)
    counts = dram("scratch_counts", (TILES, P, N), F32)

    def sb(name, shape, dt=F32):
        return nc.sbuf_tensor(unique(name), shape, dt)

    def ps(name, shape):
        return nc.psum_tensor(unique(name), shape, F32)

    with ExitStack() as whole:
        keep = whole.enter_context
        X = keep(sb("X", [P, TILES, D]))
        H = keep(sb("H", [P, TILES, D]))
        stats = keep(sb("stats", [P, TILES, 6]))
        mv = keep(sb("mv", [P, TILES, 2]))
        rstd = keep(sb("rstd", [P, TILES]))
        ident = keep(sb("ident", [128, 128]))
        ones = keep(sb("ones", [128, P]))
        out_degree = keep(sb("out_degree", [P, TILES]))
        in_parts = keep(sb("in_parts", [P, TILES, 7]))

        W = {name: keep(sb(name, [D, D])) for name in ("W0", "Ws0", "Ws1", "Wn0", "Wn1", "Wa", "Wq", "Wk", "Wv", "W3")}
        W["bias"] = keep(sb("bias", [1, 5, D]))

        with ExitStack() as lists:
            hold = lists.enter_context
            src_hi = hold(sb("src_hi", [P, 2 * WINDOWS]))
            src_lo = hold(sb("src_lo", [P, 2 * WINDOWS]))
            dst_in = hold(sb("dst_in", [P, 2 * WINDOWS]))
            weight = hold(sb("weight", [P, 2 * WINDOWS]))
            iota = hold(sb("iota", [P, P]))
            iota_tile = hold(sb("iota_tile", [P, TILES]))
            window_starts(nc, T, table, starts, X, H, stats, mv, rstd, ident, ones, iota, iota_tile)
            edge_slots(nc, table, starts, ident, src_hi, src_lo, dst_in, weight)
            adjacency(nc, counts, countsT, weightsT, ident, ones, src_hi, src_lo, dst_in, weight, iota,
                      iota_tile, out_degree, in_parts)
        load_weights(nc, T, W, ident)
        gcn_layer(nc, counts, X, H, W, ones, out_degree)
        per_node = keep(sb("per_node", [P, TILES]))
        one_over_degree(nc, in_parts, per_node)
        with ExitStack() as heads:
            hold = heads.enter_context
            QA = hold(sb("QA", [D, HEADS, N], BF16))
            KA = hold(sb("KA", [D, HEADS, N], BF16))
            QB = hold(sb("QB", [D, HEADS // 2, N], BF16))
            KB = hold(sb("KB", [D, HEADS // 2, N], BF16))
            V = hold(sb("V", [P, TILES, HEADS, HID + 1]))
            with sb("HT", [D, N]) as HT:
                normalize(nc, X, H, HT, stats, mv, rstd, ident)
                project(nc, HT, W, QA, QB, KA, KB, V)
            attention(nc, counts, countsT, X, H, QA, QB, KA, KB, V, ident)
        with sb("HT", [D, N]) as HT:
            normalize(nc, X, H, HT, stats, mv, rstd, ident)
            with sb("Z", [P, TILES, D]) as Z:
                weighted_step(nc, weightsT, H, HT, Z, W, ones, per_node, 0)
                turn(nc, Z, HT, ident)
                weighted_step(nc, weightsT, Z, HT, H, W, ones, per_node, 1)
                turn(nc, H, HT, ident)
            weighted_output(nc, X, HT, W, ones)
            normalize(nc, X, H, HT, stats, mv, rstd, ident)
            edge_layer(nc, T, X, HT, W, ones, ident, projected)


_INS = ['x', 'src', 'dst', 'edge_attr_16', 'edge_weight', 'L0_gnn_W', 'L0_gnn_b', 'L1_gnn_Wq', 'L1_gnn_Wk',
        'L1_gnn_Wv', 'L2_gnn_W_self', 'L2_gnn_b_self', 'L2_gnn_W_neigh', 'L2_gnn_b_neigh', 'L2_gnn_layer_bias',
        'L2_gnn_W_agg', 'L2_gnn_b_agg', 'L3_gnn_W', 'L3_gnn_edge_w', 'L3_gnn_b']


def kernel(**inputs):
    import numpy as _np
    import concourse.bacc as _bacc
    from concourse import mybir as _mybir
    from concourse.bass_utils import run_bass_kernel_spmd as _run

    nc = _bacc.Bacc("TRN2", target_bir_lowering=False, num_devices=1)
    arrays, operands = {}, {}
    for name in _INS:
        a = _np.ascontiguousarray(inputs[name])
        arrays[f"in_{name}"] = a
        operands[name] = nc.dram_tensor(f"in_{name}", a.shape, _mybir.dt.from_np(a.dtype), kind="ExternalInput").ap()
    operands["out"] = nc.dram_tensor("out_0", (N, D), F32, kind="ExternalOutput").ap()
    program(nc, operands)
    r = _run(nc, [arrays], core_ids=[0])
    return r.results[0]["out_0"]
```

```python
from contextlib import ExitStack
from itertools import count

import concourse.bass as bass
from concourse import mybir
from concourse.alu_op_type import AluOpType as ALU

F32 = mybir.dt.float32
BF16 = mybir.dt.bfloat16
I32 = mybir.dt.int32
ACT = mybir.ActivationFunctionType
AX = mybir.AxisListType

N = 3125
E = 103125
D = 128
P = 125
TILES = N // P
WIN = 5
WINDOWS = N // WIN
WPT = P // WIN
BLOCKS = WINDOWS // P
ROW = 25
ROWS = E // ROW
GROWS = 10
SLOTS = ROW * GROWS // 2
CHUNKS = E // P
MAGIC = 1.5 * 2 ** 23
GRP = 5
NGRP = WPT // GRP
EG = 5
EGROUPS = CHUNKS // EG
SPAN = 32
LN_EPS = 1e-5
SLOPE = 0.2
HEADS, HID = 4, 32
EDIM = 16


NAMES = count(1)


def unique(name):
    return f"{name}_{next(NAMES)}"


def chained(eng, sem, start=0):
    done = [start]

    def link(ins):
        done[0] += 1
        ins.then_inc(sem, 1)
        eng.wait_ge(sem, done[0])

    return link


def in_pairs(eng, body, n=TILES):
    with eng.Fori(0, n // 2) as i:
        body(i * 2, 0)
        body(i * 2 + 1, 1)
    if n % 2:
        body(n - 1, 0)


def row_of(ap3, t):
    return ap3[:, bass.ds(t, 1), :].rearrange("p o f -> p (o f)")


def floor_div(nc, link, out, x, d):
    link(nc.vector.tensor_scalar(out, x, 1.0 / d, -((d - 1) // 2) / d, ALU.mult, ALU.add))
    link(nc.vector.tensor_scalar(out, out, MAGIC, -MAGIC, ALU.add, ALU.add))


def layer_norm_relu(nc, dve, link, X, H, stats, mv, rstd, var_ready, std_ready, n=1):
    for t in range(TILES):
        ins = nc.vector.bn_stats(stats[:, t, :], X[:, t, :])
    link(ins)
    for t in range(TILES):
        ins = nc.vector.bn_aggr(mv[:, t, :], stats[:, t, :])
    link(ins)
    nc.vector.tensor_scalar(rstd[:], mv[:, :, 1], LN_EPS, None, ALU.add).then_inc(var_ready, 1)
    dve.wait_ge(std_ready, n)
    link(nc.vector.reciprocal(rstd[:], rstd[:]))
    for t in range(TILES):
        ins = nc.vector.tensor_scalar(H[:, t, :], X[:, t, :], mv[:, t, 0:1], rstd[:, t:t + 1],
                                      ALU.subtract, ALU.mult)
    link(ins)
    link(nc.vector.tensor_scalar(H[:], H[:], 0.0, None, ALU.max))


def standard_deviation(nc, act, rstd, var_ready, std_ready, n=1):
    act.wait_ge(var_ready, n)
    nc.scalar.activation(rstd[:], rstd[:], ACT.Sqrt).then_inc(std_ready, 1)


def window_starts(nc, T, table, starts, X, H, stats, mv, rstd, ident, ones, iota, iota_tile):
    with ExitStack() as c:
        e = c.enter_context
        dst_i = e(nc.sbuf_tensor(unique("dst_i"), [P, CHUNKS], I32))
        win_hi = e(nc.sbuf_tensor(unique("win_hi"), [P, CHUNKS], F32))
        win_lo = e(nc.sbuf_tensor(unique("win_lo"), [P, CHUNKS], F32))
        one_hi = e(nc.sbuf_tensor(unique("one_hi"), [P, CHUNKS, TILES], BF16))
        one_lo = e(nc.sbuf_tensor(unique("one_lo"), [P, CHUNKS, WPT], BF16))
        pad = e(nc.sbuf_tensor(unique("pad"), [GROWS, 3 * ROW], I32))
        iota_i = e(nc.sbuf_tensor(unique("iota_i"), [P, P], I32))
        iota_ti = e(nc.sbuf_tensor(unique("iota_ti"), [P, TILES], I32))
        fold = e(nc.sbuf_tensor(unique("fold"), [P, TILES], F32))
        same = e(nc.sbuf_tensor(unique("same"), [P, GRP], F32))
        before = e(nc.sbuf_tensor(unique("before"), [TILES, TILES], F32))
        pairs = e(nc.sbuf_tensor(unique("pairs"), [P, P], F32))
        hist = e(nc.sbuf_tensor(unique("hist"), [TILES, WPT], F32))
        upto = e(nc.sbuf_tensor(unique("upto"), [TILES, WPT], F32))
        zeros = e(nc.sbuf_tensor(unique("zeros"), [TILES, WPT], F32))
        first = e(nc.sbuf_tensor(unique("first"), [TILES, WPT], F32))
        first_i = e(nc.sbuf_tensor(unique("first_i"), [TILES, WPT], I32))
        pairs_ps = e(nc.psum_tensor(unique("pairs_ps"), [P, P], F32))
        hist_ps = e(nc.psum_tensor(unique("hist_ps"), [TILES, P], F32))
        off_ps = e(nc.psum_tensor(unique("off_ps"), [TILES, 2], F32))
        x_in = e(nc.semaphore(unique("x_in")))
        dst_in = e(nc.semaphore(unique("dst_loaded")))
        table_done = e(nc.semaphore(unique("table_done")))
        pool_done = e(nc.semaphore(unique("pool_done")))
        dve_done = e(nc.semaphore(unique("dve_done")))
        pe_done = e(nc.semaphore(unique("pe_done")))
        starts_done = e(nc.semaphore(unique("starts_done")))
        var_ready = e(nc.semaphore(unique("var_ready")))
        std_ready = e(nc.semaphore(unique("std_ready")))
        block = e(nc.Block())
        marks = {}

        @block.gpsimd
        def _(pool):
            link = chained(pool, pool_done)
            link(nc.gpsimd.memset(ident[:], 0.0))
            link(nc.gpsimd.memset(before[:], 1.0))
            link(nc.gpsimd.affine_select(out=ident[:], in_=ident[:], compare_op=ALU.not_equal, fill=1.0, base=0,
                                         pattern=[[-1, 128]], channel_multiplier=1))
            link(nc.gpsimd.affine_select(out=before[:], in_=before[:], compare_op=ALU.is_gt, fill=0.0, base=0,
                                         pattern=[[1, TILES]], channel_multiplier=-1))
            link(nc.gpsimd.iota(iota_i[:], [[1, P]], base=0, channel_multiplier=0))
            link(nc.gpsimd.iota(iota_ti[:], [[P, TILES]], base=0, channel_multiplier=0))
            link(nc.gpsimd.memset(pad[:, 0:2 * ROW], -1))
            link(nc.gpsimd.memset(pad[:, 2 * ROW:], 0))
            link(nc.gpsimd.memset(zeros[:], 0.0))
            link(nc.gpsimd.memset(ones[:], 1.0))

        def vector(dve):
            count = [0]

            def link(ins):
                count[0] += 1
                ins.then_inc(dve_done, 1)
                dve.wait_ge(dve_done, count[0])

            dve.wait_ge(pool_done, 10)
            link(nc.vector.tensor_copy(iota[:], iota_i[:]))
            link(nc.vector.tensor_copy(iota_tile[:], iota_ti[:]))
            blocks = ident[0:P, 0:P].rearrange("p (j h) -> p j h", h=TILES)
            link(nc.vector.tensor_reduce(fold[:], blocks.rearrange("p j h -> p h j"), axis=AX.X, op=ALU.add))
            link(nc.vector.tensor_reduce(same[:], blocks, axis=AX.X, op=ALU.add))
            dve.wait_ge(dst_in, 16)
            link(nc.vector.tensor_copy(win_lo[:], dst_i[:]))
            floor_div(nc, link, win_lo[:], win_lo[:], WIN)
            floor_div(nc, link, win_hi[:], win_lo[:], WPT)
            link(nc.vector.scalar_tensor_tensor(win_lo[:], win_hi[:], -float(WPT), win_lo[:], ALU.mult, ALU.add))
            step = CHUNKS // 5
            for k in range(5):
                part = slice(k * step, (k + 1) * step)
                for one, win in ((one_hi, win_hi), (one_lo, win_lo)):
                    link(nc.vector.tensor_tensor(one[:, part, :],
                                                 win[:, part].unsqueeze(2).broadcast_to([P, step, TILES]),
                                                 iota[:, 0:TILES].unsqueeze(1).broadcast_to([P, step, TILES]),
                                                 ALU.is_equal))
                marks["one", k] = count[0]
            dve.wait_ge(x_in, 16)
            layer_norm_relu(nc, dve, link, X, H, stats, mv, rstd, var_ready, std_ready)
            dve.wait_ge(pe_done, 1)
            link(nc.vector.tensor_tensor(pairs[:].rearrange("p (j m) -> p j m", m=WPT),
                                         pairs_ps[:].rearrange("p (j m) -> p j m", m=WPT),
                                         same[:].unsqueeze(2).broadcast_to([P, GRP, WPT]), ALU.mult))
            marks["pairs"] = count[0]
            dve.wait_ge(pe_done, 2)
            link(nc.vector.tensor_reduce(hist[:], hist_ps[:].rearrange("h (j m) -> h m j", m=WPT), axis=AX.X,
                                         op=ALU.add))
            link(nc.vector.tensor_tensor_scan(upto[:], hist[:], zeros[:], 0.0, ALU.add, ALU.add))
            marks["upto"] = count[0]
            dve.wait_ge(pe_done, 3)
            link(nc.vector.tensor_tensor(first[:], upto[:], hist[:], ALU.subtract))
            link(nc.vector.tensor_scalar(first[:], first[:], off_ps[:, 0:1], None, ALU.add))
            floor_div(nc, link, first[:], first[:], ROW)
            link(nc.vector.tensor_copy(first_i[:], first[:]))
            marks["starts"] = count[0]

        block.vector(vector)

        @block.scalar
        def _(act):
            standard_deviation(nc, act, rstd, var_ready, std_ready)

        @block.tensor
        def _(pe):
            per = CHUNKS // GRP
            for k in range(per):
                if k % (per // 5) == 0:
                    pe.wait_ge(dve_done, marks["one", k // (per // 5)])
                ins = nc.tensor.matmul(pairs_ps[:], one_hi[:, GRP * k:GRP * (k + 1), :].rearrange("p j h -> p (j h)"),
                                       one_lo[:, GRP * k:GRP * (k + 1), :].rearrange("p j h -> p (j h)"),
                                       start=(k == 0), stop=(k == per - 1))
            ins.then_inc(pe_done, 1)
            pe.wait_ge(dve_done, marks["pairs"])
            nc.tensor.matmul(hist_ps[:], fold[:], pairs[:], start=True, stop=True).then_inc(pe_done, 1)
            pe.wait_ge(dve_done, marks["upto"])
            nc.tensor.matmul(off_ps[:, 0:1], before[:], upto[:, WPT - 1:WPT], start=True, stop=True).then_inc(pe_done, 1)

        @block.sync
        def _(sp):
            sp.dma_start(dst_i[:], T["dst"].rearrange("(p c) -> p c", p=P)).then_inc(dst_in, 16)
            sp.dma_start(X[:], T["x"].rearrange("(t p) f -> p t f", p=P)).then_inc(x_in, 16)
            for k, name in enumerate(("src", "dst", "edge_weight")):
                column = table[0:ROWS, k * ROW:(k + 1) * ROW]
                if name == "edge_weight":
                    column = column.bitcast(F32)
                sp.dma_start(column, T[name].rearrange("(r e) -> r e", e=ROW)).then_inc(table_done, 16)
            sp.wait_ge(pool_done, 10)
            sp.dma_start(table[ROWS:ROWS + GROWS, :], pad[:]).then_inc(table_done, 16)
            sp.wait_ge(table_done, 64)
            sp.wait_ge(dve_done, marks["starts"])
            sp.dma_start(starts.rearrange("(h m) -> h m", m=WPT), first_i[:]).then_inc(starts_done, 16)
            sp.wait_ge(starts_done, 16)


def edge_slots(nc, table, starts, ident, src_hi, src_lo, dst_in, weight):
    KINDS = 3
    with ExitStack() as c:
        e = c.enter_context
        row0 = e(nc.sbuf_tensor(unique("row0"), [P, BLOCKS], I32))
        row_f = e(nc.sbuf_tensor(unique("row_f"), [P, BLOCKS], F32))
        off_i = e(nc.sbuf_tensor(unique("off_i"), [P, GROWS], I32))
        off_f = e(nc.sbuf_tensor(unique("off_f"), [P, GROWS], F32))
        index = e(nc.sbuf_tensor(unique("index"), [P, GROWS, BLOCKS], I32))
        rows = e(nc.sbuf_tensor(unique("rows"), [P, BLOCKS, GROWS, KINDS * ROW], I32))
        flat = e(nc.sbuf_tensor(unique("flat"), [P, BLOCKS, KINDS, GROWS * ROW], F32))
        win_i = e(nc.sbuf_tensor(unique("win_i"), [P, 2 * WINDOWS], I32))
        src_f = e(nc.sbuf_tensor(unique("src_f"), [P, 2 * WINDOWS], F32))
        turned = e(nc.psum_tensor(unique("turned"), [P, 2, 512], F32))
        loaded = e(nc.semaphore(unique("loaded")))
        pool_ready = e(nc.semaphore(unique("pool_ready")))
        gathered = [e(nc.semaphore(unique(f"gathered{b}"))) for b in range(BLOCKS)]
        index_ready = e(nc.semaphore(unique("index_ready")))
        flat_ready = e(nc.semaphore(unique("flat_ready")))
        turn_done = e(nc.semaphore(unique("turn_done")))
        copied = e(nc.semaphore(unique("copied")))
        slots_done = e(nc.semaphore(unique("slots_done")))
        block = e(nc.Block())

        @block.sync
        def _(sp):
            with nc.allow_non_contiguous_dma(reason="one start a partition"):
                sp.dma_start(row0[:], starts.rearrange("(b p) -> p b", p=P)).then_inc(loaded, 16)

        @block.gpsimd
        def _(pool):
            nc.gpsimd.iota(off_i[:], [[1, GROWS]], base=0, channel_multiplier=0).then_inc(pool_ready, 1)
            nc.gpsimd.iota(win_i[:].rearrange("p (w h) -> p w h", h=2), [[WIN, WINDOWS], [0, 2]], base=0,
                           channel_multiplier=0).then_inc(pool_ready, 1)
            pool.wait_ge(index_ready, 1)
            for b in range(BLOCKS):
                for j in range(GROWS):
                    nc.gpsimd.indirect_dma_start(rows[:, b, j, :], None, table,
                                                 bass.IndirectOffsetOnAxis(ap=index[:, j, b:b + 1], axis=0)
                                                 ).then_inc(gathered[b], 16)

        @block.vector
        def _(dve):
            link = chained(dve, slots_done)
            dve.wait_ge(pool_ready, 2)
            link(nc.vector.tensor_copy(off_f[:], off_i[:]))
            dve.wait_ge(loaded, 16)
            link(nc.vector.tensor_copy(row_f[:], row0[:]))
            nc.vector.tensor_tensor(index[:], row_f[:].unsqueeze(1).broadcast_to([P, GROWS, BLOCKS]),
                                    off_f[:].unsqueeze(2).broadcast_to([P, GROWS, BLOCKS]),
                                    ALU.add).then_inc(index_ready, 1)
            for b in range(BLOCKS):
                dve.wait_ge(gathered[b], 16 * GROWS)
                for k in range(KINDS):
                    part = rows[:, b, :, k * ROW:(k + 1) * ROW]
                    if k == 2:
                        part = part.bitcast(F32)
                    nc.vector.tensor_copy(flat[:, b, k, :].rearrange("p (j e) -> p j e", e=ROW),
                                          part).then_inc(flat_ready, 1)
            dve.wait_ge(copied, 3 * 2 * BLOCKS)
            floor_div(nc, link, src_hi[:], src_f[:], P)
            link(nc.vector.tensor_scalar(src_hi[:], src_hi[:], float(P), None, ALU.mult))
            link(nc.vector.tensor_tensor(src_lo[:], src_f[:], src_hi[:], ALU.subtract))
            link(nc.vector.tensor_copy(src_f[:], win_i[:]))
            link(nc.vector.tensor_tensor(dst_in[:], dst_in[:], src_f[:], ALU.subtract))

        @block.tensor
        def _(pe):
            for b in range(BLOCKS):
                pe.wait_ge(flat_ready, KINDS * (b + 1))
                for h in range(2):
                    n = 2 * b + h
                    if n >= 2:
                        pe.wait_ge(copied, 3 * (n - 1))
                    for k in range(KINDS):
                        ins = nc.tensor.transpose(turned[:, h, k * P:(k + 1) * P], flat[:, b, k, h * P:(h + 1) * P],
                                                  ident[0:P, 0:P])
                    ins.then_inc(turn_done, 1)

        @block.scalar
        def _(act):
            for b in range(BLOCKS):
                for h in range(2):
                    act.wait_ge(turn_done, 2 * b + h + 1)
                    for k, out in enumerate((src_f, dst_in, weight)):
                        out = out[:].rearrange("p (w h) -> p h w", h=2)[:, h, b * P:(b + 1) * P]
                        nc.scalar.copy(out, turned[:, h, k * P:(k + 1) * P]).then_inc(copied, 1)


def adjacency(nc, counts, countsT, weightsT, ident, src_hi, src_lo, dst_in, weight, iota, iota_tile,
              out_degree, in_parts):
    PER = 3 + 2 * NGRP
    G = 2 * GRP
    WID = 2 * WIN
    ROUNDS = (TILES + 3) // 4
    after = [[0, 1], [2, 3], [4], [5], [6]]
    assert sum(after, []) == list(range(ROUNDS)) and len(after) == NGRP
    with ExitStack() as c:
        e = c.enter_context
        tile_hot = e(nc.sbuf_tensor(unique("tile_hot"), [P, 2, 2 * WPT, TILES], F32))
        dst_hot = e(nc.sbuf_tensor(unique("dst_hot"), [P, 2, 2 * WPT, WID], F32))
        lo_hot = e(nc.sbuf_tensor(unique("lo_hot"), [P, 2, G, P], F32))
        lo_hot_short = e(nc.sbuf_tensor(unique("lo_hot_short"), [P, 2, G, P], BF16))
        pair_hot = e(nc.sbuf_tensor(unique("pair_hot"), [P, 2, G, P], BF16))
        pair_weight = e(nc.sbuf_tensor(unique("pair_weight"), [P, 2, G, P], F32))
        cT = e(nc.sbuf_tensor(unique("cT"), [P, 2, N], F32))
        wT = e(nc.sbuf_tensor(unique("wT"), [P, 2, N], F32))
        cc = e(nc.sbuf_tensor(unique("cc"), [P, 2, N], F32))
        degree_parts = e(nc.sbuf_tensor(unique("degree_parts"), [P, TILES, TILES], F32))
        built = [e(nc.psum_tensor(unique(f"built{i}"), [P, 3 * 512], F32)) for i in range(2)]
        flipped = e(nc.psum_tensor(unique("flipped"), [P, 2, 512], F32))
        made = e(nc.semaphore(unique("made")))
        weighed = e(nc.semaphore(unique("pairs_weighed")))
        pool_go = e(nc.semaphore(unique("pool_go")))
        grouped = e(nc.semaphore(unique("grouped")))
        copied = e(nc.semaphore(unique("cT_copied")))
        turned = e(nc.semaphore(unique("tile_turned")))
        straight = e(nc.semaphore(unique("straight")))
        shortened = e(nc.semaphore(unique("shortened")))
        summed = e(nc.semaphore(unique("summed")))
        stored = [e(nc.semaphore(unique(f"stored{u}"))) for u in range(2)]
        turned_stored = [e(nc.semaphore(unique(f"turned_stored{u}"))) for u in range(2)]
        free = e(nc.semaphore(unique("tiles_free")))
        cc_free = e(nc.semaphore(unique("cc_free")))
        block = e(nc.Block())

        def one_behind(eng, body):
            body(0, 0, False)
            with eng.Fori(0, (TILES - 1) // 2) as i:
                body(i * 2 + 1, 1, True)
                body(i * 2 + 2, 0, True)

        @block.vector
        def _(dve):
            dve.sem_inc(summed, 2)

            def reduce_degrees(t, u):
                dve.wait_ge(copied, t * (2 * NGRP) + (4 + 2 * NGRP))
                nc.vector.tensor_reduce(row_of(degree_parts, t), cT[:, u, :].rearrange("p (a d) -> p a d", d=P),
                                        axis=AX.X, op=ALU.add).then_inc(summed, 1)

            def tile(t, u, before):
                halves = bass.ds(t * (2 * WPT), 2 * WPT)
                nc.vector.tensor_tensor(tile_hot[:, u], src_hi[:, halves].unsqueeze(2).broadcast_to([P, 2 * WPT, TILES]),
                                        iota_tile[:].unsqueeze(1).broadcast_to([P, 2 * WPT, TILES]),
                                        ALU.is_equal).then_inc(made, 1)
                nc.vector.tensor_tensor(dst_hot[:, u, :, 0:WIN],
                                        dst_in[:, halves].unsqueeze(2).broadcast_to([P, 2 * WPT, WIN]),
                                        iota[:, 0:WIN].unsqueeze(1).broadcast_to([P, 2 * WPT, WIN]),
                                        ALU.is_equal).then_inc(made, 1)
                dve.wait_ge(made, t * PER + 2)
                nc.vector.tensor_tensor(dst_hot[:, u, :, WIN:WID], dst_hot[:, u, :, 0:WIN],
                                        weight[:, halves].unsqueeze(2).broadcast_to([P, 2 * WPT, WIN]),
                                        ALU.mult).then_inc(made, 1)
                for q in range(NGRP):
                    b = (NGRP * u + q) % 2
                    dve.wait_ge(grouped, t * NGRP + (q + 1))
                    nc.vector.tensor_tensor(lo_hot[:, b],
                                            src_lo[:, bass.ds(t * (2 * WPT) + q * G, G)].unsqueeze(2).broadcast_to([P, G, P]),
                                            iota[:].unsqueeze(1).broadcast_to([P, G, P]),
                                            ALU.is_equal).then_inc(made, 1)
                    part = slice(q * G, (q + 1) * G)
                    nc.vector.tensor_tensor(pair_hot[:, b].rearrange("p g (a k) -> p g a k", k=WIN),
                                            tile_hot[:, u, part].unsqueeze(3).broadcast_to([P, G, TILES, WIN]),
                                            dst_hot[:, u, part, 0:WIN].unsqueeze(2).broadcast_to([P, G, TILES, WIN]),
                                            ALU.mult).then_inc(made, 1)
                    if before and q == 2:
                        reduce_degrees(t - 1, 1 - u)

            one_behind(dve, tile)
            reduce_degrees(TILES - 1, 0)
            dve.wait_ge(summed, 2 + TILES)
            nc.vector.tensor_reduce(out_degree[:], degree_parts[:].rearrange("p t a -> p a t"), axis=AX.X, op=ALU.add)

        @block.gpsimd
        def _(pool):
            def tile(t, u, before):
                for q in range(NGRP):
                    b = (NGRP * u + q) % 2
                    pool.wait_ge(made, t * PER + 3)
                    pool.wait_ge(grouped, t * NGRP + (q + 1))
                    pool.sem_inc(pool_go, 1)
                    part = slice(q * G, (q + 1) * G)
                    nc.gpsimd.tensor_tensor(pair_weight[:, b].rearrange("p g (a k) -> p g a k", k=WIN),
                                            tile_hot[:, u, part].unsqueeze(3).broadcast_to([P, G, TILES, WIN]),
                                            dst_hot[:, u, part, WIN:WID].unsqueeze(2).broadcast_to([P, G, TILES, WIN]),
                                            ALU.mult).then_inc(weighed, 1)

            one_behind(pool, tile)

        @block.tensor
        def _(pe):
            pe.sem_inc(grouped, 2)

            def turn_round(t, u, r):
                b = (ROUNDS * u + r) % 2
                if r == 0:
                    pe.wait_ge(copied, t * (2 * NGRP) + (4 + 2 * NGRP))
                pe.wait_ge(straight, t * ROUNDS + (r + 1))
                for a in range(4 * r, min(4 * r + 4, TILES)):
                    ins = nc.tensor.transpose(flipped[:, b, (a % 4) * P:(a % 4 + 1) * P],
                                              cT[:, u, a * P:(a + 1) * P], ident[0:P, 0:P])
                ins.then_inc(turned, 1)

            def tile(t, u, before):
                for q in range(NGRP):
                    b = (NGRP * u + q) % 2
                    pe.wait_ge(made, t * PER + (3 + 2 * (q + 1)))
                    pe.wait_ge(weighed, t * NGRP + (q + 1))
                    pe.wait_ge(copied, t * (2 * NGRP) + 2 * (q + 1))
                    for w in range(GRP):
                        for h in range(2):
                            nc.tensor.matmul(built[b][:, 256 * w + P:256 * w + 2 * P], lo_hot[:, b, 2 * w + h],
                                             pair_weight[:, b, 2 * w + h], start=(h == 0), stop=(h == 1))
                    pe.wait_ge(shortened, t * NGRP + (q + 1))
                    for w in range(GRP):
                        for h in range(2):
                            ins = nc.tensor.matmul(built[b][:, 256 * w:256 * w + P], lo_hot_short[:, b, 2 * w + h],
                                                   pair_hot[:, b, 2 * w + h], start=(h == 0), stop=(h == 1))
                    ins.then_inc(grouped, 1)
                    if before:
                        for r in after[q]:
                            turn_round(t - 1, 1 - u, r)

            one_behind(pe, tile)
            for r in range(ROUNDS):
                turn_round(TILES - 1, 0, r)

        @block.scalar
        def _(act):
            act.sem_inc(copied, 4)
            act.sem_inc(straight, 2)

            def copy_round(t, u, r):
                b = (ROUNDS * u + r) % 2
                n = min(4, TILES - 4 * r) * P
                if r == 0:
                    act.wait_ge(cc_free, t + 1)
                act.wait_ge(turned, t * ROUNDS + (r + 1))
                nc.scalar.activation(cc[:, u, 4 * P * r:4 * P * r + n], flipped[:, b, 0:n], ACT.Copy,
                                     accum_out=in_parts[:, bass.ds(t, 1), r:r + 1].rearrange("p o f -> p (o f)")
                                     ).then_inc(straight, 1)

            def shorten(t, u, q):
                b = (NGRP * u + q) % 2
                act.wait_ge(made, t * PER + (4 + 2 * q))
                act.wait_ge(grouped, t * NGRP + (q + 1))
                nc.scalar.copy(lo_hot_short[:, b], lo_hot[:, b]).then_inc(shortened, 1)

            def tile(t, u, before):
                act.wait_ge(free, t + 1)
                act.wait_ge(summed, t + 1)
                for q in range(NGRP):
                    b = (NGRP * u + q) % 2
                    shorten(t, u, q)
                    act.wait_ge(grouped, t * NGRP + (q + 3))
                    seen = built[b][:, 0:256 * GRP].rearrange("p (w k) -> p w k", k=256)[:, :, 0:TILES * WID]
                    seen = seen.rearrange("p w (c a k) -> p w c a k", c=2, k=WIN)
                    for c, out in enumerate((cT, wT)):
                        o = out[:, u, :].rearrange("p (a w k) -> p w a k", w=WPT, k=WIN)[:, q * GRP:(q + 1) * GRP]
                        nc.scalar.copy(o, seen[:, :, c]).then_inc(copied, 1)
                    if before:
                        for r in after[q]:
                            copy_round(t - 1, 1 - u, r)

            one_behind(act, tile)
            for r in range(ROUNDS):
                copy_round(TILES - 1, 0, r)

        @block.sync
        def _(sp):
            sp.sem_inc(free, 2)
            sp.sem_inc(cc_free, 2)
            row = lambda d, t: d[bass.ds(t, 1)].rearrange("o p n -> (o p) n")

            def store_turned(t, u):
                sp.wait_ge(straight, t * ROUNDS + (2 + ROUNDS))
                sp.dma_start(row(counts, t), cc[:, u, :]).then_inc(turned_stored[u], 16)

            def landed(t, u):
                sp.wait_ge(stored[u], (t - u) * 16 + 32)
                sp.sem_inc(free, 1)

            def turned_landed(t, u):
                sp.wait_ge(turned_stored[u], (t - u) * 8 + 16)
                sp.sem_inc(cc_free, 1)

            def tile(t, u, before):
                if before:
                    landed(t - 1, 1 - u)
                    store_turned(t - 1, 1 - u)
                sp.wait_ge(copied, t * (2 * NGRP) + (4 + 2 * NGRP))
                sp.dma_start(row(countsT, t), cT[:, u, :]).then_inc(stored[u], 16)
                sp.dma_start(row(weightsT, t), wT[:, u, :]).then_inc(stored[u], 16)
                if before:
                    turned_landed(t - 1, 1 - u)

            one_behind(sp, tile)
            landed(TILES - 1, 0)
            store_turned(TILES - 1, 0)
            turned_landed(TILES - 1, 0)


def in_turns(eng, body, k, n=TILES):
    assert n % k == 0
    with eng.Fori(0, n // k) as i:
        for u in range(k):
            body(i * k + u, u)


def quads():
    return [(r, 4 * r, min(4, TILES - 4 * r)) for r in range((TILES + 3) // 4)]


def turn_tiles(nc, pe, X, ident, flipped, turned, moved, before):
    for r, a0, n in quads():
        if r >= 2:
            pe.wait_ge(moved, before + r - 1)
        for a in range(a0, a0 + n):
            ins = nc.tensor.transpose(flipped[:, r % 2, (a - a0) * P:(a - a0 + 1) * P], X[:, a, :], ident[0:P, 0:P])
        ins.then_inc(turned, 1)


def move_tiles(nc, act, XT, flipped, turned, moved, before):
    for r, a0, n in quads():
        act.wait_ge(turned, before + r + 1)
        nc.scalar.copy(XT[:, a0 * P:(a0 + n) * P], flipped[:, r % 2, 0:n * P]).then_inc(moved, 1)


def load_weights(nc, T, W, ident):
    turned_names = [("W0", T["L0_gnn_W"]), ("Ws0", T["L2_gnn_W_self"][0]), ("Ws1", T["L2_gnn_W_self"][1]),
                    ("Wn0", T["L2_gnn_W_neigh"][0]), ("Wn1", T["L2_gnn_W_neigh"][1]), ("Wa", T["L2_gnn_W_agg"])]
    with ExitStack() as c:
        e = c.enter_context
        raw = e(nc.sbuf_tensor(unique("raw"), [D, len(turned_names), D], F32))
        parts = e(nc.sbuf_tensor(unique("parts"), [1, 6, D], F32))
        flipped = e(nc.psum_tensor(unique("flipped_w"), [D, 2, 512], F32))
        raw_in = e(nc.semaphore(unique("raw_in")))
        rest_in = e(nc.semaphore(unique("rest_in")))
        turned = e(nc.semaphore(unique("w_turned")))
        moved = e(nc.semaphore(unique("w_moved")))
        block = e(nc.Block())

        @block.sync
        def _(sp):
            for k, (_, w) in enumerate(turned_names):
                sp.dma_start(raw[:, k, :], w).then_inc(raw_in, 16)
            for k, name in enumerate(("Wq", "Wk", "Wv")):
                sp.dma_start(W[name][:].rearrange("i (h o) -> i h o", h=HEADS),
                             T["L1_gnn_" + name].rearrange("h i o -> i h o")).then_inc(rest_in, 16)
            sp.dma_start(W["W3"][:], T["L3_gnn_W"]).then_inc(rest_in, 16)
            rows = [T["L2_gnn_b_self"], T["L2_gnn_b_neigh"], T["L2_gnn_layer_bias"]]
            for k, b in enumerate(rows):
                sp.dma_start(parts[0:1, 2 * k:2 * k + 2, :], b.rearrange("(o l) d -> o l d", o=1)).then_inc(rest_in, 16)
            for k, name in enumerate(("L0_gnn_b", "L2_gnn_b_agg", "L3_gnn_b")):
                sp.dma_start(W["bias"][0:1, k, :], T[name].rearrange("(o d) -> o d", o=1)).then_inc(rest_in, 16)
            sp.wait_ge(rest_in, 16 * 10)

        @block.tensor
        def _(pe):
            pe.wait_ge(raw_in, 16 * len(turned_names))
            for k in range(len(turned_names)):
                ins = nc.tensor.transpose(flipped[:, k // 4, (k % 4) * D:(k % 4 + 1) * D], raw[:, k, :], ident[:])
            ins.then_inc(turned, 1)

        @block.vector
        def _(dve):
            dve.wait_ge(turned, 1)
            for k, (name, _) in enumerate(turned_names):
                nc.vector.tensor_copy(W[name][:], flipped[:, k // 4, (k % 4) * D:(k % 4 + 1) * D])
            dve.wait_ge(rest_in, 16 * 10)
            nc.vector.tensor_tensor(parts[0:1, 0:2, :], parts[0:1, 0:2, :], parts[0:1, 2:4, :], ALU.add).then_inc(moved, 1)
            dve.wait_ge(moved, 1)
            nc.vector.tensor_tensor(W["bias"][0:1, 3:5, :], parts[0:1, 0:2, :], parts[0:1, 4:6, :], ALU.add)


def gcn_layer(nc, counts, X, H, W, ones, out_degree):
    BUFS = 5
    with ExitStack() as c:
        e = c.enter_context
        block_in = e(nc.sbuf_tensor(unique("counts_in"), [P, BUFS, N], F32))
        scaled = e(nc.sbuf_tensor(unique("scaled"), [P, BUFS, D], F32))
        inv = e(nc.sbuf_tensor(unique("inv"), [P, TILES], F32))
        some = e(nc.sbuf_tensor(unique("some"), [P, TILES], F32))
        aggT = e(nc.sbuf_tensor(unique("aggT"), [D, N], F32))
        agg = e(nc.psum_tensor(unique("agg"), [D, 7, 512], F32))
        last = e(nc.psum_tensor(unique("last_bank"), [P, 512], F32))
        loaded = [e(nc.semaphore(unique(f"loaded{u}"))) for u in range(BUFS)]
        used = e(nc.semaphore(unique("used")))
        scaled_done = e(nc.semaphore(unique("scaled_done")))
        bias_done = e(nc.semaphore(unique("bias_done")))
        agg_moved = e(nc.semaphore(unique("agg_moved")))
        inv_done = e(nc.semaphore(unique("inv_done")))
        root_ready = e(nc.semaphore(unique("root_ready")))
        root_done = e(nc.semaphore(unique("root_done")))
        lin_done = e(nc.semaphore(unique("lin_done")))
        lin_added = e(nc.semaphore(unique("lin_added")))
        block = e(nc.Block())

        @block.sync
        def _(sp):
            def tile(t, u):
                sp.wait_ge(used, t + 1)
                sp.dma_start(block_in[:, u, :], counts[bass.ds(t, 1)].rearrange("o p n -> (o p) n")).then_inc(loaded[u], 16)

            in_turns(sp, tile, BUFS)

        @block.scalar
        def _(act):
            act.wait_ge(root_ready, 1)
            nc.scalar.activation(inv[:], inv[:], ACT.Sqrt).then_inc(root_done, 1)
            act.wait_ge(used, BUFS + TILES)
            for k in range(7):
                n = min(512, N - 512 * k)
                if k % 2:
                    nc.scalar.copy(aggT[:, 512 * k:512 * k + n], agg[:, k, 0:n]).then_inc(agg_moved, 1)

        @block.vector
        def _(dve):
            link = chained(dve, inv_done)
            link(nc.vector.tensor_scalar(some[:], out_degree[:], 0.0, None, ALU.is_gt))
            nc.vector.tensor_scalar(inv[:], out_degree[:], 1.0, None, ALU.max).then_inc(root_ready, 1)
            dve.wait_ge(root_done, 1)
            link(nc.vector.reciprocal(inv[:], inv[:]))
            link(nc.vector.tensor_tensor(inv[:], inv[:], some[:], ALU.mult))

            def tile(t, u):
                dve.wait_ge(used, t + 1)
                nc.vector.tensor_scalar(scaled[:, u, :], row_of(H, t), inv[:, bass.ds(t, 1)], None,
                                        ALU.mult).then_inc(scaled_done, 1)

            in_turns(dve, tile, BUFS)
            dve.wait_ge(bias_done, 1)
            link(nc.vector.tensor_tensor(X[:], X[:], last[:, 0:D].unsqueeze(1).broadcast_to([P, TILES, D]), ALU.add))
            dve.wait_ge(used, BUFS + TILES)
            for k in range(0, 7, 2):
                n = min(512, N - 512 * k)
                nc.vector.tensor_copy(aggT[:, 512 * k:512 * k + n], agg[:, k, 0:n]).then_inc(agg_moved, 1)
            for r, a0, n in quads():
                dve.wait_ge(lin_done, r + 1)
                for a in range(a0, a0 + n):
                    ins = nc.vector.scalar_tensor_tensor(X[:, a, :], agg[0:P, r % 2, (a - a0) * D:(a - a0 + 1) * D],
                                                         inv[:, a:a + 1], X[:, a, :], ALU.mult, ALU.add)
                ins.then_inc(lin_added, 1)

        @block.tensor
        def _(pe):
            pe.sem_inc(used, BUFS)
            nc.tensor.matmul(last[:, 0:D], ones[0:1, 0:P], W["bias"][0:1, 0, :], start=True, stop=True).then_inc(bias_done, 1)

            def turn(i, first=False, last_turn=False):
                for u in range(BUFS):
                    pe.wait_ge(scaled_done, i * BUFS + (u + 1))
                    pe.wait_ge(loaded[u], i * 16 + 16)
                    for k in range(7):
                        n = min(512, N - 512 * k)
                        ins = nc.tensor.matmul(agg[:, k, 0:n], scaled[:, u, :], block_in[:, u, 512 * k:512 * k + n],
                                               start=(first and u == 0), stop=(last_turn and u == BUFS - 1))
                    ins.then_inc(used, 1)

            turn(0, first=True)
            with pe.Fori(1, TILES // BUFS - 1) as i:
                turn(i)
            turn(TILES // BUFS - 1, last_turn=True)
            pe.wait_ge(agg_moved, 7)
            for r, a0, n in quads():
                if r >= 2:
                    pe.wait_ge(lin_added, r - 1)
                for a in range(a0, a0 + n):
                    ins = nc.tensor.matmul(agg[0:P, r % 2, (a - a0) * D:(a - a0 + 1) * D], aggT[:, a * P:(a + 1) * P],
                                           W["W0"][:], start=True, stop=True)
                ins.then_inc(lin_done, 1)


def normalize(nc, X, H, HT, stats, mv, rstd, ident):
    with ExitStack() as c:
        e = c.enter_context
        flipped = e(nc.psum_tensor(unique("flipped_h"), [D, 2, 512], F32))
        normed = e(nc.semaphore(unique("normed")))
        var_ready = e(nc.semaphore(unique("var_ready")))
        std_ready = e(nc.semaphore(unique("std_ready")))
        h_ready = e(nc.semaphore(unique("h_ready")))
        turned = e(nc.semaphore(unique("h_turned")))
        moved = e(nc.semaphore(unique("h_moved")))
        block = e(nc.Block())

        @block.vector
        def _(dve):
            layer_norm_relu(nc, dve, chained(dve, normed), X, H, stats, mv, rstd, var_ready, std_ready)
            dve.sem_inc(h_ready, 1)

        @block.scalar
        def _(act):
            standard_deviation(nc, act, rstd, var_ready, std_ready)
            move_tiles(nc, act, HT, flipped, turned, moved, 0)

        @block.tensor
        def _(pe):
            pe.wait_ge(h_ready, 1)
            turn_tiles(nc, pe, H, ident, flipped, turned, moved, 0)


def turn(nc, Y, YT, ident):
    with ExitStack() as c:
        e = c.enter_context
        flipped = e(nc.psum_tensor(unique("flipped_y"), [D, 2, 512], F32))
        turned = e(nc.semaphore(unique("y_turned")))
        moved = e(nc.semaphore(unique("y_moved")))
        block = e(nc.Block())

        @block.scalar
        def _(act):
            move_tiles(nc, act, YT, flipped, turned, moved, 0)

        @block.tensor
        def _(pe):
            turn_tiles(nc, pe, Y, ident, flipped, turned, moved, 0)


def project(nc, HT, W, QA, QB, KA, KB, V):
    CH = 500
    pieces = [(k, CH * k, min(CH, N - CH * k)) for k in range((N + CH - 1) // CH)]
    n = len(pieces)
    with ExitStack() as c:
        e = c.enter_context
        part = [[e(nc.sbuf_tensor(unique("part"), [D, N], BF16)) for _ in range(3)] for _ in range(2)]
        rest = e(nc.sbuf_tensor(unique("rest"), [D, 2, CH], F32))
        out = e(nc.psum_tensor(unique("projection"), [D, 2, 512], F32))
        multiplied = e(nc.semaphore(unique("projected")))
        first = e(nc.semaphore(unique("first_parts")))
        split = e(nc.semaphore(unique("split")))
        v_ready = e(nc.semaphore(unique("v_multiplied")))
        v_moved = e(nc.semaphore(unique("v_moved")))
        spread = e(nc.semaphore(unique("spread")))
        block = e(nc.Block())

        @block.tensor
        def _(pe):
            for m, name in enumerate(("Wq", "Wk")):
                for k, at, w in pieces:
                    p = m * n + k
                    if p >= 2:
                        pe.wait_ge(split, 3 * (p - 1))
                    nc.tensor.matmul(out[:, p % 2, 0:w], W[name][:], HT[:, at:at + w], start=True, stop=True).then_inc(multiplied, 1)
            pe.wait_ge(split, 3 * 2 * n)
            for r, a0, m in quads():
                if r >= 2:
                    pe.wait_ge(v_moved, r - 1)
                for a in range(a0, a0 + m):
                    ins = nc.tensor.matmul(out[0:P, r % 2, (a - a0) * D:(a - a0 + 1) * D], HT[:, a * P:(a + 1) * P],
                                           W["Wv"][:], start=True, stop=True)
                ins.then_inc(v_ready, 1)

        @block.scalar
        def _(act):
            for m in range(2):
                for k, at, w in pieces:
                    p = m * n + k
                    act.wait_ge(multiplied, p + 1)
                    nc.scalar.copy(part[m][0][:, at:at + w], out[:, p % 2, 0:w]).then_inc(first, 1)
            for r, a0, m in quads():
                act.wait_ge(v_ready, r + 1)
                nc.scalar.copy(V[:, a0:a0 + m, :, 0:HID],
                               out[0:P, r % 2, 0:m * D].rearrange("p (a h o) -> p a h o", h=HEADS, o=HID)).then_inc(v_moved, 1)

        @block.vector
        def _(dve):
            nc.vector.memset(V[:, :, :, HID:HID + 1], 1.0)
            for m in range(2):
                for k, at, w in pieces:
                    p = m * n + k
                    dve.wait_ge(first, p + 1)
                    here = slice(at, at + w)
                    r = rest[:, p % 2, 0:w]
                    nc.vector.tensor_tensor(r, out[:, p % 2, 0:w], part[m][0][:, here], ALU.subtract).then_inc(split, 1)
                    dve.wait_ge(split, 3 * p + 1)
                    nc.vector.tensor_copy(part[m][1][:, here], r).then_inc(split, 1)
                    dve.wait_ge(split, 3 * p + 2)
                    nc.vector.tensor_tensor(part[m][2][:, here], r, part[m][1][:, here], ALU.subtract).then_inc(split, 1)

        @block.sync
        def _(sp):
            count = 0
            for m, (A, B, rows_a, rows_b) in enumerate(((QA, QB, (0, 1, 0, 1), (2, 0)), (KA, KB, (0, 0, 1, 1), (0, 2)))):
                sp.wait_ge(split, 3 * n * (m + 1))
                for h in range(HEADS):
                    head = slice(h * HID, (h + 1) * HID)
                    for k, which in enumerate(rows_a):
                        sp.dma_start(A[k * HID:(k + 1) * HID, h, :], part[m][which][head, :]).then_inc(spread, 16)
                    for k, which in enumerate(rows_b):
                        at = 64 * (h % 2) + k * HID
                        sp.dma_start(B[at:at + HID, h // 2, :], part[m][which][head, :]).then_inc(spread, 16)
                    count += 6
            sp.wait_ge(spread, 16 * count)


def attention(nc, counts, countsT, X, H, QA, QB, KA, KB, V, ident):
    PW = 4 * P
    PIECES = len(quads())
    TP = HEADS * PIECES
    LAG = PIECES + 2
    SPANS = ((0, 2 * PW), (2 * PW, 4 * PW), (4 * PW, N))
    NS = len(SPANS)
    width = [n * P for _, _, n in quads()]
    with ExitStack() as c:
        e = c.enter_context
        count_in = e(nc.sbuf_tensor(unique("count_in"), [P, N], F32))
        countT_in = e(nc.sbuf_tensor(unique("countT_in"), [P, 2, N], F32))
        absent = e(nc.sbuf_tensor(unique("absent"), [P, 2, N], BF16))
        low = e(nc.sbuf_tensor(unique("low"), [P, P], BF16))
        key_a = e(nc.sbuf_tensor(unique("key_a"), [D, 2, HEADS, P], BF16))
        key_b = e(nc.sbuf_tensor(unique("key_b"), [D, 2, HEADS, P], BF16))
        score1 = e(nc.sbuf_tensor(unique("score1"), [P, N], F32))
        score = [H[:].rearrange("p t d -> p (t d)")[:, 0:N], score1[:]]
        rising = e(nc.sbuf_tensor(unique("rising"), [P, 2, PW], F32))
        weighed = e(nc.sbuf_tensor(unique("weighed"), [P, 4, PW], F32))
        peaks = e(nc.sbuf_tensor(unique("peaks"), [P, 2, PIECES], F32))
        shift = e(nc.sbuf_tensor(unique("shift"), [P, 2, 2], F32))
        norm = e(nc.sbuf_tensor(unique("norm"), [P, 2 * HEADS], F32))
        heads_out = e(nc.sbuf_tensor(unique("heads_out"), [P, HEADS, HID], F32))
        raw = e(nc.psum_tensor(unique("raw"), [P, 4, 512], F32))
        probsT = e(nc.psum_tensor(unique("probsT"), [P, 2, 512], F32))
        mixed = e(nc.psum_tensor(unique("mixed_values"), [P, 2, 512], F32))
        c_loaded = e(nc.semaphore(unique("c_loaded")))
        ct_loaded = [e(nc.semaphore(unique(f"ct_loaded{u}"))) for u in range(2)]
        low_ready = e(nc.semaphore(unique("low_ready")))
        absent_done = e(nc.semaphore(unique("absent_done")))
        vector_go = e(nc.semaphore(unique("vector_go")))
        pool_go = e(nc.semaphore(unique("pool_go")))
        keys_done = e(nc.semaphore(unique("keys_done")))
        scored = e(nc.semaphore(unique("scored")))
        scaled = e(nc.semaphore(unique("scaled")))
        leaky = e(nc.semaphore(unique("leaky")))
        shifted = e(nc.semaphore(unique("shifted")))
        exped = e(nc.semaphore(unique("exped")))
        turned = e(nc.semaphore(unique("probs_turned")))
        counted = e(nc.semaphore(unique("counted")))
        summed = e(nc.semaphore(unique("values_summed")))
        norm_steps = e(nc.semaphore(unique("norm_steps")))
        tile_out = e(nc.semaphore(unique("tile_out")))
        block = e(nc.Block())

        def slots(score_piece, value_piece):
            def run(t, u, before=True):
                for p in range(TP):
                    score_piece(t, u, p // PIECES, p % PIECES)
                    q = p - LAG
                    if q >= 0:
                        value_piece(t, u, q // PIECES, q % PIECES)
                    elif before:
                        value_piece(t - 1, 1 - u, (q + TP) // PIECES, (q + TP) % PIECES)
            return run

        def all_tiles(eng, score_piece, value_piece):
            run = slots(score_piece, value_piece)
            run(0, 0, before=False)
            with eng.Fori(0, (TILES - 1) // 2) as i:
                run(i * 2 + 1, 1)
                run(i * 2 + 2, 0)
            for q in range(TP - LAG, TP):
                value_piece(TILES - 1, 0, q // PIECES, q % PIECES)

        @block.sync
        def _(sp):
            def tile(t, u):
                row = lambda d: d[bass.ds(t, 1)].rearrange("o p n -> (o p) n")
                sp.wait_ge(absent_done, t + 1)
                sp.dma_start(count_in[:], row(counts)).then_inc(c_loaded, 16)
                sp.wait_ge(tile_out, t + 1)
                sp.dma_start(countT_in[:, u, :], row(countsT)).then_inc(ct_loaded[u], 16)

            in_pairs(sp, tile)

        @block.gpsimd
        def _(pool):
            nc.gpsimd.memset(key_b[:], 0.0).then_inc(keys_done, 1)
            pool.sem_inc(absent_done, 1)
            pool.wait_ge(keys_done, 1)

            def tile(t, u):
                pool.wait_ge(tile_out, t + 1)
                pool.sem_inc(pool_go, 1)
                here = bass.ds(t * P, P)
                nc.gpsimd.tensor_copy(key_a[:, u], KA[:, :, here]).then_inc(keys_done, 1)
                for s in range(2):
                    pool.wait_ge(keys_done, t * 3 + (2 + s))
                    pool.sem_inc(pool_go, 1)
                    rows = slice(64 * s, 64 * s + 64)
                    nc.gpsimd.tensor_copy(key_b[rows, u].rearrange("p (j s) n -> p s j n", s=2)[:, s], KB[rows, :, here]).then_inc(keys_done, 1)
                pool.wait_ge(c_loaded, t * 16 + 16)
                pool.wait_ge(keys_done, t * 3 + 4)
                pool.sem_inc(pool_go, 1)
                nc.gpsimd.tensor_scalar(absent[:, u, :], count_in[:], 0.0, None, ALU.is_equal).then_inc(absent_done, 1)

            in_pairs(pool, tile)

        @block.tensor
        def _(pe):
            pe.sem_inc(summed, 4)
            pe.wait_ge(low_ready, 1)

            def score_piece(t, u, h, r):
                p = h * PIECES + r
                if p == 0:
                    pe.wait_ge(absent_done, t + 2)
                    pe.wait_ge(keys_done, t * 3 + 4)
                pe.wait_ge(leaky, t * TP + (p + 1))
                at, w = PW * r, width[r]
                out = raw[:, p % 4, 0:w]
                nc.tensor.matmul(out, key_a[:, u, h, :], QA[:, h, at:at + w], start=True, stop=False)
                nc.tensor.matmul(out, key_b[:, u, h, :], QB[:, h // 2, at:at + w], start=False, stop=False)
                nc.tensor.matmul(out, low[:], absent[:, u, at:at + w], start=False, stop=True).then_inc(scored, 1)

            def sum_piece(t, u, h, r):
                p = h * PIECES + r
                pe.wait_ge(counted, t * TP + (p + 3))
                if p == 0:
                    pe.wait_ge(tile_out, t + 1)
                for k in range(width[r] // P):
                    a = 4 * r + k
                    ins = nc.tensor.matmul(mixed[:, u, h * (HID + 1):(h + 1) * (HID + 1)], weighed[:, p % 4, k * P:(k + 1) * P],
                                           V[:, a, h, :], start=(a == 0), stop=(a == TILES - 1))
                ins.then_inc(summed, 1)

            def value_piece(t, u, h, r):
                p = h * PIECES + r
                for s, (at, end) in enumerate(SPANS):
                    if at == PW * r:
                        pe.wait_ge(exped, t * (HEADS * NS) + (h * NS + s + 1))
                pe.wait_ge(counted, t * TP + (p + 1))
                for k in range(width[r] // P):
                    a = 4 * r + k
                    ins = nc.tensor.transpose(probsT[:, p % 2, k * P:(k + 1) * P], score[h % 2][:, a * P:(a + 1) * P],
                                              ident[0:P, 0:P])
                ins.then_inc(turned, 1)
                if p > 0:
                    sum_piece(t, u, (p - 1) // PIECES, (p - 1) % PIECES)
                if p == TP - 1:
                    sum_piece(t, u, h, r)

            all_tiles(pe, score_piece, value_piece)

        @block.scalar
        def _(act):
            def score_piece(t, u, h, r):
                p = h * PIECES + r
                act.wait_ge(scored, t * TP + (p + 1))
                act.wait_ge(leaky, t * TP + (p + 3))
                nc.scalar.activation(rising[:, p % 2, 0:width[r]], raw[:, p % 4, 0:width[r]], ACT.Relu,
                                     scale=1.0 / SLOPE - 1.0).then_inc(scaled, 1)

            def value_piece(t, u, h, r):
                if 2 * r < 2 * NS and r < NS:
                    at, end = SPANS[r]
                    act.wait_ge(shifted, t * (2 * HEADS) + (2 * h + 2))
                    nc.scalar.activation(score[h % 2][:, at:end], score[h % 2][:, at:end], ACT.Exp,
                                         bias=shift[:, h % 2, 1:2]).then_inc(exped, 1)

            AHEAD = PIECES
            def run(t, u, before=True):
                for p in range(TP):
                    score_piece(t, u, p // PIECES, p % PIECES)
                    q = p - AHEAD
                    if q >= 0:
                        value_piece(t, u, q // PIECES, q % PIECES)
                    elif before:
                        value_piece(t - 1, 1 - u, (q + TP) // PIECES, (q + TP) % PIECES)

            run(0, 0, before=False)
            with act.Fori(0, (TILES - 1) // 2) as i:
                run(i * 2 + 1, 1)
                run(i * 2 + 2, 0)
            for r in range(NS):
                value_piece(TILES - 1, 0, HEADS - 1, r)

        @block.vector
        def _(dve):
            dve.sem_inc(leaky, 4)
            dve.sem_inc(counted, 2)
            dve.sem_inc(tile_out, 2)
            nc.vector.tensor_scalar(low[:], ident[0:P, 0:P], -1e30, None, ALU.mult).then_inc(low_ready, 1)

            def score_piece(t, u, h, r):
                p, b = h * PIECES + r, h % 2
                dve.wait_ge(scaled, t * TP + (p + 1))
                dve.sem_inc(vector_go, 1)
                at, w = PW * r, width[r]
                nc.vector.tensor_tensor_reduce(out=score[b][:, at:at + w], in0=raw[:, p % 4, 0:w],
                                               in1=rising[:, p % 2, 0:w], scale=SLOPE, scalar=-3e38, op0=ALU.add,
                                               op1=ALU.max, accum_out=peaks[:, b, r:r + 1]).then_inc(leaky, 1)
                if r == PIECES - 1:
                    dve.wait_ge(leaky, t * TP + (p + 5))
                    nc.vector.tensor_reduce(shift[:, b, 0:1], peaks[:, b, :], axis=AX.X, op=ALU.max).then_inc(shifted, 1)
                    dve.wait_ge(shifted, t * (2 * HEADS) + (2 * h + 1))
                    nc.vector.tensor_scalar(shift[:, b, 1:2], shift[:, b, 0:1], -1.0, None, ALU.mult).then_inc(shifted, 1)

            def value_piece(t, u, h, r):
                p = h * PIECES + r
                if p == 0:
                    dve.wait_ge(ct_loaded[u], (t - u) * 8 + 16)
                dve.wait_ge(turned, t * TP + (p + 1))
                dve.wait_ge(summed, t * TP + (p + 1))
                nc.vector.tensor_tensor(weighed[:, p % 4, 0:width[r]], probsT[:, p % 2, 0:width[r]],
                                        countT_in[:, u, PW * r:PW * r + width[r]], ALU.mult).then_inc(counted, 1)
                if p == TP - 1:
                    finish(t, u)

            def finish(t, u):
                sums = mixed[:, u, 0:HEADS * (HID + 1)].rearrange("p (h o) -> p h o", o=HID + 1)
                dve.wait_ge(summed, t * TP + (TP + 4))
                nc.vector.tensor_scalar(norm[:, 0:HEADS], sums[:, :, HID], 1e-9, None, ALU.max).then_inc(norm_steps, 1)
                dve.wait_ge(norm_steps, t * 3 + 1)
                nc.vector.reciprocal(norm[:, HEADS:], norm[:, 0:HEADS]).then_inc(norm_steps, 1)
                dve.wait_ge(norm_steps, t * 3 + 2)
                nc.vector.tensor_tensor(heads_out[:], sums[:, :, 0:HID],
                                        norm[:, HEADS:].unsqueeze(2).broadcast_to([P, HEADS, HID]), ALU.mult).then_inc(norm_steps, 1)
                dve.wait_ge(norm_steps, t * 3 + 3)
                nc.vector.tensor_tensor(row_of(X, t), row_of(X, t), heads_out[:].rearrange("p h o -> p (h o)"),
                                        ALU.add).then_inc(tile_out, 1)

            all_tiles(dve, score_piece, value_piece)


def one_over_degree(nc, in_parts, per_node):
    with nc.semaphore(unique("degree_done")) as degree_done, nc.Block() as block:
        @block.vector
        def _(dve):
            link = chained(dve, degree_done)
            link(nc.vector.tensor_reduce(per_node[:], in_parts[:], axis=AX.X, op=ALU.add))
            link(nc.vector.tensor_scalar(per_node[:], per_node[:], 1.0, None, ALU.add))
            link(nc.vector.reciprocal(per_node[:], per_node[:]))


def weighted_step(nc, weightsT, Y, YT, Z, W, ones, per_node, step):
    BUFS = 5
    with ExitStack() as c:
        e = c.enter_context
        block_in = e(nc.sbuf_tensor(unique("weights_in"), [P, BUFS, N], F32))
        own = e(nc.sbuf_tensor(unique("own"), [D, BUFS, P], F32))
        total = e(nc.sbuf_tensor(unique("total"), [D, BUFS, P], F32))
        self_part = e(nc.sbuf_tensor(unique("self_part"), [P, D], F32))
        mixed = e(nc.sbuf_tensor(unique("mixed"), [P, D], F32))
        agg = e(nc.psum_tensor(unique("agg"), [D, BUFS, 512], F32))
        lin = e(nc.psum_tensor(unique("lin"), [P, 2 * D], F32))
        loaded = [e(nc.semaphore(unique(f"w_loaded{u}"))) for u in range(BUFS)]
        summed = e(nc.semaphore(unique("agg_summed")))
        own_ready = e(nc.semaphore(unique("own_ready")))
        totalled = e(nc.semaphore(unique("totalled")))
        applied = e(nc.semaphore(unique("applied")))
        self_copied = e(nc.semaphore(unique("self_copied")))
        mixed_done = e(nc.semaphore(unique("mixed_done")))
        z_done = e(nc.semaphore(unique("z_done")))
        block = e(nc.Block())

        @block.sync
        def _(sp):
            def tile(t, u):
                sp.wait_ge(summed, t + 1)
                sp.dma_start(block_in[:, u, :], weightsT[bass.ds(t, 1)].rearrange("o p n -> (o p) n")).then_inc(loaded[u], 16)

            in_turns(sp, tile, BUFS)

        @block.scalar
        def _(act):
            def copy_own(t, u):
                act.wait_ge(applied, t + 1)
                nc.scalar.copy(own[:, u, :], YT[:, bass.ds(t * P, P)]).then_inc(own_ready, 1)

            def tile(t, u):
                copy_own(t, u)
                act.wait_ge(applied, t + (BUFS + 1))
                act.wait_ge(mixed_done, t + 1)
                nc.scalar.copy(self_part[:], lin[:, D:2 * D]).then_inc(self_copied, 1)

            in_turns(act, tile, BUFS)

        @block.vector
        def _(dve):
            dve.sem_inc(totalled, BUFS)
            dve.sem_inc(mixed_done, 1)

            def tile(t, u):
                dve.wait_ge(summed, t + (BUFS + 1))
                dve.wait_ge(own_ready, t + 1)
                nc.vector.tensor_tensor(total[:, u, :], agg[:, u, 0:P], own[:, u, :], ALU.add).then_inc(totalled, 1)
                dve.wait_ge(self_copied, t + 1)
                nc.vector.scalar_tensor_tensor(mixed[:], lin[:, 0:D], per_node[:, bass.ds(t, 1)], self_part[:],
                                               ALU.mult, ALU.add).then_inc(mixed_done, 1)
                dve.wait_ge(mixed_done, t + 2)
                nc.vector.scalar_tensor_tensor(row_of(Z, t), mixed[:], SLOPE, mixed[:], ALU.mult,
                                               ALU.max).then_inc(z_done, 1)

            in_turns(dve, tile, BUFS)

        @block.tensor
        def _(pe):
            pe.sem_inc(summed, BUFS)
            pe.sem_inc(applied, BUFS)

            def tile(t, u, i):
                pe.wait_ge(loaded[u], i * 16 + 16)
                pe.wait_ge(totalled, t + 1)
                for a in range(TILES):
                    ins = nc.tensor.matmul(agg[:, u, 0:P], Y[:, a, :], block_in[:, u, a * P:(a + 1) * P],
                                           start=(a == 0), stop=(a == TILES - 1))
                ins.then_inc(summed, 1)
                pe.wait_ge(totalled, t + (BUFS + 1))
                pe.wait_ge(mixed_done, t + 1)
                nc.tensor.matmul(lin[:, 0:D], total[:, u, :], W[f"Wn{step}"][:], start=True, stop=True)
                nc.tensor.matmul(lin[:, D:2 * D], own[:, u, :], W[f"Ws{step}"][:], start=True, stop=False)
                nc.tensor.matmul(lin[:, D:2 * D], ones[0:1, 0:P], W["bias"][0:1, 3 + step, :], start=False,
                                 stop=True).then_inc(applied, 1)

            with pe.Fori(0, TILES // BUFS) as i:
                for u in range(BUFS):
                    tile(i * BUFS + u, u, i)


def weighted_output(nc, X, YT, W, ones):
    with ExitStack() as c:
        e = c.enter_context
        lin = e(nc.psum_tensor(unique("lin"), [P, 2, 512], F32))
        bias = e(nc.psum_tensor(unique("bias_rows"), [P, D], F32))
        multiplied = e(nc.semaphore(unique("multiplied")))
        added = e(nc.semaphore(unique("rows_added")))
        block = e(nc.Block())

        @block.tensor
        def _(pe):
            nc.tensor.matmul(bias[:], ones[0:1, 0:P], W["bias"][0:1, 1, :], start=True, stop=True)
            for r, a0, n in quads():
                if r >= 2:
                    pe.wait_ge(added, r)
                for a in range(a0, a0 + n):
                    ins = nc.tensor.matmul(lin[:, r % 2, (a - a0) * D:(a - a0 + 1) * D], YT[:, a * P:(a + 1) * P],
                                           W["Wa"][:], start=True, stop=True)
                ins.then_inc(multiplied, 1)

        @block.vector
        def _(dve):
            dve.wait_ge(multiplied, 1)
            nc.vector.tensor_tensor(X[:], X[:], bias[:].unsqueeze(1).broadcast_to([P, TILES, D]), ALU.add).then_inc(added, 1)
            dve.wait_ge(added, 1)
            for r, a0, n in quads():
                dve.wait_ge(multiplied, r + 1)
                part = X[:, a0:a0 + n, :].rearrange("p a d -> p (a d)")
                nc.vector.tensor_tensor(part, part, lin[:, r % 2, 0:n * D], ALU.add).then_inc(added, 1)


def edge_layer(nc, T, X, HT, W, ones, ident, projected):
    BUFS = 3
    EDGES = EG * P
    ROWS16 = EG * EDIM
    with ExitStack() as c:
        e = c.enter_context
        rows = e(nc.sbuf_tensor(unique("xw_rows"), [P, TILES, D], F32))
        src_i = e(nc.sbuf_tensor(unique("src_i"), [P, EGROUPS, EG], I32))
        dst_i = e(nc.sbuf_tensor(unique("dst_i"), [P, EGROUPS, EG], I32))
        dst_rel = e(nc.sbuf_tensor(unique("dst_rel"), [P, EGROUPS, EG], F32))
        base_i = e(nc.sbuf_tensor(unique("base_i"), [1, EGROUPS], I32))
        base_f = e(nc.sbuf_tensor(unique("base_f"), [1, EGROUPS], F32))
        span_i = e(nc.sbuf_tensor(unique("span_i"), [P, SPAN], I32))
        span = e(nc.sbuf_tensor(unique("span"), [P, SPAN], F32))
        attr = e(nc.sbuf_tensor(unique("attr"), [P, BUFS, ROWS16], F32))
        mix = e(nc.sbuf_tensor(unique("mix"), [ROWS16, EG, D], F32))
        attrT = e(nc.sbuf_tensor(unique("attrT"), [ROWS16, BUFS, P], F32))
        gathered = e(nc.sbuf_tensor(unique("gathered_rows"), [P, BUFS, EG, D], F32))
        message = e(nc.sbuf_tensor(unique("message"), [P, BUFS, EG, D], F32))
        index = e(nc.sbuf_tensor(unique("index"), [P, BUFS, EG], I32))
        hot = e(nc.sbuf_tensor(unique("hot"), [P, BUFS, EG, SPAN], F32))
        acc = e(nc.sbuf_tensor(unique("acc"), [D, N + SPAN], F32))
        with ExitStack() as c1:
            e = c1.enter_context
            lin = e(nc.psum_tensor(unique("lin"), [P, 2, 512], F32))
            bias = e(nc.psum_tensor(unique("bias_rows"), [P, D], F32))
            bases = e(nc.psum_tensor(unique("bases"), [P, EGROUPS], F32))
            edges_in = e(nc.semaphore(unique("edges_in")))
            attr_in = e(nc.semaphore(unique("attr_in")))
            mix_zero = e(nc.semaphore(unique("mix_zero")))
            pool_done = e(nc.semaphore(unique("pool_done")))
            multiplied = e(nc.semaphore(unique("multiplied")))
            copied = e(nc.semaphore(unique("rows_copied")))
            rel_done = e(nc.semaphore(unique("rel_done")))
            base_ready = e(nc.semaphore(unique("base_ready")))
            base_spread = e(nc.semaphore(unique("base_spread")))
            stored = e(nc.semaphore(unique("rows_stored")))
            block = e(nc.Block())

            @block.gpsimd
            def _(pool):
                nc.gpsimd.memset(mix[:], 0.0).then_inc(mix_zero, 1)
                nc.gpsimd.memset(acc[:], 0.0)
                nc.gpsimd.iota(span_i[:], [[1, SPAN]], base=0, channel_multiplier=0).then_inc(pool_done, 1)

            @block.sync
            def _(sp):
                with nc.allow_non_contiguous_dma(reason="runs of five edges, and one destination of every group"):
                    sp.dma_start(base_i[:], T["dst"].rearrange("(o g r) -> o g r", o=1, r=EDGES)[:, :, 0]).then_inc(edges_in, 16)
                    sp.dma_start(src_i[:], T["src"].rearrange("(g p c) -> p g c", p=P, c=EG)).then_inc(edges_in, 16)
                    sp.dma_start(dst_i[:], T["dst"].rearrange("(g p c) -> p g c", p=P, c=EG)).then_inc(edges_in, 16)
                sp.wait_ge(mix_zero, 1)
                for k in range(EG):
                    sp.dma_start(mix[k * EDIM:(k + 1) * EDIM, k, :], T["L3_gnn_edge_w"]).then_inc(attr_in, 16)
                sp.wait_ge(copied, len(quads()))
                sp.dma_start(projected.rearrange("(t p) f -> p t f", p=P), rows[:]).then_inc(stored, 16)
                sp.wait_ge(stored, 16)
                sp.wait_ge(attr_in, 16 * EG)

            @block.tensor
            def _(pe):
                for r, a0, n in quads():
                    if r >= 2:
                        pe.wait_ge(copied, r - 1)
                    for a in range(a0, a0 + n):
                        ins = nc.tensor.matmul(lin[:, r % 2, (a - a0) * D:(a - a0 + 1) * D], HT[:, a * P:(a + 1) * P],
                                               W["W3"][:], start=True, stop=True)
                    ins.then_inc(multiplied, 1)
                nc.tensor.matmul(bias[:], ones[0:1, 0:P], W["bias"][0:1, 2, :], start=True, stop=True).then_inc(base_spread, 1)
                pe.wait_ge(base_ready, 1)
                nc.tensor.matmul(bases[:], ones[0:1, 0:P], base_f[:], start=True, stop=True).then_inc(base_spread, 1)

            @block.scalar
            def _(act):
                for r, a0, n in quads():
                    act.wait_ge(multiplied, r + 1)
                    nc.scalar.copy(rows[:, a0:a0 + n, :].rearrange("p a d -> p (a d)"), lin[:, r % 2, 0:n * D]).then_inc(copied, 1)

            @block.vector
            def _(dve):
                link = chained(dve, rel_done)
                dve.wait_ge(pool_done, 1)
                nc.vector.tensor_copy(span[:], span_i[:])
                dve.wait_ge(edges_in, 48)
                nc.vector.tensor_copy(base_f[:], base_i[:]).then_inc(base_ready, 1)
                link(nc.vector.tensor_copy(dst_rel[:], dst_i[:]))
                dve.wait_ge(base_spread, 2)
                nc.vector.tensor_tensor(X[:], X[:], bias[:].unsqueeze(1).broadcast_to([P, TILES, D]), ALU.add)
                link(nc.vector.tensor_tensor(dst_rel[:], dst_rel[:], bases[:].unsqueeze(2).broadcast_to([P, EGROUPS, EG]),
                                             ALU.subtract))

        with ExitStack() as c2:
            e = c2.enter_context
            flat = e(nc.psum_tensor(unique("attr_flipped"), [ROWS16, P], F32))
            factor = [e(nc.psum_tensor(unique(f"factor{u}"), [P, 2, 512], F32)) for u in range(BUFS)]
            sums = e(nc.psum_tensor(unique("sums"), [D, SPAN], F32))
            started = e(nc.semaphore(unique("started")))
            arrived = [e(nc.semaphore(unique(f"arrived{u}"))) for u in range(BUFS)]
            attr_loaded = [e(nc.semaphore(unique(f"attr_loaded{u}"))) for u in range(BUFS)]
            turned = e(nc.semaphore(unique("attr_turned")))
            kept = e(nc.semaphore(unique("attr_kept")))
            factored = e(nc.semaphore(unique("factored")))
            made = e(nc.semaphore(unique("message_made")))
            reduced = e(nc.semaphore(unique("reduced")))
            added = e(nc.semaphore(unique("sums_added")))
            indexed = e(nc.semaphore(unique("indexed")))
            block = e(nc.Block())

            @block.sync
            def _(sp):
                attributes = T["edge_attr_16"].rearrange("(g p c) k -> g p (c k)", p=P, c=EG)

                def group(g, u):
                    sp.wait_ge(factored, g + 1)
                    sp.dma_start(attr[:, u, :], attributes[bass.ds(g, 1)].rearrange("o p n -> (o p) n")).then_inc(attr_loaded[u], 16)

                in_turns(sp, group, BUFS, EGROUPS)

            @block.gpsimd
            def _(pool):
                def group(g, u):
                    pool.wait_ge(indexed, g + 1)
                    pool.sem_inc(started, 1)
                    for k in range(EG):
                        nc.gpsimd.indirect_dma_start(gathered[:, u, k, :], None, projected,
                                                     bass.IndirectOffsetOnAxis(ap=index[:, u, k:k + 1], axis=0)
                                                     ).then_inc(arrived[u], 16)

                in_turns(pool, group, BUFS, EGROUPS)

            @block.scalar
            def _(act):
                act.sem_inc(kept, 1)

                def copy_index(g, u):
                    act.wait_ge(made, g + 1)
                    nc.scalar.copy(index[:, u, :], row_of(src_i, g)).then_inc(indexed, 1)

                def keep_attributes(g, u):
                    act.wait_ge(turned, g + 1)
                    act.wait_ge(factored, g + 1)
                    nc.scalar.copy(attrT[:, u, :], flat[:]).then_inc(kept, 1)

                copy_index(0, 0)
                keep_attributes(0, 0)
                copy_index(1, 1)

                def group(g, u):
                    keep_attributes(g + 1, (u + 1) % BUFS)
                    copy_index(g + 2, (u + 2) % BUFS)

                with act.Fori(0, EGROUPS // BUFS - 1) as i:
                    for u in range(BUFS):
                        group(i * BUFS + u, u)
                for g in range(EGROUPS - BUFS, EGROUPS - 2):
                    group(g, g % BUFS)
                keep_attributes(EGROUPS - 1, (EGROUPS - 1) % BUFS)

            @block.tensor
            def _(pe):
                pe.sem_inc(factored, BUFS)
                pe.sem_inc(reduced, BUFS)

                def factors(g, u, i):
                    pe.wait_ge(kept, g + 1)
                    pe.wait_ge(attr_loaded[u], i * 16 + 16)
                    nc.tensor.transpose(flat[:], attr[:, u, :], ident[0:P, 0:P]).then_inc(turned, 1)
                    pe.wait_ge(kept, g + 2)
                    pe.wait_ge(made, g + 1)
                    for h in range(2):
                        ins = nc.tensor.matmul(factor[u][:, h, 0:EG * D // 2], attrT[:, u, :],
                                               mix[:].rearrange("r c d -> r (c d)")[:, h * EG * D // 2:(h + 1) * EG * D // 2],
                                               start=True, stop=True)
                    ins.then_inc(factored, 1)

                def sum_edges(g, u):
                    pe.wait_ge(made, g + (BUFS + 1))
                    pe.wait_ge(added, g + 1)
                    for k in range(EG):
                        ins = nc.tensor.matmul(sums[:], message[:, u, k, :], hot[:, u, k, :], start=(k == 0),
                                               stop=(k == EG - 1))
                    ins.then_inc(reduced, 1)

                factors(0, 0, 0)
                with pe.Fori(0, EGROUPS // BUFS - 1) as i:
                    for u in range(BUFS):
                        factors(i * BUFS + (u + 1), (u + 1) % BUFS, i + (u + 1) // BUFS)
                        sum_edges(i * BUFS + u, u)
                for g in range(EGROUPS - BUFS, EGROUPS):
                    if g + 1 < EGROUPS:
                        factors(g + 1, (g + 1) % BUFS, (g + 1) // BUFS)
                    sum_edges(g, g % BUFS)

            @block.vector
            def _(dve):
                dve.sem_inc(made, BUFS)
                dve.sem_inc(added, 1)
                with dve.Fori(0, EGROUPS // BUFS) as i:
                    for u in range(BUFS):
                        g = i * BUFS + u
                        dve.wait_ge(reduced, g + 1)
                        nc.vector.tensor_tensor(hot[:, u], dst_rel[:, bass.ds(g, 1), :].rearrange("p o c -> p (o c)").unsqueeze(2).broadcast_to([P, EG, SPAN]),
                                                span[:].unsqueeze(1).broadcast_to([P, EG, SPAN]), ALU.is_equal)
                        dve.wait_ge(factored, g + (BUFS + 1))
                        dve.wait_ge(arrived[u], i * (16 * EG) + 16 * EG)
                        nc.vector.tensor_tensor(message[:, u].rearrange("p c d -> p (c d)").rearrange("p (h n) -> p h n", h=2),
                                                gathered[:, u].rearrange("p c d -> p (c d)").rearrange("p (h n) -> p h n", h=2),
                                                factor[u][:, :, 0:EG * D // 2], ALU.mult).then_inc(made, 1)
                        base = dve.value_load(base_i[0:1, bass.ds(g, 1)], min_val=0, max_val=N - 1)
                        dve.wait_ge(reduced, g + (BUFS + 1))
                        dve.wait_ge(added, g + 1)
                        nc.vector.tensor_tensor(acc[:, bass.ds(base, SPAN)], acc[:, bass.ds(base, SPAN)], sums[:],
                                                ALU.add).then_inc(added, 1)

        with ExitStack() as c3:
            e = c3.enter_context
            back = e(nc.psum_tensor(unique("back"), [P, 2, 512], F32))
            turned = e(nc.semaphore(unique("acc_turned")))
            added = e(nc.semaphore(unique("acc_added")))
            stored = e(nc.semaphore(unique("out_stored")))
            block = e(nc.Block())

            @block.tensor
            def _(pe):
                for r, a0, n in quads():
                    if r >= 2:
                        pe.wait_ge(added, r - 1)
                    for a in range(a0, a0 + n):
                        ins = nc.tensor.transpose(back[:, r % 2, (a - a0) * D:(a - a0 + 1) * D], acc[:, a * P:(a + 1) * P], ident[:])
                    ins.then_inc(turned, 1)

            @block.vector
            def _(dve):
                for r, a0, n in quads():
                    dve.wait_ge(turned, r + 1)
                    part = X[:, a0:a0 + n, :].rearrange("p a d -> p (a d)")
                    nc.vector.tensor_tensor(part, part, back[:, r % 2, 0:n * D], ALU.add).then_inc(added, 1)

            @block.sync
            def _(sp):
                out = T["out"].rearrange("(t p) f -> p t f", p=P)
                for r, a0, n in quads():
                    sp.wait_ge(added, r + 1)
                    sp.dma_start(out[:, a0:a0 + n, :], X[:, a0:a0 + n, :]).then_inc(stored, 16)
                sp.wait_ge(stored, 16 * len(quads()))


def program(nc, T):
    dram = lambda name, shape, dt: nc.dram_tensor(name, shape, dt, kind="Internal").ap()
    table = dram("scratch_table", (ROWS + GROWS, 3 * ROW), I32)
    starts = dram("scratch_starts", (WINDOWS,), I32)
    countsT = dram("scratch_countsT", (TILES, P, N), F32)
    weightsT = dram("scratch_weightsT", (TILES, P, N), F32)
    projected = dram("scratch_projected", (N, D), F32)
    counts = dram("scratch_counts", (TILES, P, N), F32)

    def sb(name, shape, dt=F32):
        return nc.sbuf_tensor(unique(name), shape, dt)

    def ps(name, shape):
        return nc.psum_tensor(unique(name), shape, F32)

    with ExitStack() as whole:
        keep = whole.enter_context
        X = keep(sb("X", [P, TILES, D]))
        H = keep(sb("H", [P, TILES, D]))
        stats = keep(sb("stats", [P, TILES, 6]))
        mv = keep(sb("mv", [P, TILES, 2]))
        rstd = keep(sb("rstd", [P, TILES]))
        ident = keep(sb("ident", [128, 128]))
        ones = keep(sb("ones", [128, P]))
        out_degree = keep(sb("out_degree", [P, TILES]))
        in_parts = keep(sb("in_parts", [P, TILES, 7]))

        W = {name: keep(sb(name, [D, D])) for name in ("W0", "Ws0", "Ws1", "Wn0", "Wn1", "Wa", "Wq", "Wk", "Wv", "W3")}
        W["bias"] = keep(sb("bias", [1, 5, D]))

        with ExitStack() as lists:
            hold = lists.enter_context
            src_hi = hold(sb("src_hi", [P, 2 * WINDOWS]))
            src_lo = hold(sb("src_lo", [P, 2 * WINDOWS]))
            dst_in = hold(sb("dst_in", [P, 2 * WINDOWS]))
            weight = hold(sb("weight", [P, 2 * WINDOWS]))
            iota = hold(sb("iota", [P, P]))
            iota_tile = hold(sb("iota_tile", [P, TILES]))
            window_starts(nc, T, table, starts, X, H, stats, mv, rstd, ident, ones, iota, iota_tile)
            edge_slots(nc, table, starts, ident, src_hi, src_lo, dst_in, weight)
            adjacency(nc, counts, countsT, weightsT, ident, src_hi, src_lo, dst_in, weight, iota,
                      iota_tile, out_degree, in_parts)
        load_weights(nc, T, W, ident)
        gcn_layer(nc, counts, X, H, W, ones, out_degree)
        per_node = keep(sb("per_node", [P, TILES]))
        one_over_degree(nc, in_parts, per_node)
        with ExitStack() as heads:
            hold = heads.enter_context
            QA = hold(sb("QA", [D, HEADS, N], BF16))
            KA = hold(sb("KA", [D, HEADS, N], BF16))
            QB = hold(sb("QB", [D, HEADS // 2, N], BF16))
            KB = hold(sb("KB", [D, HEADS // 2, N], BF16))
            V = hold(sb("V", [P, TILES, HEADS, HID + 1]))
            with sb("HT", [D, N]) as HT:
                normalize(nc, X, H, HT, stats, mv, rstd, ident)
                project(nc, HT, W, QA, QB, KA, KB, V)
            attention(nc, counts, countsT, X, H, QA, QB, KA, KB, V, ident)
        with sb("HT", [D, N]) as HT:
            normalize(nc, X, H, HT, stats, mv, rstd, ident)
            with sb("Z", [P, TILES, D]) as Z:
                weighted_step(nc, weightsT, H, HT, Z, W, ones, per_node, 0)
                turn(nc, Z, HT, ident)
                weighted_step(nc, weightsT, Z, HT, H, W, ones, per_node, 1)
                turn(nc, H, HT, ident)
            weighted_output(nc, X, HT, W, ones)
            normalize(nc, X, H, HT, stats, mv, rstd, ident)
            edge_layer(nc, T, X, HT, W, ones, ident, projected)


_INS = ['x', 'src', 'dst', 'edge_attr_16', 'edge_weight', 'L0_gnn_W', 'L0_gnn_b', 'L1_gnn_Wq', 'L1_gnn_Wk',
        'L1_gnn_Wv', 'L2_gnn_W_self', 'L2_gnn_b_self', 'L2_gnn_W_neigh', 'L2_gnn_b_neigh', 'L2_gnn_layer_bias',
        'L2_gnn_W_agg', 'L2_gnn_b_agg', 'L3_gnn_W', 'L3_gnn_edge_w', 'L3_gnn_b']


def kernel(**inputs):
    import numpy as _np
    import concourse.bacc as _bacc
    from concourse import mybir as _mybir
    from concourse.bass_utils import run_bass_kernel_spmd as _run

    nc = _bacc.Bacc("TRN2", target_bir_lowering=False, num_devices=1)
    arrays, operands = {}, {}
    for name in _INS:
        a = _np.ascontiguousarray(inputs[name])
        arrays[f"in_{name}"] = a
        operands[name] = nc.dram_tensor(f"in_{name}", a.shape, _mybir.dt.from_np(a.dtype), kind="ExternalInput").ap()
    operands["out"] = nc.dram_tensor("out_0", (N, D), F32, kind="ExternalOutput").ap()
    program(nc, operands)
    r = _run(nc, [arrays], core_ids=[0])
    return r.results[0]["out_0"]
```

```python
from contextlib import ExitStack
from itertools import count

import concourse.bass as bass
from concourse import mybir
from concourse.alu_op_type import AluOpType as ALU

F32 = mybir.dt.float32
BF16 = mybir.dt.bfloat16
I32 = mybir.dt.int32
ACT = mybir.ActivationFunctionType
AX = mybir.AxisListType

N = 3125
E = 103125
D = 128
P = 125
TILES = N // P
WIN = 5
WINDOWS = N // WIN
WPT = P // WIN
BLOCKS = WINDOWS // P
ROW = 25
ROWS = E // ROW
GROWS = 10
SLOTS = ROW * GROWS // 2
CHUNKS = E // P
MAGIC = 1.5 * 2 ** 23
GRP = 5
NGRP = WPT // GRP
EG = 5
EGROUPS = CHUNKS // EG
SPAN = 32
LN_EPS = 1e-5
SLOPE = 0.2
HEADS, HID = 4, 32
EDIM = 16


NAMES = count(1)


def unique(name):
    return f"{name}_{next(NAMES)}"


def recorded_semaphores(nc, enter, used):
    def sem(name):
        used.append(enter(nc.semaphore(unique(name))))
        return used[-1]

    return sem


def clear_used(pool, used):
    for s in used:
        pool.sem_clear(s)


def chained(eng, sem, start=0):
    done = [start]

    def link(ins):
        done[0] += 1
        ins.then_inc(sem, 1)
        eng.wait_ge(sem, done[0])

    return link


def in_pairs(eng, body, n=TILES):
    with eng.Fori(0, n // 2) as i:
        body(i * 2, 0)
        body(i * 2 + 1, 1)
    if n % 2:
        body(n - 1, 0)


def row_of(ap3, t):
    return ap3[:, bass.ds(t, 1), :].rearrange("p o f -> p (o f)")


def floor_div(nc, link, out, x, d):
    link(nc.vector.tensor_scalar(out, x, 1.0 / d, -((d - 1) // 2) / d, ALU.mult, ALU.add))
    link(nc.vector.tensor_scalar(out, out, MAGIC, -MAGIC, ALU.add, ALU.add))


def quads():
    return [(r, 4 * r, min(4, TILES - 4 * r)) for r in range((TILES + 3) // 4)]


NORM_PARTS = ((0, 12), (12, TILES))


def layer_norm_relu(nc, dve, link, X, H, norm, var_ready, std_ready, inv_ready):
    stats, mv, rstd = norm
    for s, (a, b) in enumerate(NORM_PARTS):
        for t in range(a, b):
            ins = nc.vector.bn_stats(stats[:, t, :], X[:, t, :])
        link(ins)
        for t in range(a, b):
            ins = nc.vector.bn_aggr(mv[:, t, :], stats[:, t, :])
        link(ins)
        nc.vector.tensor_scalar(rstd[:, a:b], mv[:, a:b, 1], LN_EPS, None, ALU.add).then_inc(var_ready, 1)
        for t in range(a, b):
            nc.vector.tensor_scalar(H[:, t, :], X[:, t, :], mv[:, t, 0:1], 0.0, ALU.subtract, ALU.max)
        dve.wait_ge(std_ready, s + 1)
        nc.vector.reciprocal(rstd[:, a:b], rstd[:, a:b]).then_inc(inv_ready, 1)


def scale_rows(nc, act, H, norm, var_ready, std_ready, inv_ready, h_ready):
    stats, mv, rstd = norm
    for s, (a, b) in enumerate(NORM_PARTS):
        act.wait_ge(var_ready, s + 1)
        nc.scalar.activation(rstd[:, a:b], rstd[:, a:b], ACT.Sqrt).then_inc(std_ready, 1)
        act.wait_ge(inv_ready, s + 1)
        for r, a0, n in quads():
            if a <= a0 < b:
                for t in range(a0, a0 + n):
                    ins = nc.scalar.activation(H[:, t, :], H[:, t, :], ACT.Copy, scale=rstd[:, t:t + 1])
                ins.then_inc(h_ready, 1)


def window_starts(nc, T, table, starts, X, ident, ones, iota, iota_tile, irregular):
    used = []
    with ExitStack() as c:
        e = c.enter_context
        sem = recorded_semaphores(nc, e, used)
        dst_i = e(nc.sbuf_tensor(unique("dst_i"), [P, CHUNKS + 1], I32))
        ends_i = e(nc.sbuf_tensor(unique("ends_i"), [EGROUPS // EG, 2, EG], I32))
        falls = e(nc.sbuf_tensor(unique("falls"), [P, CHUNKS], F32))
        wide = e(nc.sbuf_tensor(unique("wide"), [EGROUPS // EG, EG], F32))
        over = e(nc.sbuf_tensor(unique("over"), [TILES, WPT], F32))
        end = e(nc.sbuf_tensor(unique("end"), [TILES, WPT], F32))
        faults = e(nc.sbuf_tensor(unique("faults"), [P, 3], F32))
        faults_ps = e(nc.psum_tensor(unique("faults_ps"), [1, 2], F32))
        win_hi = e(nc.sbuf_tensor(unique("win_hi"), [P, CHUNKS], F32))
        win_lo = e(nc.sbuf_tensor(unique("win_lo"), [P, CHUNKS], F32))
        one_hi = e(nc.sbuf_tensor(unique("one_hi"), [P, CHUNKS, TILES], BF16))
        one_lo = e(nc.sbuf_tensor(unique("one_lo"), [P, CHUNKS, WPT], BF16))
        pad = e(nc.sbuf_tensor(unique("pad"), [GROWS, 3 * ROW], I32))
        iota_i = e(nc.sbuf_tensor(unique("iota_i"), [P, P], I32))
        iota_ti = e(nc.sbuf_tensor(unique("iota_ti"), [P, TILES], I32))
        fold = e(nc.sbuf_tensor(unique("fold"), [P, TILES], F32))
        same = e(nc.sbuf_tensor(unique("same"), [P, GRP], F32))
        before = e(nc.sbuf_tensor(unique("before"), [TILES, TILES], F32))
        pairs = e(nc.sbuf_tensor(unique("pairs"), [P, P], F32))
        hist = e(nc.sbuf_tensor(unique("hist"), [TILES, WPT], F32))
        upto = e(nc.sbuf_tensor(unique("upto"), [TILES, WPT], F32))
        zeros = e(nc.sbuf_tensor(unique("zeros"), [TILES, WPT], F32))
        first = e(nc.sbuf_tensor(unique("first"), [TILES, WPT], F32))
        first_i = e(nc.sbuf_tensor(unique("first_i"), [TILES, WPT], I32))
        pairs_ps = e(nc.psum_tensor(unique("pairs_ps"), [P, P], F32))
        hist_ps = e(nc.psum_tensor(unique("hist_ps"), [TILES, P], F32))
        off_ps = e(nc.psum_tensor(unique("off_ps"), [TILES, 2], F32))
        x_in = sem("x_in")
        dst_in = sem("dst_loaded")
        ends_in = sem("ends_in")
        table_done = sem("table_done")
        pool_done = sem("pool_done")
        dve_done = sem("dve_done")
        pe_done = sem("pe_done")
        starts_done = sem("starts_done")
        block = e(nc.Block())
        marks = {}

        @block.gpsimd
        def _(pool):
            link = chained(pool, pool_done)
            link(nc.gpsimd.memset(ident[:], 0.0))
            link(nc.gpsimd.memset(before[:], 1.0))
            link(nc.gpsimd.affine_select(out=ident[:], in_=ident[:], compare_op=ALU.not_equal, fill=1.0, base=0,
                                         pattern=[[-1, 128]], channel_multiplier=1))
            link(nc.gpsimd.affine_select(out=before[:], in_=before[:], compare_op=ALU.is_gt, fill=0.0, base=0,
                                         pattern=[[1, TILES]], channel_multiplier=-1))
            link(nc.gpsimd.iota(iota_i[:], [[1, P]], base=0, channel_multiplier=0))
            link(nc.gpsimd.iota(iota_ti[:], [[P, TILES]], base=0, channel_multiplier=0))
            link(nc.gpsimd.memset(pad[:, 0:2 * ROW], -1))
            link(nc.gpsimd.memset(pad[:, 2 * ROW:], 0))
            link(nc.gpsimd.memset(zeros[:], 0.0))
            link(nc.gpsimd.memset(ones[:], 1.0))
            link(nc.gpsimd.memset(dst_i[:, CHUNKS:], N))

        def vector(dve):
            count = [0]

            def link(ins):
                count[0] += 1
                ins.then_inc(dve_done, 1)
                dve.wait_ge(dve_done, count[0])

            dve.wait_ge(pool_done, 11)
            link(nc.vector.tensor_copy(iota[:], iota_i[:]))
            link(nc.vector.tensor_copy(iota_tile[:], iota_ti[:]))
            blocks = ident[0:P, 0:P].rearrange("p (j h) -> p j h", h=TILES)
            link(nc.vector.tensor_reduce(fold[:], blocks.rearrange("p j h -> p h j"), axis=AX.X, op=ALU.add))
            link(nc.vector.tensor_reduce(same[:], blocks, axis=AX.X, op=ALU.add))
            dve.wait_ge(dst_in, 16)
            link(nc.vector.tensor_copy(win_lo[:], dst_i[:, 0:CHUNKS]))
            floor_div(nc, link, win_lo[:], win_lo[:], WIN)
            floor_div(nc, link, win_hi[:], win_lo[:], WPT)
            link(nc.vector.scalar_tensor_tensor(win_lo[:], win_hi[:], -float(WPT), win_lo[:], ALU.mult, ALU.add))
            step = CHUNKS // 5
            for k in range(5):
                part = slice(k * step, (k + 1) * step)
                for one, win in ((one_hi, win_hi), (one_lo, win_lo)):
                    link(nc.vector.tensor_tensor(one[:, part, :],
                                                 win[:, part].unsqueeze(2).broadcast_to([P, step, TILES]),
                                                 iota[:, 0:TILES].unsqueeze(1).broadcast_to([P, step, TILES]),
                                                 ALU.is_equal))
                marks["one", k] = count[0]
            dve.wait_ge(ends_in, 48)
            link(nc.vector.tensor_tensor(falls[:], dst_i[:, 1:], dst_i[:, 0:CHUNKS], ALU.is_lt))
            link(nc.vector.tensor_reduce(faults[:, 0:1], falls[:], axis=AX.X, op=ALU.add))
            link(nc.vector.tensor_tensor(wide[:], ends_i[:, 1, :], ends_i[:, 0, :], ALU.subtract))
            link(nc.vector.tensor_scalar(wide[:], wide[:], float(SPAN), None, ALU.is_ge))
            link(nc.vector.tensor_reduce(faults[0:EGROUPS // EG, 1:2], wide[:], axis=AX.X, op=ALU.add))
            dve.wait_ge(pe_done, 1)
            link(nc.vector.tensor_tensor(pairs[:].rearrange("p (j m) -> p j m", m=WPT),
                                         pairs_ps[:].rearrange("p (j m) -> p j m", m=WPT),
                                         same[:].unsqueeze(2).broadcast_to([P, GRP, WPT]), ALU.mult))
            marks["pairs"] = count[0]
            dve.wait_ge(pe_done, 2)
            link(nc.vector.tensor_reduce(hist[:], hist_ps[:].rearrange("h (j m) -> h m j", m=WPT), axis=AX.X,
                                         op=ALU.add))
            link(nc.vector.tensor_tensor_scan(upto[:], hist[:], zeros[:], 0.0, ALU.add, ALU.add))
            marks["upto"] = count[0]
            dve.wait_ge(pe_done, 3)
            link(nc.vector.tensor_tensor(first[:], upto[:], hist[:], ALU.subtract))
            link(nc.vector.tensor_scalar(first[:], first[:], off_ps[:, 0:1], None, ALU.add))
            floor_div(nc, link, first[:], first[:], ROW)
            link(nc.vector.tensor_copy(first_i[:], first[:]))
            marks["starts"] = count[0]
            link(nc.vector.tensor_scalar(end[:], upto[:], off_ps[:, 0:1], None, ALU.add))
            link(nc.vector.scalar_tensor_tensor(over[:], first[:], float(ROW), end[:], ALU.mult, ALU.subtract))
            link(nc.vector.tensor_scalar(over[:], over[:], -float(ROW * GROWS), None, ALU.is_lt))
            link(nc.vector.tensor_reduce(faults[0:TILES, 2:3], over[:], axis=AX.X, op=ALU.add))
            marks["faults"] = count[0]
            dve.wait_ge(pe_done, 4)
            link(nc.vector.tensor_scalar(irregular[:], faults_ps[:, 0:1], 1.0, None, ALU.min))

        block.vector(vector)

        @block.tensor
        def _(pe):
            per = CHUNKS // GRP
            for k in range(per):
                if k % (per // 5) == 0:
                    pe.wait_ge(dve_done, marks["one", k // (per // 5)])
                ins = nc.tensor.matmul(pairs_ps[:], one_hi[:, GRP * k:GRP * (k + 1), :].rearrange("p j h -> p (j h)"),
                                       one_lo[:, GRP * k:GRP * (k + 1), :].rearrange("p j h -> p (j h)"),
                                       start=(k == 0), stop=(k == per - 1))
            ins.then_inc(pe_done, 1)
            pe.wait_ge(dve_done, marks["pairs"])
            nc.tensor.matmul(hist_ps[:], fold[:], pairs[:], start=True, stop=True).then_inc(pe_done, 1)
            pe.wait_ge(dve_done, marks["upto"])
            nc.tensor.matmul(off_ps[:, 0:1], before[:], upto[:, WPT - 1:WPT], start=True, stop=True).then_inc(pe_done, 1)
            pe.wait_ge(dve_done, marks["faults"])
            for k, n in enumerate((P, EGROUPS // EG, TILES)):
                ins = nc.tensor.matmul(faults_ps[:, 0:1], faults[0:n, k:k + 1], ones[0:n, 0:1], start=(k == 0), stop=(k == 2))
            ins.then_inc(pe_done, 1)

        @block.sync
        def _(sp):
            sp.dma_start(dst_i[:, 0:CHUNKS], T["dst"].rearrange("(p c) -> p c", p=P)).then_inc(dst_in, 16)
            sp.dma_start(X[:], T["x"].rearrange("(t p) f -> p t f", p=P)).then_inc(x_in, 16)
            for k, name in enumerate(("src", "dst", "edge_weight")):
                column = table[0:ROWS, k * ROW:(k + 1) * ROW]
                if name == "edge_weight":
                    column = column.bitcast(F32)
                sp.dma_start(column, T[name].rearrange("(r e) -> r e", e=ROW)).then_inc(table_done, 16)
            sp.wait_ge(pool_done, 11)
            with nc.allow_non_contiguous_dma(reason="an edge a row, and two of every edge group"):
                sp.dma_start(dst_i[0:P - 1, CHUNKS:], T["dst"].rearrange("(p c) -> p c", p=P)[1:P, 0:1]).then_inc(ends_in, 16)
                grouped = T["dst"].rearrange("(p k r) -> p k r", k=EG, r=EG * P)
                sp.dma_start(ends_i[:, 0, :], grouped[:, :, 0]).then_inc(ends_in, 16)
                sp.dma_start(ends_i[:, 1, :], grouped[:, :, EG * P - 1]).then_inc(ends_in, 16)
            sp.dma_start(table[ROWS:ROWS + GROWS, :], pad[:]).then_inc(table_done, 16)
            sp.wait_ge(table_done, 64)
            sp.wait_ge(dve_done, marks["starts"])
            sp.dma_start(starts.rearrange("(h m) -> h m", m=WPT), first_i[:]).then_inc(starts_done, 16)
            sp.wait_ge(starts_done, 16)
            sp.wait_ge(x_in, 16)

    return used


TURNED = ("W0", "Ws0", "Ws1", "Wn0", "Wn1", "Wa")


def fetch_weights(sp, T, W, raw, parts, raw_in, rest_in):
    sources = (T["L0_gnn_W"], T["L2_gnn_W_self"][0], T["L2_gnn_W_self"][1], T["L2_gnn_W_neigh"][0],
               T["L2_gnn_W_neigh"][1], T["L2_gnn_W_agg"])
    for k, w in enumerate(sources):
        sp.dma_start(raw[:, k, :], w).then_inc(raw_in, 16)
    for k, name in enumerate(("Wq", "Wk", "Wv")):
        sp.dma_start(W[name][:].rearrange("i (h o) -> i h o", h=HEADS),
                     T["L1_gnn_" + name].rearrange("h i o -> i h o")).then_inc(rest_in, 16)
    sp.dma_start(W["W3"][:], T["L3_gnn_W"]).then_inc(rest_in, 16)
    rows = [T["L2_gnn_b_self"], T["L2_gnn_b_neigh"], T["L2_gnn_layer_bias"]]
    for k, b in enumerate(rows):
        sp.dma_start(parts[0:1, 2 * k:2 * k + 2, :], b.rearrange("(o l) d -> o l d", o=1)).then_inc(rest_in, 16)
    for k, name in enumerate(("L0_gnn_b", "L2_gnn_b_agg", "L3_gnn_b")):
        sp.dma_start(W["bias"][0:1, k, :], T[name].rearrange("(o d) -> o d", o=1)).then_inc(rest_in, 16)


def turn_weights(nc, pe, raw, ident, flipped, raw_in, turned):
    pe.wait_ge(raw_in, 16 * len(TURNED))
    for k in range(len(TURNED)):
        ins = nc.tensor.transpose(flipped[:, k // 4, (k % 4) * D:(k % 4 + 1) * D], raw[:, k, :], ident[:])
    ins.then_inc(turned, 1)


def keep_weights(nc, dve, W, parts, flipped, rest_in, turned, moved):
    dve.wait_ge(turned, 1)
    for k, name in enumerate(TURNED):
        nc.vector.tensor_copy(W[name][:], flipped[:, k // 4, (k % 4) * D:(k % 4 + 1) * D])
    dve.wait_ge(rest_in, 16 * 10)
    nc.vector.tensor_tensor(parts[0:1, 0:2, :], parts[0:1, 0:2, :], parts[0:1, 2:4, :], ALU.add).then_inc(moved, 1)
    dve.wait_ge(moved, 1)
    nc.vector.tensor_tensor(W["bias"][0:1, 3:5, :], parts[0:1, 0:2, :], parts[0:1, 4:6, :], ALU.add)


def edge_slots(nc, T, W, table, starts, X, H, norm, ident, src_hi, src_lo, dst_in, weight, used_before):
    KINDS = 3
    used = []
    with ExitStack() as c:
        e = c.enter_context
        sem = recorded_semaphores(nc, e, used)
        gathered = [sem(f"gathered{b}") for b in range(BLOCKS)]
        row0 = e(nc.sbuf_tensor(unique("row0"), [P, BLOCKS], I32))
        row_f = e(nc.sbuf_tensor(unique("row_f"), [P, BLOCKS], F32))
        off_i = e(nc.sbuf_tensor(unique("off_i"), [P, GROWS], I32))
        off_f = e(nc.sbuf_tensor(unique("off_f"), [P, GROWS], F32))
        index = e(nc.sbuf_tensor(unique("index"), [P, GROWS, BLOCKS], I32))
        rows = e(nc.sbuf_tensor(unique("rows"), [P, BLOCKS, GROWS, KINDS * ROW], I32))
        flat = e(nc.sbuf_tensor(unique("flat"), [P, BLOCKS, KINDS, GROWS * ROW], F32))
        win_i = e(nc.sbuf_tensor(unique("win_i"), [P, 2 * WINDOWS], I32))
        src_f = e(nc.sbuf_tensor(unique("src_f"), [P, 2 * WINDOWS], F32))
        turned = e(nc.psum_tensor(unique("turned"), [P, 2, 512], F32))
        raw = e(nc.sbuf_tensor(unique("raw"), [D, len(TURNED), D], F32))
        parts = e(nc.sbuf_tensor(unique("parts"), [1, 6, D], F32))
        flipped_w = e(nc.psum_tensor(unique("flipped_w"), [D, 2, 512], F32))
        raw_in = sem("raw_in")
        rest_in = sem("rest_in")
        w_turned = sem("w_turned")
        w_moved = sem("w_moved")
        var_ready = sem("var_ready")
        std_ready = sem("std_ready")
        inv_ready = sem("inv_ready")
        h_ready = sem("h_ready")
        loaded = sem("loaded")
        pool_ready = sem("pool_ready")
        index_ready = sem("index_ready")
        flat_ready = sem("flat_ready")
        turn_done = sem("turn_done")
        copied = sem("copied")
        slots_done = sem("slots_done")
        block = e(nc.Block())

        @block.sync
        def _(sp):
            with nc.allow_non_contiguous_dma(reason="one start a partition"):
                sp.dma_start(row0[:], starts.rearrange("(b p) -> p b", p=P)).then_inc(loaded, 16)
            fetch_weights(sp, T, W, raw, parts, raw_in, rest_in)

        @block.gpsimd
        def _(pool):
            clear_used(pool, used_before)
            nc.gpsimd.iota(off_i[:], [[1, GROWS]], base=0, channel_multiplier=0).then_inc(pool_ready, 1)
            nc.gpsimd.iota(win_i[:].rearrange("p (w h) -> p w h", h=2), [[WIN, WINDOWS], [0, 2]], base=0,
                           channel_multiplier=0).then_inc(pool_ready, 1)
            pool.wait_ge(index_ready, 1)
            for b in range(BLOCKS):
                for j in range(GROWS):
                    nc.gpsimd.indirect_dma_start(rows[:, b, j, :], None, table,
                                                 bass.IndirectOffsetOnAxis(ap=index[:, j, b:b + 1], axis=0)
                                                 ).then_inc(gathered[b], 16)

        @block.vector
        def _(dve):
            link = chained(dve, slots_done)
            dve.wait_ge(pool_ready, 2)
            link(nc.vector.tensor_copy(off_f[:], off_i[:]))
            dve.wait_ge(loaded, 16)
            link(nc.vector.tensor_copy(row_f[:], row0[:]))
            nc.vector.tensor_tensor(index[:], row_f[:].unsqueeze(1).broadcast_to([P, GROWS, BLOCKS]),
                                    off_f[:].unsqueeze(2).broadcast_to([P, GROWS, BLOCKS]),
                                    ALU.add).then_inc(index_ready, 1)
            layer_norm_relu(nc, dve, link, X, H, norm, var_ready, std_ready, inv_ready)
            keep_weights(nc, dve, W, parts, flipped_w, rest_in, w_turned, w_moved)
            for b in range(BLOCKS):
                dve.wait_ge(gathered[b], 16 * GROWS)
                for k in range(KINDS):
                    part = rows[:, b, :, k * ROW:(k + 1) * ROW]
                    if k == 2:
                        part = part.bitcast(F32)
                    nc.vector.tensor_copy(flat[:, b, k, :].rearrange("p (j e) -> p j e", e=ROW),
                                          part).then_inc(flat_ready, 1)
            dve.wait_ge(copied, 3 * 2 * BLOCKS)
            floor_div(nc, link, src_hi[:], src_f[:], P)
            link(nc.vector.tensor_scalar(src_hi[:], src_hi[:], float(P), None, ALU.mult))
            link(nc.vector.tensor_tensor(src_lo[:], src_f[:], src_hi[:], ALU.subtract))
            link(nc.vector.tensor_copy(src_f[:], win_i[:]))
            link(nc.vector.tensor_tensor(dst_in[:], dst_in[:], src_f[:], ALU.subtract))

        @block.tensor
        def _(pe):
            turn_weights(nc, pe, raw, ident, flipped_w, raw_in, w_turned)
            for b in range(BLOCKS):
                pe.wait_ge(flat_ready, KINDS * (b + 1))
                for h in range(2):
                    n = 2 * b + h
                    if n >= 2:
                        pe.wait_ge(copied, 3 * (n - 1))
                    for k in range(KINDS):
                        ins = nc.tensor.transpose(turned[:, h, k * P:(k + 1) * P], flat[:, b, k, h * P:(h + 1) * P],
                                                  ident[0:P, 0:P])
                    ins.then_inc(turn_done, 1)

        @block.scalar
        def _(act):
            scale_rows(nc, act, H, norm, var_ready, std_ready, inv_ready, h_ready)
            for b in range(BLOCKS):
                for h in range(2):
                    act.wait_ge(turn_done, 2 * b + h + 1)
                    for k, out in enumerate((src_f, dst_in, weight)):
                        out = out[:].rearrange("p (w h) -> p h w", h=2)[:, h, b * P:(b + 1) * P]
                        nc.scalar.copy(out, turned[:, h, k * P:(k + 1) * P]).then_inc(copied, 1)

    return used


def adjacency(nc, counts, countsT, weightsT, ident, src_hi, src_lo, dst_in, weight, iota, iota_tile,
              out_degree, in_parts, used_before):
    PER = 3 + 2 * NGRP
    G = 2 * GRP
    WID = 2 * WIN
    ROUNDS = (TILES + 3) // 4
    after = [[0, 1], [2, 3], [4], [5], [6]]
    assert sum(after, []) == list(range(ROUNDS)) and len(after) == NGRP
    with ExitStack() as c:
        e = c.enter_context
        tile_hot = e(nc.sbuf_tensor(unique("tile_hot"), [P, 2, 2 * WPT, TILES], F32))
        dst_hot = e(nc.sbuf_tensor(unique("dst_hot"), [P, 2, 2 * WPT, WID], F32))
        lo_hot = e(nc.sbuf_tensor(unique("lo_hot"), [P, 2, G, P], F32))
        lo_hot_short = e(nc.sbuf_tensor(unique("lo_hot_short"), [P, 2, G, P], BF16))
        pair_hot = e(nc.sbuf_tensor(unique("pair_hot"), [P, 2, G, P], BF16))
        pair_weight = e(nc.sbuf_tensor(unique("pair_weight"), [P, 2, G, P], F32))
        cT = e(nc.sbuf_tensor(unique("cT"), [P, 2, N], F32))
        wT = e(nc.sbuf_tensor(unique("wT"), [P, 2, N], F32))
        cc = e(nc.sbuf_tensor(unique("cc"), [P, 2, N], F32))
        degree_parts = e(nc.sbuf_tensor(unique("degree_parts"), [P, TILES, TILES], F32))
        built = [e(nc.psum_tensor(unique(f"built{i}"), [P, 3 * 512], F32)) for i in range(2)]
        flipped = e(nc.psum_tensor(unique("flipped"), [P, 2, 512], F32))
        made = e(nc.semaphore(unique("made")))
        weighed = e(nc.semaphore(unique("pairs_weighed")))
        pool_go = e(nc.semaphore(unique("pool_go")))
        grouped = e(nc.semaphore(unique("grouped")))
        copied = e(nc.semaphore(unique("cT_copied")))
        turned = e(nc.semaphore(unique("tile_turned")))
        straight = e(nc.semaphore(unique("straight")))
        shortened = e(nc.semaphore(unique("shortened")))
        summed = e(nc.semaphore(unique("summed")))
        stored = [e(nc.semaphore(unique(f"stored{u}"))) for u in range(2)]
        turned_stored = [e(nc.semaphore(unique(f"turned_stored{u}"))) for u in range(2)]
        last_stored = e(nc.semaphore(unique("last_stored")))
        free = e(nc.semaphore(unique("tiles_free")))
        cc_free = e(nc.semaphore(unique("cc_free")))
        block = e(nc.Block())

        def one_behind(eng, body):
            body(0, 0, False)
            with eng.Fori(0, (TILES - 1) // 2) as i:
                body(i * 2 + 1, 1, True)
                body(i * 2 + 2, 0, True)

        @block.vector
        def _(dve):
            dve.sem_inc(summed, 2)

            def reduce_degrees(t, u):
                dve.wait_ge(copied, t * (2 * NGRP) + (4 + 2 * NGRP))
                nc.vector.tensor_reduce(row_of(degree_parts, t), cT[:, u, :].rearrange("p (a d) -> p a d", d=P),
                                        axis=AX.X, op=ALU.add).then_inc(summed, 1)

            def tile(t, u, before):
                halves = bass.ds(t * (2 * WPT), 2 * WPT)
                nc.vector.tensor_tensor(tile_hot[:, u], src_hi[:, halves].unsqueeze(2).broadcast_to([P, 2 * WPT, TILES]),
                                        iota_tile[:].unsqueeze(1).broadcast_to([P, 2 * WPT, TILES]),
                                        ALU.is_equal).then_inc(made, 1)
                nc.vector.tensor_tensor(dst_hot[:, u, :, 0:WIN],
                                        dst_in[:, halves].unsqueeze(2).broadcast_to([P, 2 * WPT, WIN]),
                                        iota[:, 0:WIN].unsqueeze(1).broadcast_to([P, 2 * WPT, WIN]),
                                        ALU.is_equal).then_inc(made, 1)
                dve.wait_ge(made, t * PER + 2)
                nc.vector.tensor_tensor(dst_hot[:, u, :, WIN:WID], dst_hot[:, u, :, 0:WIN],
                                        weight[:, halves].unsqueeze(2).broadcast_to([P, 2 * WPT, WIN]),
                                        ALU.mult).then_inc(made, 1)
                for q in range(NGRP):
                    b = (NGRP * u + q) % 2
                    dve.wait_ge(grouped, t * NGRP + (q + 1))
                    nc.vector.tensor_tensor(lo_hot[:, b],
                                            src_lo[:, bass.ds(t * (2 * WPT) + q * G, G)].unsqueeze(2).broadcast_to([P, G, P]),
                                            iota[:].unsqueeze(1).broadcast_to([P, G, P]),
                                            ALU.is_equal).then_inc(made, 1)
                    part = slice(q * G, (q + 1) * G)
                    nc.vector.tensor_tensor(pair_hot[:, b].rearrange("p g (a k) -> p g a k", k=WIN),
                                            tile_hot[:, u, part].unsqueeze(3).broadcast_to([P, G, TILES, WIN]),
                                            dst_hot[:, u, part, 0:WIN].unsqueeze(2).broadcast_to([P, G, TILES, WIN]),
                                            ALU.mult).then_inc(made, 1)
                    if before and q == 2:
                        reduce_degrees(t - 1, 1 - u)

            one_behind(dve, tile)
            reduce_degrees(TILES - 1, 0)
            dve.wait_ge(summed, 2 + TILES)
            nc.vector.tensor_reduce(out_degree[:], degree_parts[:].rearrange("p t a -> p a t"), axis=AX.X, op=ALU.add)

        @block.gpsimd
        def _(pool):
            clear_used(pool, used_before)

            def tile(t, u, before):
                for q in range(NGRP):
                    b = (NGRP * u + q) % 2
                    pool.wait_ge(made, t * PER + 3)
                    pool.wait_ge(grouped, t * NGRP + (q + 1))
                    pool.sem_inc(pool_go, 1)
                    part = slice(q * G, (q + 1) * G)
                    nc.gpsimd.tensor_tensor(pair_weight[:, b].rearrange("p g (a k) -> p g a k", k=WIN),
                                            tile_hot[:, u, part].unsqueeze(3).broadcast_to([P, G, TILES, WIN]),
                                            dst_hot[:, u, part, WIN:WID].unsqueeze(2).broadcast_to([P, G, TILES, WIN]),
                                            ALU.mult).then_inc(weighed, 1)

            one_behind(pool, tile)

        @block.tensor
        def _(pe):
            pe.sem_inc(grouped, 2)

            def turn_round(t, u, r):
                b = (ROUNDS * u + r) % 2
                if r == 0:
                    pe.wait_ge(copied, t * (2 * NGRP) + (4 + 2 * NGRP))
                pe.wait_ge(straight, t * ROUNDS + (r + 1))
                for a in range(4 * r, min(4 * r + 4, TILES)):
                    ins = nc.tensor.transpose(flipped[:, b, (a % 4) * P:(a % 4 + 1) * P],
                                              cT[:, u, a * P:(a + 1) * P], ident[0:P, 0:P])
                ins.then_inc(turned, 1)

            def tile(t, u, before):
                for q in range(NGRP):
                    b = (NGRP * u + q) % 2
                    pe.wait_ge(made, t * PER + (3 + 2 * (q + 1)))
                    pe.wait_ge(weighed, t * NGRP + (q + 1))
                    pe.wait_ge(copied, t * (2 * NGRP) + 2 * (q + 1))
                    for w in range(GRP):
                        for h in range(2):
                            nc.tensor.matmul(built[b][:, 256 * w + P:256 * w + 2 * P], lo_hot[:, b, 2 * w + h],
                                             pair_weight[:, b, 2 * w + h], start=(h == 0), stop=(h == 1))
                    pe.wait_ge(shortened, t * NGRP + (q + 1))
                    for w in range(GRP):
                        for h in range(2):
                            ins = nc.tensor.matmul(built[b][:, 256 * w:256 * w + P], lo_hot_short[:, b, 2 * w + h],
                                                   pair_hot[:, b, 2 * w + h], start=(h == 0), stop=(h == 1))
                    ins.then_inc(grouped, 1)
                    if before:
                        for r in after[q]:
                            turn_round(t - 1, 1 - u, r)

            one_behind(pe, tile)
            for r in range(ROUNDS):
                turn_round(TILES - 1, 0, r)

        @block.scalar
        def _(act):
            act.sem_inc(copied, 4)
            act.sem_inc(straight, 2)

            def copy_round(t, u, r):
                b = (ROUNDS * u + r) % 2
                n = min(4, TILES - 4 * r) * P
                if r == 0:
                    act.wait_ge(cc_free, t + 1)
                act.wait_ge(turned, t * ROUNDS + (r + 1))
                nc.scalar.activation(cc[:, u, 4 * P * r:4 * P * r + n], flipped[:, b, 0:n], ACT.Copy,
                                     accum_out=in_parts[:, bass.ds(t, 1), r:r + 1].rearrange("p o f -> p (o f)")
                                     ).then_inc(straight, 1)

            def shorten(t, u, q):
                b = (NGRP * u + q) % 2
                act.wait_ge(made, t * PER + (4 + 2 * q))
                act.wait_ge(grouped, t * NGRP + (q + 1))
                nc.scalar.copy(lo_hot_short[:, b], lo_hot[:, b]).then_inc(shortened, 1)

            def tile(t, u, before):
                act.wait_ge(free, t + 1)
                act.wait_ge(summed, t + 1)
                for q in range(NGRP):
                    b = (NGRP * u + q) % 2
                    shorten(t, u, q)
                    act.wait_ge(grouped, t * NGRP + (q + 3))
                    seen = built[b][:, 0:256 * GRP].rearrange("p (w k) -> p w k", k=256)[:, :, 0:TILES * WID]
                    seen = seen.rearrange("p w (c a k) -> p w c a k", c=2, k=WIN)
                    for c, out in enumerate((cT, wT)):
                        o = out[:, u, :].rearrange("p (a w k) -> p w a k", w=WPT, k=WIN)[:, q * GRP:(q + 1) * GRP]
                        nc.scalar.copy(o, seen[:, :, c]).then_inc(copied, 1)
                    if before:
                        for r in after[q]:
                            copy_round(t - 1, 1 - u, r)

            one_behind(act, tile)
            for r in range(ROUNDS):
                copy_round(TILES - 1, 0, r)

        @block.sync
        def _(sp):
            sp.sem_inc(free, 2)
            sp.sem_inc(cc_free, 2)
            row = lambda d, t: d[bass.ds(t, 1)].rearrange("o p n -> (o p) n")

            def store_turned(t, u):
                sp.wait_ge(straight, t * ROUNDS + (2 + ROUNDS))
                sp.dma_start(row(counts, t), cc[:, u, :]).then_inc(turned_stored[u], 16)

            def landed(t, u):
                sp.wait_ge(stored[u], (t - u) * 16 + 32)
                sp.sem_inc(free, 1)

            def turned_landed(t, u):
                sp.wait_ge(turned_stored[u], (t - u) * 8 + 16)
                sp.sem_inc(cc_free, 1)

            def tile(t, u, before):
                if before:
                    landed(t - 1, 1 - u)
                    store_turned(t - 1, 1 - u)
                sp.wait_ge(copied, t * (2 * NGRP) + (4 + 2 * NGRP))
                sp.dma_start(row(countsT, t), cT[:, u, :]).then_inc(stored[u], 16)
                sp.dma_start(row(weightsT, t), wT[:, u, :]).then_inc(stored[u], 16)
                if before:
                    turned_landed(t - 1, 1 - u)

            one_behind(sp, tile)
            landed(TILES - 1, 0)
            for r, a0, n in quads():
                sp.wait_ge(straight, (TILES - 1) * ROUNDS + r + 3)
                sp.dma_start(counts[TILES - 1][:, a0 * P:(a0 + n) * P], cc[:, 0, a0 * P:(a0 + n) * P]).then_inc(last_stored, 16)
            sp.wait_ge(last_stored, 16 * ROUNDS)


def general_adjacency(nc, T, counts, countsT, weightsT, iota, iota_tile, out_degree, in_parts):
    STEP = 11
    STEPS = CHUNKS // STEP
    with ExitStack() as c:
        e = c.enter_context
        src_i = e(nc.sbuf_tensor(unique("src_i"), [P, CHUNKS], I32))
        dst_i = e(nc.sbuf_tensor(unique("dst_i"), [P, CHUNKS], I32))
        wgt = e(nc.sbuf_tensor(unique("wgt"), [P, CHUNKS], F32))
        src_f = e(nc.sbuf_tensor(unique("src_f"), [P, CHUNKS], F32))
        dst_f = e(nc.sbuf_tensor(unique("dst_f"), [P, CHUNKS], F32))
        src_rel = e(nc.sbuf_tensor(unique("src_rel"), [P, CHUNKS], F32))
        dst_rel = e(nc.sbuf_tensor(unique("dst_rel"), [P, CHUNKS], F32))
        src_hot = e(nc.sbuf_tensor(unique("src_hot"), [P, STEP, P], F32))
        dst_hot = e(nc.sbuf_tensor(unique("dst_hot"), [P, STEP, 2, P], F32))
        made_blocks = e(nc.sbuf_tensor(unique("made_blocks"), [P, 3, P], F32))
        sums = e(nc.sbuf_tensor(unique("sums"), [P, 2], F32))
        turned_ps = e(nc.psum_tensor(unique("turned_ps"), [P, 2 * P], F32))
        counts_ps = e(nc.psum_tensor(unique("counts_ps"), [P, P], F32))
        loaded = e(nc.semaphore(unique("edges_loaded")))
        made = e(nc.semaphore(unique("hot_made")))
        multiplied = e(nc.semaphore(unique("multiplied")))
        copied = e(nc.semaphore(unique("blocks_copied")))
        stored = e(nc.semaphore(unique("blocks_stored")))
        nc.all_engine_barrier()
        with nc.Block() as block:
            @block.sync
            def _(sp):
                for out, name in ((src_i, "src"), (dst_i, "dst"), (wgt, "edge_weight")):
                    sp.dma_start(out[:], T[name].rearrange("(p c) -> p c", p=P)).then_inc(loaded, 16)

            @block.vector
            def _(dve):
                dve.wait_ge(loaded, 48)
                nc.vector.tensor_copy(src_f[:], src_i[:])
                nc.vector.tensor_copy(dst_f[:], dst_i[:])
                nc.vector.memset(out_degree[:], 0.0)
                nc.vector.memset(in_parts[:], 0.0)

        with nc.Fori(0, TILES) as t:
            with nc.Fori(0, TILES) as a:
                with nc.Block() as block:
                    @block.vector
                    def _(dve):
                        nc.vector.tensor_scalar(src_rel[:], src_f[:], iota_tile[:, bass.ds(a, 1)], None,
                                                ALU.subtract).then_inc(made, 1)
                        nc.vector.tensor_scalar(dst_rel[:], dst_f[:], iota_tile[:, bass.ds(t, 1)], None,
                                                ALU.subtract).then_inc(made, 1)
                        dve.wait_ge(made, 2)

                        def step(k):
                            here = bass.ds(k * STEP, STEP)
                            spread = lambda x: x.unsqueeze(2).broadcast_to([P, STEP, P])
                            each = iota[:].unsqueeze(1).broadcast_to([P, STEP, P])
                            nc.vector.tensor_tensor(src_hot[:], spread(src_rel[:, here]), each, ALU.is_equal)
                            nc.vector.tensor_tensor(dst_hot[:, :, 0, :], spread(dst_rel[:, here]), each,
                                                    ALU.is_equal).then_inc(made, 1)
                            dve.wait_ge(made, k * 2 + 3)
                            nc.vector.tensor_tensor(dst_hot[:, :, 1, :], spread(wgt[:, here]), dst_hot[:, :, 0, :],
                                                    ALU.mult).then_inc(made, 1)
                            dve.wait_ge(multiplied, k + 1)

                        with dve.Fori(0, STEPS) as k:
                            step(k)
                        nc.vector.tensor_copy(made_blocks[:, 0:2, :], turned_ps[:].rearrange("p (c d) -> p c d", c=2))
                        nc.vector.tensor_copy(made_blocks[:, 2, :], counts_ps[:]).then_inc(copied, 1)
                        nc.vector.tensor_reduce(sums[:, 0:1], turned_ps[:, 0:P], axis=AX.X, op=ALU.add)
                        nc.vector.tensor_reduce(sums[:, 1:2], counts_ps[:], axis=AX.X, op=ALU.add).then_inc(copied, 1)
                        dve.wait_ge(copied, 2)
                        nc.vector.tensor_tensor(out_degree[:, bass.ds(a, 1)], out_degree[:, bass.ds(a, 1)],
                                                sums[:, 0:1], ALU.add)
                        into = in_parts[:, bass.ds(t, 1), 0:1].rearrange("p o f -> p (o f)")
                        nc.vector.tensor_tensor(into, into, sums[:, 1:2], ALU.add)

                    @block.tensor
                    def _(pe):
                        def step(k, first=False, last=False):
                            pe.wait_ge(made, k * 2 + 4)
                            for j in range(STEP):
                                edge = dict(start=first and j == 0, stop=last and j == STEP - 1)
                                nc.tensor.matmul(turned_ps[:], src_hot[:, j, :], dst_hot[:, j].rearrange("p c d -> p (c d)"), **edge)
                                ins = nc.tensor.matmul(counts_ps[:], dst_hot[:, j, 0, :], src_hot[:, j, :], **edge)
                            ins.then_inc(multiplied, 1)

                        step(0, first=True)
                        with pe.Fori(1, STEPS - 1) as k:
                            step(k)
                        step(STEPS - 1, last=True)

                    @block.sync
                    def _(sp):
                        sp.wait_ge(copied, 1)
                        with nc.allow_non_contiguous_dma(reason="a block of a wider array"):
                            for k, out in enumerate((countsT, weightsT, counts)):
                                sp.dma_start(out[bass.ds(t, 1), :, bass.ds(a * P, P)].rearrange("o p n -> (o p) n"),
                                             made_blocks[:, k, :]).then_inc(stored, 16)
                        sp.wait_ge(stored, 48)

                clear_semaphores(nc, (made, multiplied, copied, stored))


def clear_semaphores(nc, semaphores):
    with nc.Block() as block:
        @block.gpsimd
        def _(pool):
            for s in semaphores:
                pool.sem_clear(s)


def in_turns(eng, body, k, n=TILES):
    assert n % k == 0
    with eng.Fori(0, n // k) as i:
        for u in range(k):
            body(i * k + u, u)


def turn_tiles(nc, pe, X, ident, flipped, turned, moved, before):
    for r, a0, n in quads():
        if r >= 2:
            pe.wait_ge(moved, before + r - 1)
        for a in range(a0, a0 + n):
            ins = nc.tensor.transpose(flipped[:, r % 2, (a - a0) * P:(a - a0 + 1) * P], X[:, a, :], ident[0:P, 0:P])
        ins.then_inc(turned, 1)


def move_tiles(nc, act, XT, flipped, turned, moved, before):
    for r, a0, n in quads():
        act.wait_ge(turned, before + r + 1)
        nc.scalar.copy(XT[:, a0 * P:(a0 + n) * P], flipped[:, r % 2, 0:n * P]).then_inc(moved, 1)


def gcn_layer(nc, counts, X, H, W, ones, out_degree):
    BUFS = 5
    with ExitStack() as c:
        e = c.enter_context
        block_in = e(nc.sbuf_tensor(unique("counts_in"), [P, BUFS, N], F32))
        scaled = e(nc.sbuf_tensor(unique("scaled"), [P, BUFS, D], F32))
        inv = e(nc.sbuf_tensor(unique("inv"), [P, TILES], F32))
        some = e(nc.sbuf_tensor(unique("some"), [P, TILES], F32))
        aggT = e(nc.sbuf_tensor(unique("aggT"), [D, N], F32))
        agg = e(nc.psum_tensor(unique("agg"), [D, 7, 512], F32))
        last = e(nc.psum_tensor(unique("last_bank"), [P, 512], F32))
        loaded = [e(nc.semaphore(unique(f"loaded{u}"))) for u in range(BUFS)]
        used = e(nc.semaphore(unique("used")))
        scaled_done = e(nc.semaphore(unique("scaled_done")))
        bias_done = e(nc.semaphore(unique("bias_done")))
        agg_moved = e(nc.semaphore(unique("agg_moved")))
        inv_done = e(nc.semaphore(unique("inv_done")))
        root_ready = e(nc.semaphore(unique("root_ready")))
        root_done = e(nc.semaphore(unique("root_done")))
        lin_done = e(nc.semaphore(unique("lin_done")))
        lin_added = e(nc.semaphore(unique("lin_added")))
        block = e(nc.Block())

        @block.sync
        def _(sp):
            def tile(t, u):
                sp.wait_ge(used, t + 1)
                sp.dma_start(block_in[:, u, :], counts[bass.ds(t, 1)].rearrange("o p n -> (o p) n")).then_inc(loaded[u], 16)

            in_turns(sp, tile, BUFS)

        @block.scalar
        def _(act):
            act.wait_ge(root_ready, 1)
            nc.scalar.activation(inv[:], inv[:], ACT.Sqrt).then_inc(root_done, 1)
            act.wait_ge(used, BUFS + TILES)
            for k in range(7):
                n = min(512, N - 512 * k)
                if k % 2:
                    nc.scalar.copy(aggT[:, 512 * k:512 * k + n], agg[:, k, 0:n]).then_inc(agg_moved, 1)

        @block.vector
        def _(dve):
            link = chained(dve, inv_done)
            link(nc.vector.tensor_scalar(some[:], out_degree[:], 0.0, None, ALU.is_gt))
            nc.vector.tensor_scalar(inv[:], out_degree[:], 1.0, None, ALU.max).then_inc(root_ready, 1)
            dve.wait_ge(root_done, 1)
            link(nc.vector.reciprocal(inv[:], inv[:]))
            link(nc.vector.tensor_tensor(inv[:], inv[:], some[:], ALU.mult))

            def tile(t, u):
                dve.wait_ge(used, t + 1)
                nc.vector.tensor_scalar(scaled[:, u, :], row_of(H, t), inv[:, bass.ds(t, 1)], None,
                                        ALU.mult).then_inc(scaled_done, 1)

            in_turns(dve, tile, BUFS)
            dve.wait_ge(bias_done, 1)
            link(nc.vector.tensor_tensor(X[:], X[:], last[:, 0:D].unsqueeze(1).broadcast_to([P, TILES, D]), ALU.add))
            dve.wait_ge(used, BUFS + TILES)
            for k in range(0, 7, 2):
                n = min(512, N - 512 * k)
                nc.vector.tensor_copy(aggT[:, 512 * k:512 * k + n], agg[:, k, 0:n]).then_inc(agg_moved, 1)
            for r, a0, n in quads():
                dve.wait_ge(lin_done, r + 1)
                for a in range(a0, a0 + n):
                    ins = nc.vector.scalar_tensor_tensor(X[:, a, :], agg[0:P, r % 2, (a - a0) * D:(a - a0 + 1) * D],
                                                         inv[:, a:a + 1], X[:, a, :], ALU.mult, ALU.add)
                ins.then_inc(lin_added, 1)

        @block.tensor
        def _(pe):
            pe.sem_inc(used, BUFS)
            nc.tensor.matmul(last[:, 0:D], ones[0:1, 0:P], W["bias"][0:1, 0, :], start=True, stop=True).then_inc(bias_done, 1)

            def turn(i, first=False, last_turn=False):
                for u in range(BUFS):
                    pe.wait_ge(scaled_done, i * BUFS + (u + 1))
                    pe.wait_ge(loaded[u], i * 16 + 16)
                    for k in range(7):
                        n = min(512, N - 512 * k)
                        ins = nc.tensor.matmul(agg[:, k, 0:n], scaled[:, u, :], block_in[:, u, 512 * k:512 * k + n],
                                               start=(first and u == 0), stop=(last_turn and u == BUFS - 1))
                    ins.then_inc(used, 1)

            turn(0, first=True)
            with pe.Fori(1, TILES // BUFS - 1) as i:
                turn(i)
            turn(TILES // BUFS - 1, last_turn=True)
            pe.wait_ge(agg_moved, 7)
            for r, a0, n in quads():
                if r >= 2:
                    pe.wait_ge(lin_added, r - 1)
                for a in range(a0, a0 + n):
                    ins = nc.tensor.matmul(agg[0:P, r % 2, (a - a0) * D:(a - a0 + 1) * D], aggT[:, a * P:(a + 1) * P],
                                           W["W0"][:], start=True, stop=True)
                ins.then_inc(lin_done, 1)


def normalize(nc, X, H, HT, norm, ident):
    with ExitStack() as c:
        e = c.enter_context
        flipped = e(nc.psum_tensor(unique("flipped_h"), [D, 4, 512], F32))
        normed = e(nc.semaphore(unique("normed")))
        var_ready = e(nc.semaphore(unique("var_ready")))
        std_ready = e(nc.semaphore(unique("std_ready")))
        inv_ready = e(nc.semaphore(unique("inv_ready")))
        h_ready = e(nc.semaphore(unique("h_ready")))
        turned = e(nc.semaphore(unique("h_turned")))
        moved = e(nc.semaphore(unique("h_moved")))
        block = e(nc.Block())

        @block.vector
        def _(dve):
            layer_norm_relu(nc, dve, chained(dve, normed), X, H, norm, var_ready, std_ready, inv_ready)
            for r, a0, n in quads():
                dve.wait_ge(turned, r + 1)
                nc.vector.tensor_copy(HT[:, a0 * P:(a0 + n) * P], flipped[:, r % 4, 0:n * P]).then_inc(moved, 1)

        @block.scalar
        def _(act):
            scale_rows(nc, act, H, norm, var_ready, std_ready, inv_ready, h_ready)

        @block.tensor
        def _(pe):
            for r, a0, n in quads():
                pe.wait_ge(h_ready, r + 1)
                if r >= 4:
                    pe.wait_ge(moved, r - 3)
                for a in range(a0, a0 + n):
                    ins = nc.tensor.transpose(flipped[:, r % 4, (a - a0) * P:(a - a0 + 1) * P], H[:, a, :], ident[0:P, 0:P])
                ins.then_inc(turned, 1)


def turn(nc, Y, YT, ident):
    with ExitStack() as c:
        e = c.enter_context
        flipped = e(nc.psum_tensor(unique("flipped_y"), [D, 2, 512], F32))
        turned = e(nc.semaphore(unique("y_turned")))
        moved = e(nc.semaphore(unique("y_moved")))
        block = e(nc.Block())

        @block.scalar
        def _(act):
            move_tiles(nc, act, YT, flipped, turned, moved, 0)

        @block.tensor
        def _(pe):
            turn_tiles(nc, pe, Y, ident, flipped, turned, moved, 0)


def project(nc, HT, W, QA, QB, KA, KB, V):
    CH = 500
    pieces = [(k, CH * k, min(CH, N - CH * k)) for k in range((N + CH - 1) // CH)]
    n = len(pieces)
    with ExitStack() as c:
        e = c.enter_context
        part = [[e(nc.sbuf_tensor(unique("part"), [D, N], BF16)) for _ in range(3)] for _ in range(2)]
        rest = e(nc.sbuf_tensor(unique("rest"), [D, 2, CH], F32))
        out = e(nc.psum_tensor(unique("projection"), [D, 2, 512], F32))
        multiplied = e(nc.semaphore(unique("projected")))
        first = e(nc.semaphore(unique("first_parts")))
        split = e(nc.semaphore(unique("split")))
        v_ready = e(nc.semaphore(unique("v_multiplied")))
        v_moved = e(nc.semaphore(unique("v_moved")))
        spread = e(nc.semaphore(unique("spread")))
        block = e(nc.Block())

        @block.tensor
        def _(pe):
            for m, name in enumerate(("Wq", "Wk")):
                for k, at, w in pieces:
                    p = m * n + k
                    if p >= 2:
                        pe.wait_ge(split, 3 * (p - 1))
                    nc.tensor.matmul(out[:, p % 2, 0:w], W[name][:], HT[:, at:at + w], start=True, stop=True).then_inc(multiplied, 1)
            pe.wait_ge(split, 3 * 2 * n)
            for r, a0, m in quads():
                if r >= 2:
                    pe.wait_ge(v_moved, r - 1)
                for a in range(a0, a0 + m):
                    ins = nc.tensor.matmul(out[0:P, r % 2, (a - a0) * D:(a - a0 + 1) * D], HT[:, a * P:(a + 1) * P],
                                           W["Wv"][:], start=True, stop=True)
                ins.then_inc(v_ready, 1)

        @block.scalar
        def _(act):
            for m in range(2):
                for k, at, w in pieces:
                    p = m * n + k
                    act.wait_ge(multiplied, p + 1)
                    nc.scalar.copy(part[m][0][:, at:at + w], out[:, p % 2, 0:w]).then_inc(first, 1)
            for r, a0, m in quads():
                act.wait_ge(v_ready, r + 1)
                nc.scalar.copy(V[:, a0:a0 + m, :, 0:HID],
                               out[0:P, r % 2, 0:m * D].rearrange("p (a h o) -> p a h o", h=HEADS, o=HID)).then_inc(v_moved, 1)

        @block.vector
        def _(dve):
            nc.vector.memset(V[:, :, :, HID:HID + 1], 1.0)
            for m in range(2):
                for k, at, w in pieces:
                    p = m * n + k
                    dve.wait_ge(first, p + 1)
                    here = slice(at, at + w)
                    r = rest[:, p % 2, 0:w]
                    nc.vector.tensor_tensor(r, out[:, p % 2, 0:w], part[m][0][:, here], ALU.subtract).then_inc(split, 1)
                    dve.wait_ge(split, 3 * p + 1)
                    nc.vector.tensor_copy(part[m][1][:, here], r).then_inc(split, 1)
                    dve.wait_ge(split, 3 * p + 2)
                    nc.vector.tensor_tensor(part[m][2][:, here], r, part[m][1][:, here], ALU.subtract).then_inc(split, 1)

        @block.sync
        def _(sp):
            count = 0
            for m, (A, B, rows_a, rows_b) in enumerate(((QA, QB, (0, 1, 0, 1), (2, 0)), (KA, KB, (0, 0, 1, 1), (0, 2)))):
                sp.wait_ge(split, 3 * n * (m + 1))
                for h in range(HEADS):
                    head = slice(h * HID, (h + 1) * HID)
                    for k, which in enumerate(rows_a):
                        sp.dma_start(A[k * HID:(k + 1) * HID, h, :], part[m][which][head, :]).then_inc(spread, 16)
                    for k, which in enumerate(rows_b):
                        at = 64 * (h % 2) + k * HID
                        sp.dma_start(B[at:at + HID, h // 2, :], part[m][which][head, :]).then_inc(spread, 16)
                    count += 6
            sp.wait_ge(spread, 16 * count)


def attention(nc, counts, countsT, X, H, QA, QB, KA, KB, V, ident):
    PW = 4 * P
    PIECES = len(quads())
    TP = HEADS * PIECES
    LAG = PIECES + 2
    EXP_LAG = PIECES + 1
    width = [n * P for _, _, n in quads()]
    with ExitStack() as c:
        e = c.enter_context
        count_in = e(nc.sbuf_tensor(unique("count_in"), [P, N], F32))
        countT_in = e(nc.sbuf_tensor(unique("countT_in"), [P, 2, N], F32))
        absent = e(nc.sbuf_tensor(unique("absent"), [P, 2, N], BF16))
        low = e(nc.sbuf_tensor(unique("low"), [P, P], BF16))
        key_a = e(nc.sbuf_tensor(unique("key_a"), [D, 2, HEADS, P], BF16))
        key_b = e(nc.sbuf_tensor(unique("key_b"), [D, 2, HEADS, P], BF16))
        score1 = e(nc.sbuf_tensor(unique("score1"), [P, N], F32))
        score = [H[:].rearrange("p t d -> p (t d)")[:, 0:N], score1[:]]
        rising = e(nc.sbuf_tensor(unique("rising"), [P, 2, PW], F32))
        weighed = e(nc.sbuf_tensor(unique("weighed"), [P, 4, PW], F32))
        peaks = e(nc.sbuf_tensor(unique("peaks"), [P, 2, PIECES], F32))
        shift = e(nc.sbuf_tensor(unique("shift"), [P, 2, 2], F32))
        norm = e(nc.sbuf_tensor(unique("norm"), [P, 2 * HEADS], F32))
        heads_out = e(nc.sbuf_tensor(unique("heads_out"), [P, HEADS, HID], F32))
        raw = e(nc.psum_tensor(unique("raw"), [P, 4, 512], F32))
        probsT = e(nc.psum_tensor(unique("probsT"), [P, 2, 512], F32))
        mixed = e(nc.psum_tensor(unique("mixed_values"), [P, 2, 512], F32))
        c_loaded = e(nc.semaphore(unique("c_loaded")))
        ct_loaded = [e(nc.semaphore(unique(f"ct_loaded{u}"))) for u in range(2)]
        low_ready = e(nc.semaphore(unique("low_ready")))
        absent_done = e(nc.semaphore(unique("absent_done")))
        vector_go = e(nc.semaphore(unique("vector_go")))
        pool_go = e(nc.semaphore(unique("pool_go")))
        keys_done = e(nc.semaphore(unique("keys_done")))
        scored = e(nc.semaphore(unique("scored")))
        scaled = e(nc.semaphore(unique("scaled")))
        leaky = e(nc.semaphore(unique("leaky")))
        shifted = e(nc.semaphore(unique("shifted")))
        exped = e(nc.semaphore(unique("exped")))
        turned = e(nc.semaphore(unique("probs_turned")))
        counted = e(nc.semaphore(unique("counted")))
        summed = e(nc.semaphore(unique("values_summed")))
        norm_steps = e(nc.semaphore(unique("norm_steps")))
        tile_out = e(nc.semaphore(unique("tile_out")))
        block = e(nc.Block())

        def slots(score_piece, value_piece):
            def run(t, u, before=True):
                for p in range(TP):
                    score_piece(t, u, p // PIECES, p % PIECES)
                    q = p - LAG
                    if q >= 0:
                        value_piece(t, u, q // PIECES, q % PIECES)
                    elif before:
                        value_piece(t - 1, 1 - u, (q + TP) // PIECES, (q + TP) % PIECES)
            return run

        def all_tiles(eng, score_piece, value_piece):
            run = slots(score_piece, value_piece)
            run(0, 0, before=False)
            with eng.Fori(0, (TILES - 1) // 2) as i:
                run(i * 2 + 1, 1)
                run(i * 2 + 2, 0)
            for q in range(TP - LAG, TP):
                value_piece(TILES - 1, 0, q // PIECES, q % PIECES)

        @block.sync
        def _(sp):
            def tile(t, u):
                row = lambda d: d[bass.ds(t, 1)].rearrange("o p n -> (o p) n")
                sp.wait_ge(absent_done, t + 1)
                sp.dma_start(count_in[:], row(counts)).then_inc(c_loaded, 16)
                sp.wait_ge(tile_out, t + 1)
                sp.dma_start(countT_in[:, u, :], row(countsT)).then_inc(ct_loaded[u], 16)

            in_pairs(sp, tile)

        @block.gpsimd
        def _(pool):
            nc.gpsimd.memset(key_b[:], 0.0).then_inc(keys_done, 1)
            pool.sem_inc(absent_done, 1)
            pool.wait_ge(keys_done, 1)

            def tile(t, u):
                pool.wait_ge(tile_out, t + 1)
                pool.sem_inc(pool_go, 1)
                here = bass.ds(t * P, P)
                nc.gpsimd.tensor_copy(key_a[:, u], KA[:, :, here]).then_inc(keys_done, 1)
                for s in range(2):
                    pool.wait_ge(keys_done, t * 3 + (2 + s))
                    pool.sem_inc(pool_go, 1)
                    rows = slice(64 * s, 64 * s + 64)
                    nc.gpsimd.tensor_copy(key_b[rows, u].rearrange("p (j s) n -> p s j n", s=2)[:, s], KB[rows, :, here]).then_inc(keys_done, 1)
                pool.wait_ge(c_loaded, t * 16 + 16)
                pool.wait_ge(keys_done, t * 3 + 4)
                pool.sem_inc(pool_go, 1)
                nc.gpsimd.tensor_scalar(absent[:, u, :], count_in[:], 0.0, None, ALU.is_equal).then_inc(absent_done, 1)

            in_pairs(pool, tile)

        @block.tensor
        def _(pe):
            pe.sem_inc(summed, 4)
            pe.wait_ge(low_ready, 1)

            def score_piece(t, u, h, r):
                p = h * PIECES + r
                if p == 0:
                    pe.wait_ge(absent_done, t + 2)
                    pe.wait_ge(keys_done, t * 3 + 4)
                pe.wait_ge(leaky, t * TP + (p + 1))
                at, w = PW * r, width[r]
                out = raw[:, p % 4, 0:w]
                nc.tensor.matmul(out, key_a[:, u, h, :], QA[:, h, at:at + w], start=True, stop=False)
                nc.tensor.matmul(out, key_b[:, u, h, :], QB[:, h // 2, at:at + w], start=False, stop=False)
                nc.tensor.matmul(out, low[:], absent[:, u, at:at + w], start=False, stop=True).then_inc(scored, 1)

            def sum_piece(t, u, h, r):
                p = h * PIECES + r
                pe.wait_ge(counted, t * TP + (p + 3))
                if p == 0:
                    pe.wait_ge(tile_out, t + 1)
                for k in range(width[r] // P):
                    a = 4 * r + k
                    ins = nc.tensor.matmul(mixed[:, u, h * (HID + 1):(h + 1) * (HID + 1)], weighed[:, p % 4, k * P:(k + 1) * P],
                                           V[:, a, h, :], start=(a == 0), stop=(a == TILES - 1))
                ins.then_inc(summed, 1)

            def value_piece(t, u, h, r):
                p = h * PIECES + r
                pe.wait_ge(exped, t * TP + (p + 1))
                pe.wait_ge(counted, t * TP + (p + 1))
                for k in range(width[r] // P):
                    a = 4 * r + k
                    ins = nc.tensor.transpose(probsT[:, p % 2, k * P:(k + 1) * P], score[h % 2][:, a * P:(a + 1) * P],
                                              ident[0:P, 0:P])
                ins.then_inc(turned, 1)
                if p > 0:
                    sum_piece(t, u, (p - 1) // PIECES, (p - 1) % PIECES)
                if p == TP - 1:
                    sum_piece(t, u, h, r)

            all_tiles(pe, score_piece, value_piece)

        @block.scalar
        def _(act):
            def score_piece(t, u, h, r):
                p = h * PIECES + r
                act.wait_ge(scored, t * TP + (p + 1))
                act.wait_ge(leaky, t * TP + (p + 3))
                nc.scalar.activation(rising[:, p % 2, 0:width[r]], raw[:, p % 4, 0:width[r]], ACT.Relu,
                                     scale=1.0 / SLOPE - 1.0).then_inc(scaled, 1)

            def value_piece(t, u, h, r):
                at, w = PW * r, width[r]
                if r == 0:
                    act.wait_ge(shifted, t * (2 * HEADS) + (2 * h + 2))
                nc.scalar.activation(score[h % 2][:, at:at + w], score[h % 2][:, at:at + w], ACT.Exp,
                                     bias=shift[:, h % 2, 1:2]).then_inc(exped, 1)

            def run(t, u, before=True):
                for p in range(TP):
                    score_piece(t, u, p // PIECES, p % PIECES)
                    q = p - EXP_LAG
                    if q >= 0:
                        value_piece(t, u, q // PIECES, q % PIECES)
                    elif before:
                        value_piece(t - 1, 1 - u, (q + TP) // PIECES, (q + TP) % PIECES)

            run(0, 0, before=False)
            with act.Fori(0, (TILES - 1) // 2) as i:
                run(i * 2 + 1, 1)
                run(i * 2 + 2, 0)
            for q in range(TP - EXP_LAG, TP):
                value_piece(TILES - 1, 0, q // PIECES, q % PIECES)

        @block.vector
        def _(dve):
            dve.sem_inc(leaky, 4)
            dve.sem_inc(counted, 2)
            dve.sem_inc(tile_out, 2)
            nc.vector.tensor_scalar(low[:], ident[0:P, 0:P], -1e30, None, ALU.mult).then_inc(low_ready, 1)

            def score_piece(t, u, h, r):
                p, b = h * PIECES + r, h % 2
                dve.wait_ge(scaled, t * TP + (p + 1))
                dve.sem_inc(vector_go, 1)
                at, w = PW * r, width[r]
                nc.vector.tensor_tensor_reduce(out=score[b][:, at:at + w], in0=raw[:, p % 4, 0:w],
                                               in1=rising[:, p % 2, 0:w], scale=SLOPE, scalar=-3e38, op0=ALU.add,
                                               op1=ALU.max, accum_out=peaks[:, b, r:r + 1]).then_inc(leaky, 1)
                if r == PIECES - 1:
                    dve.wait_ge(leaky, t * TP + (p + 5))
                    nc.vector.tensor_reduce(shift[:, b, 0:1], peaks[:, b, :], axis=AX.X, op=ALU.max).then_inc(shifted, 1)
                    dve.wait_ge(shifted, t * (2 * HEADS) + (2 * h + 1))
                    nc.vector.tensor_scalar(shift[:, b, 1:2], shift[:, b, 0:1], -1.0, None, ALU.mult).then_inc(shifted, 1)

            def value_piece(t, u, h, r):
                p = h * PIECES + r
                if p == 0:
                    dve.wait_ge(ct_loaded[u], (t - u) * 8 + 16)
                dve.wait_ge(turned, t * TP + (p + 1))
                dve.wait_ge(summed, t * TP + (p + 1))
                nc.vector.tensor_tensor(weighed[:, p % 4, 0:width[r]], probsT[:, p % 2, 0:width[r]],
                                        countT_in[:, u, PW * r:PW * r + width[r]], ALU.mult).then_inc(counted, 1)
                if p == TP - 1:
                    finish(t, u)

            def finish(t, u):
                sums = mixed[:, u, 0:HEADS * (HID + 1)].rearrange("p (h o) -> p h o", o=HID + 1)
                dve.wait_ge(summed, t * TP + (TP + 4))
                nc.vector.tensor_scalar(norm[:, 0:HEADS], sums[:, :, HID], 1e-9, None, ALU.max).then_inc(norm_steps, 1)
                dve.wait_ge(norm_steps, t * 3 + 1)
                nc.vector.reciprocal(norm[:, HEADS:], norm[:, 0:HEADS]).then_inc(norm_steps, 1)
                dve.wait_ge(norm_steps, t * 3 + 2)
                nc.vector.tensor_tensor(heads_out[:], sums[:, :, 0:HID],
                                        norm[:, HEADS:].unsqueeze(2).broadcast_to([P, HEADS, HID]), ALU.mult).then_inc(norm_steps, 1)
                dve.wait_ge(norm_steps, t * 3 + 3)
                nc.vector.tensor_tensor(row_of(X, t), row_of(X, t), heads_out[:].rearrange("p h o -> p (h o)"),
                                        ALU.add).then_inc(tile_out, 1)

            all_tiles(dve, score_piece, value_piece)


def one_over_degree(nc, in_parts, per_node):
    with nc.semaphore(unique("degree_done")) as degree_done, nc.Block() as block:
        @block.vector
        def _(dve):
            link = chained(dve, degree_done)
            link(nc.vector.tensor_reduce(per_node[:], in_parts[:], axis=AX.X, op=ALU.add))
            link(nc.vector.tensor_scalar(per_node[:], per_node[:], 1.0, None, ALU.add))
            link(nc.vector.reciprocal(per_node[:], per_node[:]))


def weighted_step(nc, weightsT, Y, YT, Z, W, ones, per_node, step):
    BUFS = 5
    with ExitStack() as c:
        e = c.enter_context
        block_in = e(nc.sbuf_tensor(unique("weights_in"), [P, BUFS, N], F32))
        own = e(nc.sbuf_tensor(unique("own"), [D, BUFS, P], F32))
        total = e(nc.sbuf_tensor(unique("total"), [D, BUFS, P], F32))
        self_part = e(nc.sbuf_tensor(unique("self_part"), [P, D], F32))
        mixed = e(nc.sbuf_tensor(unique("mixed"), [P, D], F32))
        agg = e(nc.psum_tensor(unique("agg"), [D, BUFS, 512], F32))
        lin = e(nc.psum_tensor(unique("lin"), [P, 2 * D], F32))
        loaded = [e(nc.semaphore(unique(f"w_loaded{u}"))) for u in range(BUFS)]
        summed = e(nc.semaphore(unique("agg_summed")))
        own_ready = e(nc.semaphore(unique("own_ready")))
        totalled = e(nc.semaphore(unique("totalled")))
        applied = e(nc.semaphore(unique("applied")))
        self_copied = e(nc.semaphore(unique("self_copied")))
        mixed_done = e(nc.semaphore(unique("mixed_done")))
        z_done = e(nc.semaphore(unique("z_done")))
        block = e(nc.Block())

        @block.sync
        def _(sp):
            def tile(t, u):
                sp.wait_ge(summed, t + 1)
                sp.dma_start(block_in[:, u, :], weightsT[bass.ds(t, 1)].rearrange("o p n -> (o p) n")).then_inc(loaded[u], 16)

            in_turns(sp, tile, BUFS)

        @block.scalar
        def _(act):
            def copy_own(t, u):
                act.wait_ge(applied, t + 1)
                nc.scalar.copy(own[:, u, :], YT[:, bass.ds(t * P, P)]).then_inc(own_ready, 1)

            def tile(t, u):
                copy_own(t, u)
                act.wait_ge(applied, t + (BUFS + 1))
                act.wait_ge(mixed_done, t + 1)
                nc.scalar.copy(self_part[:], lin[:, D:2 * D]).then_inc(self_copied, 1)

            in_turns(act, tile, BUFS)

        @block.vector
        def _(dve):
            dve.sem_inc(totalled, BUFS)
            dve.sem_inc(mixed_done, 1)

            def tile(t, u):
                dve.wait_ge(summed, t + (BUFS + 1))
                dve.wait_ge(own_ready, t + 1)
                nc.vector.tensor_tensor(total[:, u, :], agg[:, u, 0:P], own[:, u, :], ALU.add).then_inc(totalled, 1)
                dve.wait_ge(self_copied, t + 1)
                nc.vector.scalar_tensor_tensor(mixed[:], lin[:, 0:D], per_node[:, bass.ds(t, 1)], self_part[:],
                                               ALU.mult, ALU.add).then_inc(mixed_done, 1)
                dve.wait_ge(mixed_done, t + 2)
                nc.vector.scalar_tensor_tensor(row_of(Z, t), mixed[:], SLOPE, mixed[:], ALU.mult,
                                               ALU.max).then_inc(z_done, 1)

            in_turns(dve, tile, BUFS)

        @block.tensor
        def _(pe):
            pe.sem_inc(summed, BUFS)
            pe.sem_inc(applied, BUFS)

            def sum_sources(t, u, i):
                pe.wait_ge(loaded[u], i * 16 + 16)
                pe.wait_ge(totalled, t + 1)
                for a in range(TILES):
                    ins = nc.tensor.matmul(agg[:, u, 0:P], Y[:, a, :], block_in[:, u, a * P:(a + 1) * P],
                                           start=(a == 0), stop=(a == TILES - 1))
                ins.then_inc(summed, 1)

            def apply_weights(t, u):
                pe.wait_ge(totalled, t + (BUFS + 1))
                pe.wait_ge(mixed_done, t + 1)
                nc.tensor.matmul(lin[:, 0:D], total[:, u, :], W[f"Wn{step}"][:], start=True, stop=True)
                nc.tensor.matmul(lin[:, D:2 * D], own[:, u, :], W[f"Ws{step}"][:], start=True, stop=False)
                nc.tensor.matmul(lin[:, D:2 * D], ones[0:1, 0:P], W["bias"][0:1, 3 + step, :], start=False,
                                 stop=True).then_inc(applied, 1)

            sum_sources(0, 0, 0)
            with pe.Fori(0, TILES // BUFS - 1) as i:
                for u in range(BUFS):
                    sum_sources(i * BUFS + (u + 1), (u + 1) % BUFS, i + (u + 1) // BUFS)
                    apply_weights(i * BUFS + u, u)
            for t in range(TILES - BUFS, TILES):
                if t + 1 < TILES:
                    sum_sources(t + 1, (t + 1) % BUFS, (t + 1) // BUFS)
                apply_weights(t, t % BUFS)


def weighted_output(nc, X, YT, W, ones):
    with ExitStack() as c:
        e = c.enter_context
        lin = e(nc.psum_tensor(unique("lin"), [P, 2, 512], F32))
        bias = e(nc.psum_tensor(unique("bias_rows"), [P, D], F32))
        multiplied = e(nc.semaphore(unique("multiplied")))
        added = e(nc.semaphore(unique("rows_added")))
        block = e(nc.Block())

        @block.tensor
        def _(pe):
            nc.tensor.matmul(bias[:], ones[0:1, 0:P], W["bias"][0:1, 1, :], start=True, stop=True)
            for r, a0, n in quads():
                if r >= 2:
                    pe.wait_ge(added, r)
                for a in range(a0, a0 + n):
                    ins = nc.tensor.matmul(lin[:, r % 2, (a - a0) * D:(a - a0 + 1) * D], YT[:, a * P:(a + 1) * P],
                                           W["Wa"][:], start=True, stop=True)
                ins.then_inc(multiplied, 1)

        @block.vector
        def _(dve):
            dve.wait_ge(multiplied, 1)
            nc.vector.tensor_tensor(X[:], X[:], bias[:].unsqueeze(1).broadcast_to([P, TILES, D]), ALU.add).then_inc(added, 1)
            dve.wait_ge(added, 1)
            for r, a0, n in quads():
                dve.wait_ge(multiplied, r + 1)
                part = X[:, a0:a0 + n, :].rearrange("p a d -> p (a d)")
                nc.vector.tensor_tensor(part, part, lin[:, r % 2, 0:n * D], ALU.add).then_inc(added, 1)


def general_edges(nc, T, src_i, dst_i, dst_rel, attr, attrT, mix, index, gathered, message, acc, ident,
                  iota, iota_tile, projected):
    with ExitStack() as c:
        e = c.enter_context
        hot = e(nc.sbuf_tensor(unique("tile_hot"), [P, EG, P], F32))
        flat = e(nc.psum_tensor(unique("attr_flipped"), [EG * EDIM, P], F32))
        factor = e(nc.psum_tensor(unique("factor"), [P, 2, 512], F32))
        sums = e(nc.psum_tensor(unique("sums"), [D, P], F32))
        attr_loaded = e(nc.semaphore(unique("attr_loaded")))
        prepared = e(nc.semaphore(unique("prepared")))
        started = e(nc.semaphore(unique("started")))
        arrived = e(nc.semaphore(unique("arrived")))
        turned = e(nc.semaphore(unique("attr_turned")))
        kept = e(nc.semaphore(unique("attr_kept")))
        factored = e(nc.semaphore(unique("factored")))
        made = e(nc.semaphore(unique("message_made")))
        reduced = e(nc.semaphore(unique("reduced")))
        relative = e(nc.semaphore(unique("relative")))
        with nc.Fori(0, TILES) as t:
            with nc.Block() as block:
                @block.sync
                def _(sp):
                    attributes = T["edge_attr_16"].rearrange("(g p c) k -> g p (c k)", p=P, c=EG)
                    with sp.Fori(0, EGROUPS) as g:
                        sp.wait_ge(reduced, g + 1)
                        sp.dma_start(attr[:, 0, :], attributes[bass.ds(g, 1)].rearrange("o p n -> (o p) n")).then_inc(attr_loaded, 16)

                @block.gpsimd
                def _(pool):
                    with pool.Fori(0, EGROUPS) as g:
                        pool.wait_ge(prepared, g + 1)
                        pool.sem_inc(started, 1)
                        for k in range(EG):
                            nc.gpsimd.indirect_dma_start(gathered[:, 0, k, :], None, projected,
                                                         bass.IndirectOffsetOnAxis(ap=index[:, 0, k:k + 1], axis=0)
                                                         ).then_inc(arrived, 16)

                @block.tensor
                def _(pe):
                    pe.sem_inc(reduced, 1)

                    def group(g, first=False, last=False):
                        pe.wait_ge(attr_loaded, g * 16 + 16)
                        nc.tensor.transpose(flat[:], attr[:, 0, :], ident[0:P, 0:P]).then_inc(turned, 1)
                        pe.wait_ge(kept, g + 1)
                        for h in range(2):
                            ins = nc.tensor.matmul(factor[:, h, 0:EG * D // 2], attrT[:, 0, :],
                                                   mix[:].rearrange("r c d -> r (c d)")[:, h * EG * D // 2:(h + 1) * EG * D // 2],
                                                   start=True, stop=True)
                        ins.then_inc(factored, 1)
                        pe.wait_ge(made, g + 1)
                        for k in range(EG):
                            ins = nc.tensor.matmul(sums[:], message[:, 0, k, :], hot[:, k, :], start=first and k == 0,
                                                   stop=last and k == EG - 1)
                        ins.then_inc(reduced, 1)

                    group(0, first=True)
                    with pe.Fori(1, EGROUPS - 1) as g:
                        group(g)
                    group(EGROUPS - 1, last=True)

                @block.vector
                def _(dve):
                    nc.vector.tensor_copy(dst_rel[:], dst_i[:]).then_inc(relative, 1)
                    dve.wait_ge(relative, 1)
                    nc.vector.tensor_scalar(dst_rel[:], dst_rel[:], iota_tile[:, bass.ds(t, 1)], None,
                                            ALU.subtract).then_inc(relative, 1)
                    dve.wait_ge(relative, 2)
                    with dve.Fori(0, EGROUPS) as g:
                        dve.wait_ge(reduced, g + 1)
                        nc.vector.tensor_tensor(hot[:], row_of(dst_rel, g).unsqueeze(2).broadcast_to([P, EG, P]),
                                                iota[:].unsqueeze(1).broadcast_to([P, EG, P]), ALU.is_equal)
                        nc.vector.tensor_copy(index[:, 0, :], row_of(src_i, g)).then_inc(prepared, 1)
                        dve.wait_ge(turned, g + 1)
                        nc.vector.tensor_copy(attrT[:, 0, :], flat[:]).then_inc(kept, 1)
                        dve.wait_ge(factored, g + 1)
                        dve.wait_ge(arrived, g * (16 * EG) + 16 * EG)
                        nc.vector.tensor_tensor(message[:, 0].rearrange("p c d -> p (c d)").rearrange("p (h n) -> p h n", h=2),
                                                gathered[:, 0].rearrange("p c d -> p (c d)").rearrange("p (h n) -> p h n", h=2),
                                                factor[:, :, 0:EG * D // 2], ALU.mult).then_inc(made, 1)
                    dve.wait_ge(reduced, EGROUPS + 1)
                    nc.vector.tensor_copy(acc[:, bass.ds(t * P, P)], sums[:])

            clear_semaphores(nc, (attr_loaded, prepared, started, arrived, turned, kept, factored, made, reduced,
                                  relative))


def edge_layer(nc, T, X, HT, W, ones, ident, iota, iota_tile, irregular, projected):
    BUFS = 3
    EDGES = EG * P
    ROWS16 = EG * EDIM
    with ExitStack() as c:
        e = c.enter_context
        rows = e(nc.sbuf_tensor(unique("xw_rows"), [P, TILES, D], F32))
        src_i = e(nc.sbuf_tensor(unique("src_i"), [P, EGROUPS, EG], I32))
        dst_i = e(nc.sbuf_tensor(unique("dst_i"), [P, EGROUPS, EG], I32))
        dst_rel = e(nc.sbuf_tensor(unique("dst_rel"), [P, EGROUPS, EG], F32))
        base_i = e(nc.sbuf_tensor(unique("base_i"), [1, EGROUPS], I32))
        base_f = e(nc.sbuf_tensor(unique("base_f"), [1, EGROUPS], F32))
        span_i = e(nc.sbuf_tensor(unique("span_i"), [P, SPAN], I32))
        span = e(nc.sbuf_tensor(unique("span"), [P, SPAN], F32))
        attr = e(nc.sbuf_tensor(unique("attr"), [P, BUFS, ROWS16], F32))
        mix = e(nc.sbuf_tensor(unique("mix"), [ROWS16, EG, D], F32))
        attrT = e(nc.sbuf_tensor(unique("attrT"), [ROWS16, BUFS, P], F32))
        gathered = e(nc.sbuf_tensor(unique("gathered_rows"), [P, BUFS, EG, D], F32))
        message = e(nc.sbuf_tensor(unique("message"), [P, BUFS, EG, D], F32))
        index = e(nc.sbuf_tensor(unique("index"), [P, BUFS, EG], I32))
        hot = e(nc.sbuf_tensor(unique("hot"), [P, BUFS, EG, SPAN], F32))
        acc = e(nc.sbuf_tensor(unique("acc"), [D, N + SPAN], F32))
        with ExitStack() as c1:
            e = c1.enter_context
            lin = e(nc.psum_tensor(unique("lin"), [P, 2, 512], F32))
            bias = e(nc.psum_tensor(unique("bias_rows"), [P, D], F32))
            bases = e(nc.psum_tensor(unique("bases"), [P, EGROUPS], F32))
            edges_in = e(nc.semaphore(unique("edges_in")))
            attr_in = e(nc.semaphore(unique("attr_in")))
            mix_zero = e(nc.semaphore(unique("mix_zero")))
            pool_done = e(nc.semaphore(unique("pool_done")))
            multiplied = e(nc.semaphore(unique("multiplied")))
            copied = e(nc.semaphore(unique("rows_copied")))
            rel_done = e(nc.semaphore(unique("rel_done")))
            base_ready = e(nc.semaphore(unique("base_ready")))
            base_spread = e(nc.semaphore(unique("base_spread")))
            stored = e(nc.semaphore(unique("rows_stored")))
            block = e(nc.Block())

            @block.gpsimd
            def _(pool):
                nc.gpsimd.memset(mix[:], 0.0).then_inc(mix_zero, 1)
                nc.gpsimd.memset(acc[:], 0.0)
                nc.gpsimd.iota(span_i[:], [[1, SPAN]], base=0, channel_multiplier=0).then_inc(pool_done, 1)

            @block.sync
            def _(sp):
                with nc.allow_non_contiguous_dma(reason="runs of five edges, and one destination of every group"):
                    sp.dma_start(base_i[:], T["dst"].rearrange("(o g r) -> o g r", o=1, r=EDGES)[:, :, 0]).then_inc(edges_in, 16)
                    sp.dma_start(src_i[:], T["src"].rearrange("(g p c) -> p g c", p=P, c=EG)).then_inc(edges_in, 16)
                    sp.dma_start(dst_i[:], T["dst"].rearrange("(g p c) -> p g c", p=P, c=EG)).then_inc(edges_in, 16)
                sp.wait_ge(mix_zero, 1)
                for k in range(EG):
                    sp.dma_start(mix[k * EDIM:(k + 1) * EDIM, k, :], T["L3_gnn_edge_w"]).then_inc(attr_in, 16)
                sp.wait_ge(copied, len(quads()))
                sp.dma_start(projected.rearrange("(t p) f -> p t f", p=P), rows[:]).then_inc(stored, 16)
                sp.wait_ge(stored, 16)
                sp.wait_ge(attr_in, 16 * EG)

            @block.tensor
            def _(pe):
                for r, a0, n in quads():
                    if r >= 2:
                        pe.wait_ge(copied, r - 1)
                    for a in range(a0, a0 + n):
                        ins = nc.tensor.matmul(lin[:, r % 2, (a - a0) * D:(a - a0 + 1) * D], HT[:, a * P:(a + 1) * P],
                                               W["W3"][:], start=True, stop=True)
                    ins.then_inc(multiplied, 1)
                nc.tensor.matmul(bias[:], ones[0:1, 0:P], W["bias"][0:1, 2, :], start=True, stop=True).then_inc(base_spread, 1)
                pe.wait_ge(base_ready, 1)
                nc.tensor.matmul(bases[:], ones[0:1, 0:P], base_f[:], start=True, stop=True).then_inc(base_spread, 1)

            @block.scalar
            def _(act):
                for r, a0, n in quads():
                    act.wait_ge(multiplied, r + 1)
                    nc.scalar.copy(rows[:, a0:a0 + n, :].rearrange("p a d -> p (a d)"), lin[:, r % 2, 0:n * D]).then_inc(copied, 1)

            @block.vector
            def _(dve):
                link = chained(dve, rel_done)
                dve.wait_ge(pool_done, 1)
                nc.vector.tensor_copy(span[:], span_i[:])
                dve.wait_ge(edges_in, 48)
                nc.vector.tensor_copy(base_f[:], base_i[:]).then_inc(base_ready, 1)
                link(nc.vector.tensor_copy(dst_rel[:], dst_i[:]))
                dve.wait_ge(base_spread, 2)
                nc.vector.tensor_tensor(X[:], X[:], bias[:].unsqueeze(1).broadcast_to([P, TILES, D]), ALU.add)
                link(nc.vector.tensor_tensor(dst_rel[:], dst_rel[:], bases[:].unsqueeze(2).broadcast_to([P, EGROUPS, EG]),
                                             ALU.subtract))

        with ExitStack() as c2:
            e = c2.enter_context
            flat = e(nc.psum_tensor(unique("attr_flipped"), [ROWS16, P], F32))
            factor = [e(nc.psum_tensor(unique(f"factor{u}"), [P, 2, 512], F32)) for u in range(BUFS)]
            sums = e(nc.psum_tensor(unique("sums"), [D, SPAN], F32))
            started = e(nc.semaphore(unique("started")))
            arrived = [e(nc.semaphore(unique(f"arrived{u}"))) for u in range(BUFS)]
            attr_loaded = [e(nc.semaphore(unique(f"attr_loaded{u}"))) for u in range(BUFS)]
            turned = e(nc.semaphore(unique("attr_turned")))
            kept = e(nc.semaphore(unique("attr_kept")))
            factored = e(nc.semaphore(unique("factored")))
            made = e(nc.semaphore(unique("message_made")))
            reduced = e(nc.semaphore(unique("reduced")))
            added = e(nc.semaphore(unique("sums_added")))
            indexed = e(nc.semaphore(unique("indexed")))
            block = e(nc.Block())

            @block.sync
            def _(sp):
                attributes = T["edge_attr_16"].rearrange("(g p c) k -> g p (c k)", p=P, c=EG)

                def group(g, u):
                    sp.wait_ge(factored, g + 1)
                    sp.dma_start(attr[:, u, :], attributes[bass.ds(g, 1)].rearrange("o p n -> (o p) n")).then_inc(attr_loaded[u], 16)

                in_turns(sp, group, BUFS, EGROUPS)

            @block.gpsimd
            def _(pool):
                def group(g, u):
                    pool.wait_ge(indexed, g + 1)
                    pool.sem_inc(started, 1)
                    for k in range(EG):
                        nc.gpsimd.indirect_dma_start(gathered[:, u, k, :], None, projected,
                                                     bass.IndirectOffsetOnAxis(ap=index[:, u, k:k + 1], axis=0)
                                                     ).then_inc(arrived[u], 16)

                in_turns(pool, group, BUFS, EGROUPS)

            @block.scalar
            def _(act):
                act.sem_inc(kept, 1)

                def copy_index(g, u):
                    act.wait_ge(made, g + 1)
                    nc.scalar.copy(index[:, u, :], row_of(src_i, g)).then_inc(indexed, 1)

                def keep_attributes(g, u):
                    act.wait_ge(turned, g + 1)
                    act.wait_ge(factored, g + 1)
                    nc.scalar.copy(attrT[:, u, :], flat[:]).then_inc(kept, 1)

                copy_index(0, 0)
                keep_attributes(0, 0)
                copy_index(1, 1)

                def group(g, u):
                    keep_attributes(g + 1, (u + 1) % BUFS)
                    copy_index(g + 2, (u + 2) % BUFS)

                with act.Fori(0, EGROUPS // BUFS - 1) as i:
                    for u in range(BUFS):
                        group(i * BUFS + u, u)
                for g in range(EGROUPS - BUFS, EGROUPS - 2):
                    group(g, g % BUFS)
                keep_attributes(EGROUPS - 1, (EGROUPS - 1) % BUFS)

            @block.tensor
            def _(pe):
                pe.sem_inc(factored, BUFS)
                pe.sem_inc(reduced, BUFS)

                def factors(g, u, i):
                    pe.wait_ge(kept, g + 1)
                    pe.wait_ge(attr_loaded[u], i * 16 + 16)
                    nc.tensor.transpose(flat[:], attr[:, u, :], ident[0:P, 0:P]).then_inc(turned, 1)
                    pe.wait_ge(kept, g + 2)
                    pe.wait_ge(made, g + 1)
                    for h in range(2):
                        ins = nc.tensor.matmul(factor[u][:, h, 0:EG * D // 2], attrT[:, u, :],
                                               mix[:].rearrange("r c d -> r (c d)")[:, h * EG * D // 2:(h + 1) * EG * D // 2],
                                               start=True, stop=True)
                    ins.then_inc(factored, 1)

                def sum_edges(g, u):
                    pe.wait_ge(made, g + (BUFS + 1))
                    pe.wait_ge(added, g + 1)
                    for k in range(EG):
                        ins = nc.tensor.matmul(sums[:], message[:, u, k, :], hot[:, u, k, :], start=(k == 0),
                                               stop=(k == EG - 1))
                    ins.then_inc(reduced, 1)

                factors(0, 0, 0)
                with pe.Fori(0, EGROUPS // BUFS - 1) as i:
                    for u in range(BUFS):
                        factors(i * BUFS + (u + 1), (u + 1) % BUFS, i + (u + 1) // BUFS)
                        sum_edges(i * BUFS + u, u)
                for g in range(EGROUPS - BUFS, EGROUPS):
                    if g + 1 < EGROUPS:
                        factors(g + 1, (g + 1) % BUFS, (g + 1) // BUFS)
                    sum_edges(g, g % BUFS)

            @block.vector
            def _(dve):
                dve.sem_inc(made, BUFS)
                dve.sem_inc(added, 1)
                with dve.Fori(0, EGROUPS // BUFS) as i:
                    for u in range(BUFS):
                        g = i * BUFS + u
                        dve.wait_ge(reduced, g + 1)
                        nc.vector.tensor_tensor(hot[:, u], dst_rel[:, bass.ds(g, 1), :].rearrange("p o c -> p (o c)").unsqueeze(2).broadcast_to([P, EG, SPAN]),
                                                span[:].unsqueeze(1).broadcast_to([P, EG, SPAN]), ALU.is_equal)
                        dve.wait_ge(factored, g + (BUFS + 1))
                        dve.wait_ge(arrived[u], i * (16 * EG) + 16 * EG)
                        nc.vector.tensor_tensor(message[:, u].rearrange("p c d -> p (c d)").rearrange("p (h n) -> p h n", h=2),
                                                gathered[:, u].rearrange("p c d -> p (c d)").rearrange("p (h n) -> p h n", h=2),
                                                factor[u][:, :, 0:EG * D // 2], ALU.mult).then_inc(made, 1)
                        base = dve.value_load(base_i[0:1, bass.ds(g, 1)], min_val=0, max_val=N - 1)
                        dve.wait_ge(reduced, g + (BUFS + 1))
                        dve.wait_ge(added, g + 1)
                        nc.vector.tensor_tensor(acc[:, bass.ds(base, SPAN)], acc[:, bass.ds(base, SPAN)], sums[:],
                                                ALU.add).then_inc(added, 1)

        with nc.If(nc.values_load(irregular[0:1, 0:1], min_val=0, max_val=1) != 0):
            general_edges(nc, T, src_i, dst_i, dst_rel, attr, attrT, mix, index, gathered, message, acc, ident,
                          iota, iota_tile, projected)

        with ExitStack() as c3:
            e = c3.enter_context
            back = e(nc.psum_tensor(unique("back"), [P, 2, 512], F32))
            turned = e(nc.semaphore(unique("acc_turned")))
            added = e(nc.semaphore(unique("acc_added")))
            stored = e(nc.semaphore(unique("out_stored")))
            block = e(nc.Block())

            @block.tensor
            def _(pe):
                for r, a0, n in quads():
                    if r >= 2:
                        pe.wait_ge(added, r - 1)
                    for a in range(a0, a0 + n):
                        ins = nc.tensor.transpose(back[:, r % 2, (a - a0) * D:(a - a0 + 1) * D], acc[:, a * P:(a + 1) * P], ident[:])
                    ins.then_inc(turned, 1)

            @block.vector
            def _(dve):
                for r, a0, n in quads():
                    dve.wait_ge(turned, r + 1)
                    part = X[:, a0:a0 + n, :].rearrange("p a d -> p (a d)")
                    nc.vector.tensor_tensor(part, part, back[:, r % 2, 0:n * D], ALU.add).then_inc(added, 1)

            @block.sync
            def _(sp):
                out = T["out"].rearrange("(t p) f -> p t f", p=P)
                for r, a0, n in quads():
                    sp.wait_ge(added, r + 1)
                    sp.dma_start(out[:, a0:a0 + n, :], X[:, a0:a0 + n, :]).then_inc(stored, 16)
                sp.wait_ge(stored, 16 * len(quads()))


def program(nc, T):
    dram = lambda name, shape, dt: nc.dram_tensor(name, shape, dt, kind="Internal").ap()
    table = dram("scratch_table", (ROWS + GROWS, 3 * ROW), I32)
    starts = dram("scratch_starts", (WINDOWS,), I32)
    countsT = dram("scratch_countsT", (TILES, P, N), F32)
    weightsT = dram("scratch_weightsT", (TILES, P, N), F32)
    projected = dram("scratch_projected", (N, D), F32)
    counts = dram("scratch_counts", (TILES, P, N), F32)

    def sb(name, shape, dt=F32):
        return nc.sbuf_tensor(unique(name), shape, dt)

    def ps(name, shape):
        return nc.psum_tensor(unique(name), shape, F32)

    with ExitStack() as whole:
        keep = whole.enter_context
        X = keep(sb("X", [P, TILES, D]))
        H = keep(sb("H", [P, TILES, D]))
        stats = keep(sb("stats", [P, TILES, 6]))
        mv = keep(sb("mv", [P, TILES, 2]))
        rstd = keep(sb("rstd", [P, TILES]))
        norm = (stats, mv, rstd)
        ident = keep(sb("ident", [128, 128]))
        ones = keep(sb("ones", [128, P]))
        out_degree = keep(sb("out_degree", [P, TILES]))
        in_parts = keep(sb("in_parts", [P, TILES, 7]))
        iota = keep(sb("iota", [P, P]))
        iota_tile = keep(sb("iota_tile", [P, TILES]))
        irregular = keep(sb("irregular", [1, 1], I32))

        W = {name: keep(sb(name, [D, D])) for name in ("W0", "Ws0", "Ws1", "Wn0", "Wn1", "Wa", "Wq", "Wk", "Wv", "W3")}
        W["bias"] = keep(sb("bias", [1, 5, D]))

        with ExitStack() as lists:
            hold = lists.enter_context
            src_hi = hold(sb("src_hi", [P, 2 * WINDOWS]))
            src_lo = hold(sb("src_lo", [P, 2 * WINDOWS]))
            dst_in = hold(sb("dst_in", [P, 2 * WINDOWS]))
            weight = hold(sb("weight", [P, 2 * WINDOWS]))
            used = window_starts(nc, T, table, starts, X, ident, ones, iota, iota_tile, irregular)
            used = edge_slots(nc, T, W, table, starts, X, H, norm, ident, src_hi, src_lo, dst_in, weight, used)
            adjacency(nc, counts, countsT, weightsT, ident, src_hi, src_lo, dst_in, weight, iota,
                      iota_tile, out_degree, in_parts, used)
        with nc.If(nc.values_load(irregular[0:1, 0:1], min_val=0, max_val=1) != 0):
            general_adjacency(nc, T, counts, countsT, weightsT, iota, iota_tile, out_degree, in_parts)
        gcn_layer(nc, counts, X, H, W, ones, out_degree)
        per_node = keep(sb("per_node", [P, TILES]))
        one_over_degree(nc, in_parts, per_node)
        with ExitStack() as heads:
            hold = heads.enter_context
            QA = hold(sb("QA", [D, HEADS, N], BF16))
            KA = hold(sb("KA", [D, HEADS, N], BF16))
            QB = hold(sb("QB", [D, HEADS // 2, N], BF16))
            KB = hold(sb("KB", [D, HEADS // 2, N], BF16))
            V = hold(sb("V", [P, TILES, HEADS, HID + 1]))
            with sb("HT", [D, N]) as HT:
                normalize(nc, X, H, HT, norm, ident)
                project(nc, HT, W, QA, QB, KA, KB, V)
            attention(nc, counts, countsT, X, H, QA, QB, KA, KB, V, ident)
        with sb("HT", [D, N]) as HT:
            normalize(nc, X, H, HT, norm, ident)
            with sb("Z", [P, TILES, D]) as Z:
                weighted_step(nc, weightsT, H, HT, Z, W, ones, per_node, 0)
                turn(nc, Z, HT, ident)
                weighted_step(nc, weightsT, Z, HT, H, W, ones, per_node, 1)
                turn(nc, H, HT, ident)
            weighted_output(nc, X, HT, W, ones)
            normalize(nc, X, H, HT, norm, ident)
            edge_layer(nc, T, X, HT, W, ones, ident, iota, iota_tile, irregular, projected)


_INS = ['x', 'src', 'dst', 'edge_attr_16', 'edge_weight', 'L0_gnn_W', 'L0_gnn_b', 'L1_gnn_Wq', 'L1_gnn_Wk',
        'L1_gnn_Wv', 'L2_gnn_W_self', 'L2_gnn_b_self', 'L2_gnn_W_neigh', 'L2_gnn_b_neigh', 'L2_gnn_layer_bias',
        'L2_gnn_W_agg', 'L2_gnn_b_agg', 'L3_gnn_W', 'L3_gnn_edge_w', 'L3_gnn_b']


def kernel(**inputs):
    import numpy as _np
    import concourse.bacc as _bacc
    from concourse import mybir as _mybir
    from concourse.bass_utils import run_bass_kernel_spmd as _run

    nc = _bacc.Bacc("TRN2", target_bir_lowering=False, num_devices=1)
    arrays, operands = {}, {}
    for name in _INS:
        a = _np.ascontiguousarray(inputs[name])
        arrays[f"in_{name}"] = a
        operands[name] = nc.dram_tensor(f"in_{name}", a.shape, _mybir.dt.from_np(a.dtype), kind="ExternalInput").ap()
    operands["out"] = nc.dram_tensor("out_0", (N, D), F32, kind="ExternalOutput").ap()
    program(nc, operands)
    r = _run(nc, [arrays], core_ids=[0])
    return r.results[0]["out_0"]
```
